# Optimizing a Trainium2 kernel written in Bass

```python
import numpy as np
import jax
import jax.numpy as jnp

def _softmax(x, axis=-1):
    return jax.nn.softmax(x, axis=axis)

def _gelu(x):
    return jax.nn.gelu(x, approximate=True)

def _silu(x):
    return jax.nn.silu(x)

def _sigmoid(x):
    return jax.nn.sigmoid(x)

def _layernorm(x, axis=-1, eps=1e-05):
    m = jnp.mean(x, axis=axis, keepdims=True)
    v = jnp.var(x, axis=axis, keepdims=True)
    return (x - m) / jnp.sqrt(v + eps)

def _scatter_add(tgt, idx, src, axis=0):
    return tgt.at[idx].add(src)

def _segment_sum(src, seg, n):
    return jax.ops.segment_sum(src, seg, n)
kernel_name = 'mk_hybrid_d1_jaxref_r8_aa9513'

def setup_inputs(seed: int=0):
    np.random.seed(seed)
    _w = jnp.asarray

    def _L0_attn_a_setup():
        import jax, jax.numpy as jnp
        import numpy as np
        import math
        NUM_HEADS = 16
        BASE = 10000.0

        def _rope_tables(T, head_size, dtype):
            half = head_size // 2
            thetas = BASE ** (-jnp.arange(half, dtype=jnp.float32) / half)
            ang = jnp.arange(T, dtype=jnp.float32)[:, None] * thetas[None, :]
            return (jnp.sin(ang).astype(dtype), jnp.cos(ang).astype(dtype))

        def _apply_rope(x, sin, cos):
            x1 = x[..., 0::2]
            x2 = x[..., 1::2]
            r1 = x1 * cos - x2 * sin
            r2 = x1 * sin + x2 * cos
            return jnp.stack([r1, r2], axis=-1).reshape(x.shape)
        key = jax.random.key(seed)
        ks = jax.random.split(key, 5)
        B, T, C = (4, 256, 256)
        return {'x': jax.random.normal(ks[0], (B, T, C), dtype=jnp.float32), 'w_qkv': jax.random.normal(ks[1], (3 * C, C), dtype=jnp.float32) * (1.0 / math.sqrt(C)), 'b_qkv': jax.random.normal(ks[2], (3 * C,), dtype=jnp.float32) * 0.02, 'w_out': jax.random.normal(ks[3], (C, C), dtype=jnp.float32) * (1.0 / math.sqrt(C)), 'b_out': jax.random.normal(ks[4], (C,), dtype=jnp.float32) * 0.02}
    _L0_attn_a_in = _L0_attn_a_setup()

    def _L0_attn_b_setup():
        import jax, jax.numpy as jnp
        import numpy as np
        HID, H, DK, DV, KS = (256, 16, 128, 128, 4)

        def _p(key, shape, scale=0.02):
            return jax.random.normal(key, shape, dtype=jnp.float32) * scale

        def _dwconv_causal(y, w, b):
            out = jax.lax.conv_general_dilated(y.transpose(0, 2, 1), w, window_strides=(1,), padding=[(KS - 1, 0)], feature_group_count=w.shape[0])
            return out.transpose(0, 2, 1) + b

        def _silu(x):
            return x * jax.nn.sigmoid(x)

        def _gated_delta(q, k, v, alpha, beta, scale):
            B, T, nH, _ = q.shape
            qs = q.transpose(1, 0, 2, 3)
            ks = k.transpose(1, 0, 2, 3) * scale
            vs = v.transpose(1, 0, 2, 3)
            al = alpha.transpose(1, 0, 2)
            be = beta.transpose(1, 0, 2)

            def step(S, inp):
                qt, kt, vt, at, bt = inp
                err = jnp.einsum('bhvk,bhk->bhv', S, kt) - vt
                S = at[..., None, None] * S - bt[..., None, None] * err[..., None] * kt[:, :, None, :]
                o = jnp.einsum('bhvk,bhk->bhv', S, qt)
                return (S, o)
            S0 = jnp.zeros((B, nH, DV, DK), dtype=q.dtype)
            _, o = jax.lax.scan(step, S0, (qs, ks, vs, al, be))
            return o.transpose(1, 0, 2, 3)
        key = jax.random.key(seed)
        ks = jax.random.split(key, 20)
        B, T = (2, 256)
        x = jax.random.normal(ks[0], (B, T, HID), dtype=jnp.float32)
        inp = {'x': x, 'Wq': _p(ks[1], (HID, H * DK)), 'Wk': _p(ks[2], (HID, H * DK)), 'Wv': _p(ks[3], (HID, H * DV)), 'Wa': _p(ks[4], (HID, H)), 'ba': jnp.zeros((H,), jnp.float32), 'Wb': _p(ks[5], (HID, H)), 'bb': jnp.zeros((H,), jnp.float32), 'Wg': _p(ks[6], (HID, H * DV)), 'Wo': _p(ks[7], (H * DV, HID)), 'conv_q_w': _p(ks[8], (H * DK, 1, KS), 0.3), 'conv_q_b': jnp.zeros((H * DK,), jnp.float32), 'conv_k_w': _p(ks[9], (H * DK, 1, KS), 0.3), 'conv_k_b': jnp.zeros((H * DK,), jnp.float32), 'conv_v_w': _p(ks[10], (H * DV, 1, KS), 0.3), 'conv_v_b': jnp.zeros((H * DV,), jnp.float32), 'ln_w': jnp.ones((DV,), jnp.float32), 'ln_b': jnp.zeros((DV,), jnp.float32)}
        return inp
    _L0_attn_b_in = _L0_attn_b_setup()

    def _L0_ffn_setup():
        import jax, jax.numpy as jnp
        import numpy as np
        D_MODEL = 256
        NUM_TILES = 64
        D_SLICE = D_MODEL // NUM_TILES
        TILES_PER_CLUSTER = 8
        NUM_CLUSTERS = NUM_TILES // TILES_PER_CLUSTER
        GRID = 16
        LN_EPS = 1e-05
        DIMS = (np.arange(NUM_TILES)[:, None] * D_SLICE + np.arange(D_SLICE)[None, :]) % D_MODEL
        DIMS = jnp.asarray(DIMS, dtype=jnp.int32)

        def _forward(x, ln_gamma, ln_beta, spline_bases, spline_slopes, output_scale):
            B, S, D = x.shape
            N = B * S
            mu = jnp.mean(x, axis=-1, keepdims=True)
            var = jnp.mean(jnp.square(x - mu), axis=-1, keepdims=True)
            xn = (x - mu) * jax.lax.rsqrt(var + LN_EPS) * ln_gamma + ln_beta
            xf = xn.reshape(N, D)
            slope_sign = jnp.sign(jnp.mean(spline_slopes, axis=-1))
            tile_sigs = jnp.zeros((NUM_TILES, D), dtype=x.dtype)
            tile_sigs = tile_sigs.at[jnp.arange(NUM_TILES)[:, None], DIMS].set(slope_sign)
            cluster_sigs = jnp.sign(tile_sigs.reshape(NUM_CLUSTERS, TILES_PER_CLUSTER, D).mean(axis=1))
            cluster_assign = jnp.arange(NUM_TILES, dtype=jnp.int32) // TILES_PER_CLUSTER
            input_sigs = jnp.sign(xf)
            cluster_scores = input_sigs @ cluster_sigs.T
            best_cluster = jnp.argmax(cluster_scores, axis=-1)
            tile_scores = input_sigs @ tile_sigs.T
            in_cluster = cluster_assign[None, :] == best_cluster[:, None]
            tile_idx = jnp.argmax(jnp.where(in_cluster, tile_scores, -jnp.inf), axis=-1)
            tok_dims = DIMS[tile_idx]
            x_slice = jnp.take_along_axis(xf, tok_dims, axis=1)
            tok_min = x_slice.min(axis=1)
            tok_max = x_slice.max(axis=1)
            onehot = tile_idx[None, :] == jnp.arange(NUM_TILES)[:, None]
            tile_min = jnp.where(onehot, tok_min[None, :], jnp.inf).min(axis=1)
            tile_max = jnp.where(onehot, tok_max[None, :], -jnp.inf).max(axis=1)
            mn = tile_min[tile_idx][:, None]
            mx = tile_max[tile_idx][:, None]
            u = jnp.clip((x_slice - mn) / (mx - mn + 1e-08), 0.0, 1.0 - 1e-06)
            gi = jnp.clip((u * GRID).astype(jnp.int32), 0, GRID - 1)
            j = jnp.arange(D_SLICE)[None, :]
            b = spline_bases[tile_idx[:, None], j, gi]
            s = spline_slopes[tile_idx[:, None], j, gi]
            x_local = (u - gi.astype(u.dtype) / GRID) * GRID
            delta = (b + s * x_local) * output_scale[tile_idx][:, None]
            out = jnp.zeros_like(xf).at[jnp.arange(N)[:, None], tok_dims].set(delta)
            return x + out.reshape(B, S, D)
        key = jax.random.key(seed)
        k1, k2, k3, k4, k5, k6 = jax.random.split(key, 6)
        x = jax.random.normal(k1, (4, 512, D_MODEL), dtype=jnp.float32)
        ln_gamma = 1.0 + 0.1 * jax.random.normal(k2, (D_MODEL,), dtype=jnp.float32)
        ln_beta = 0.1 * jax.random.normal(k3, (D_MODEL,), dtype=jnp.float32)
        spline_bases = 0.1 * jax.random.normal(k4, (NUM_TILES, D_SLICE, GRID), dtype=jnp.float32)
        spline_slopes = 0.1 + 0.1 * jax.random.normal(k5, (NUM_TILES, D_SLICE, GRID), dtype=jnp.float32)
        output_scale = 1.0 + 0.1 * jax.random.normal(k6, (NUM_TILES,), dtype=jnp.float32)
        return {'x': x, 'ln_gamma': ln_gamma, 'ln_beta': ln_beta, 'spline_bases': spline_bases, 'spline_slopes': spline_slopes, 'output_scale': output_scale}
    _L0_ffn_in = _L0_ffn_setup()
    _d = {'L0_attn_a_x': _L0_attn_a_in['x'], 'L0_attn_a_w_qkv': _L0_attn_a_in['w_qkv'], 'L0_attn_a_b_qkv': _L0_attn_a_in['b_qkv'], 'L0_attn_a_w_out': _L0_attn_a_in['w_out'], 'L0_attn_a_b_out': _L0_attn_a_in['b_out'], 'L0_attn_b_Wq': _L0_attn_b_in['Wq'], 'L0_attn_b_Wk': _L0_attn_b_in['Wk'], 'L0_attn_b_Wv': _L0_attn_b_in['Wv'], 'L0_attn_b_Wa': _L0_attn_b_in['Wa'], 'L0_attn_b_ba': _L0_attn_b_in['ba'], 'L0_attn_b_Wb': _L0_attn_b_in['Wb'], 'L0_attn_b_bb': _L0_attn_b_in['bb'], 'L0_attn_b_Wg': _L0_attn_b_in['Wg'], 'L0_attn_b_Wo': _L0_attn_b_in['Wo'], 'L0_attn_b_conv_q_w': _L0_attn_b_in['conv_q_w'], 'L0_attn_b_conv_q_b': _L0_attn_b_in['conv_q_b'], 'L0_attn_b_conv_k_w': _L0_attn_b_in['conv_k_w'], 'L0_attn_b_conv_k_b': _L0_attn_b_in['conv_k_b'], 'L0_attn_b_conv_v_w': _L0_attn_b_in['conv_v_w'], 'L0_attn_b_conv_v_b': _L0_attn_b_in['conv_v_b'], 'L0_attn_b_ln_w': _L0_attn_b_in['ln_w'], 'L0_attn_b_ln_b': _L0_attn_b_in['ln_b'], 'L0_ffn_ln_gamma': _L0_ffn_in['ln_gamma'], 'L0_ffn_ln_beta': _L0_ffn_in['ln_beta'], 'L0_ffn_spline_bases': _L0_ffn_in['spline_bases'], 'L0_ffn_spline_slopes': _L0_ffn_in['spline_slopes'], 'L0_ffn_output_scale': _L0_ffn_in['output_scale']}
    _x0 = _d['L0_attn_a_x']
    _d['L0_attn_a_x'] = jax.random.normal(jax.random.fold_in(jax.random.key(seed), 1), (16, 256, 256), dtype=_x0.dtype)
    del _x0
    return _d

def reference(L0_attn_a_x, L0_attn_a_w_qkv, L0_attn_a_b_qkv, L0_attn_a_w_out, L0_attn_a_b_out, L0_attn_b_Wq, L0_attn_b_Wk, L0_attn_b_Wv, L0_attn_b_Wa, L0_attn_b_ba, L0_attn_b_Wb, L0_attn_b_bb, L0_attn_b_Wg, L0_attn_b_Wo, L0_attn_b_conv_q_w, L0_attn_b_conv_q_b, L0_attn_b_conv_k_w, L0_attn_b_conv_k_b, L0_attn_b_conv_v_w, L0_attn_b_conv_v_b, L0_attn_b_ln_w, L0_attn_b_ln_b, L0_ffn_ln_gamma, L0_ffn_ln_beta, L0_ffn_spline_bases, L0_ffn_spline_slopes, L0_ffn_output_scale):

    def _L0_attn_a_ref(x, w_qkv, b_qkv, w_out, b_out):
        import jax, jax.numpy as jnp
        import numpy as np
        import math
        NUM_HEADS = 16
        BASE = 10000.0

        def _rope_tables(T, head_size, dtype):
            half = head_size // 2
            thetas = BASE ** (-jnp.arange(half, dtype=jnp.float32) / half)
            ang = jnp.arange(T, dtype=jnp.float32)[:, None] * thetas[None, :]
            return (jnp.sin(ang).astype(dtype), jnp.cos(ang).astype(dtype))

        def _apply_rope(x, sin, cos):
            x1 = x[..., 0::2]
            x2 = x[..., 1::2]
            r1 = x1 * cos - x2 * sin
            r2 = x1 * sin + x2 * cos
            return jnp.stack([r1, r2], axis=-1).reshape(x.shape)
        B, T, C = x.shape
        H = NUM_HEADS
        D = C // H
        scale = 1.0 / math.sqrt(D)
        qkv = x @ w_qkv.T + b_qkv
        qkv = qkv.reshape(B, T, 3, H, D)
        qkv = jnp.transpose(qkv, (2, 0, 3, 1, 4))
        q, k, v = (qkv[0], qkv[1], qkv[2])
        sin, cos = _rope_tables(T, D, x.dtype)
        q = _apply_rope(q, sin, cos)
        k = _apply_rope(k, sin, cos)
        att = jnp.einsum('bhtd,bhsd->bhts', q, k) * scale
        causal = jnp.triu(jnp.ones((T, T), dtype=bool), k=1)
        att = jnp.where(causal, -jnp.inf, att)
        att_prob = jax.nn.softmax(att, axis=-1)
        att_v = jnp.einsum('bhts,bhsd->bhtd', att_prob, v)
        att_v = jnp.transpose(att_v, (0, 2, 1, 3)).reshape(B, T, C)
        return att_v @ w_out.T + b_out

    def _L0_attn_b_ref(x, Wq, Wk, Wv, Wa, ba, Wb, bb, Wg, Wo, conv_q_w, conv_q_b, conv_k_w, conv_k_b, conv_v_w, conv_v_b, ln_w, ln_b):
        import jax, jax.numpy as jnp
        import numpy as np
        HID, H, DK, DV, KS = (256, 16, 128, 128, 4)

        def _p(key, shape, scale=0.02):
            return jax.random.normal(key, shape, dtype=jnp.float32) * scale

        def _dwconv_causal(y, w, b):
            out = jax.lax.conv_general_dilated(y.transpose(0, 2, 1), w, window_strides=(1,), padding=[(KS - 1, 0)], feature_group_count=w.shape[0])
            return out.transpose(0, 2, 1) + b

        def _silu(x):
            return x * jax.nn.sigmoid(x)

        def _gated_delta(q, k, v, alpha, beta, scale):
            B, T, nH, _ = q.shape
            qs = q.transpose(1, 0, 2, 3)
            ks = k.transpose(1, 0, 2, 3) * scale
            vs = v.transpose(1, 0, 2, 3)
            al = alpha.transpose(1, 0, 2)
            be = beta.transpose(1, 0, 2)

            def step(S, inp):
                qt, kt, vt, at, bt = inp
                err = jnp.einsum('bhvk,bhk->bhv', S, kt) - vt
                S = at[..., None, None] * S - bt[..., None, None] * err[..., None] * kt[:, :, None, :]
                o = jnp.einsum('bhvk,bhk->bhv', S, qt)
                return (S, o)
            S0 = jnp.zeros((B, nH, DV, DK), dtype=q.dtype)
            _, o = jax.lax.scan(step, S0, (qs, ks, vs, al, be))
            return o.transpose(1, 0, 2, 3)
        B, T, _ = x.shape
        scale = DK ** (-0.5)
        q = _silu(_dwconv_causal(x @ Wq, conv_q_w, conv_q_b))
        k = _silu(_dwconv_causal(x @ Wk, conv_k_w, conv_k_b))
        v = _silu(_dwconv_causal(x @ Wv, conv_v_w, conv_v_b))
        q = q.reshape(B, T, H, DK)
        k = k.reshape(B, T, H, DK)
        v = v.reshape(B, T, H, DV)
        alpha = jax.nn.sigmoid(x @ Wa + ba)
        beta = jax.nn.sigmoid(x @ Wb + bb)
        o = _gated_delta(q, k, v, alpha, beta, scale)
        mu = o.mean(-1, keepdims=True)
        var = ((o - mu) ** 2).mean(-1, keepdims=True)
        o = (o - mu) * jax.lax.rsqrt(var + 1e-05) * ln_w + ln_b
        g = jax.nn.sigmoid(x @ Wg).reshape(B, T, H, DV)
        o = (o * g).reshape(B, T, H * DV)
        return o @ Wo

    def _L0_ffn_ref(x, ln_gamma, ln_beta, spline_bases, spline_slopes, output_scale):
        import jax, jax.numpy as jnp
        import numpy as np
        D_MODEL = 256
        NUM_TILES = 64
        D_SLICE = D_MODEL // NUM_TILES
        TILES_PER_CLUSTER = 8
        NUM_CLUSTERS = NUM_TILES // TILES_PER_CLUSTER
        GRID = 16
        LN_EPS = 1e-05
        DIMS = (np.arange(NUM_TILES)[:, None] * D_SLICE + np.arange(D_SLICE)[None, :]) % D_MODEL
        DIMS = jnp.asarray(DIMS, dtype=jnp.int32)

        def _forward(x, ln_gamma, ln_beta, spline_bases, spline_slopes, output_scale):
            B, S, D = x.shape
            N = B * S
            mu = jnp.mean(x, axis=-1, keepdims=True)
            var = jnp.mean(jnp.square(x - mu), axis=-1, keepdims=True)
            xn = (x - mu) * jax.lax.rsqrt(var + LN_EPS) * ln_gamma + ln_beta
            xf = xn.reshape(N, D)
            slope_sign = jnp.sign(jnp.mean(spline_slopes, axis=-1))
            tile_sigs = jnp.zeros((NUM_TILES, D), dtype=x.dtype)
            tile_sigs = tile_sigs.at[jnp.arange(NUM_TILES)[:, None], DIMS].set(slope_sign)
            cluster_sigs = jnp.sign(tile_sigs.reshape(NUM_CLUSTERS, TILES_PER_CLUSTER, D).mean(axis=1))
            cluster_assign = jnp.arange(NUM_TILES, dtype=jnp.int32) // TILES_PER_CLUSTER
            input_sigs = jnp.sign(xf)
            cluster_scores = input_sigs @ cluster_sigs.T
            best_cluster = jnp.argmax(cluster_scores, axis=-1)
            tile_scores = input_sigs @ tile_sigs.T
            in_cluster = cluster_assign[None, :] == best_cluster[:, None]
            tile_idx = jnp.argmax(jnp.where(in_cluster, tile_scores, -jnp.inf), axis=-1)
            tok_dims = DIMS[tile_idx]
            x_slice = jnp.take_along_axis(xf, tok_dims, axis=1)
            tok_min = x_slice.min(axis=1)
            tok_max = x_slice.max(axis=1)
            onehot = tile_idx[None, :] == jnp.arange(NUM_TILES)[:, None]
            tile_min = jnp.where(onehot, tok_min[None, :], jnp.inf).min(axis=1)
            tile_max = jnp.where(onehot, tok_max[None, :], -jnp.inf).max(axis=1)
            mn = tile_min[tile_idx][:, None]
            mx = tile_max[tile_idx][:, None]
            u = jnp.clip((x_slice - mn) / (mx - mn + 1e-08), 0.0, 1.0 - 1e-06)
            gi = jnp.clip((u * GRID).astype(jnp.int32), 0, GRID - 1)
            j = jnp.arange(D_SLICE)[None, :]
            b = spline_bases[tile_idx[:, None], j, gi]
            s = spline_slopes[tile_idx[:, None], j, gi]
            x_local = (u - gi.astype(u.dtype) / GRID) * GRID
            delta = (b + s * x_local) * output_scale[tile_idx][:, None]
            out = jnp.zeros_like(xf).at[jnp.arange(N)[:, None], tok_dims].set(delta)
            return x + out.reshape(B, S, D)
        return _forward(x, ln_gamma, ln_beta, spline_bases, spline_slopes, output_scale)
    x = L0_attn_a_x
    x = x + _L0_attn_a_ref(_layernorm(x, axis=-1), L0_attn_a_w_qkv, L0_attn_a_b_qkv, L0_attn_a_w_out, L0_attn_a_b_out)
    x = x + _L0_ffn_ref(_layernorm(x, axis=-1), L0_ffn_ln_gamma, L0_ffn_ln_beta, L0_ffn_spline_bases, L0_ffn_spline_slopes, L0_ffn_output_scale)
    x = x + _L0_attn_b_ref(_layernorm(x, axis=-1), L0_attn_b_Wq, L0_attn_b_Wk, L0_attn_b_Wv, L0_attn_b_Wa, L0_attn_b_ba, L0_attn_b_Wb, L0_attn_b_bb, L0_attn_b_Wg, L0_attn_b_Wo, L0_attn_b_conv_q_w, L0_attn_b_conv_q_b, L0_attn_b_conv_k_w, L0_attn_b_conv_k_b, L0_attn_b_conv_v_w, L0_attn_b_conv_v_b, L0_attn_b_ln_w, L0_attn_b_ln_b)
    x = x + _L0_ffn_ref(_layernorm(x, axis=-1), L0_ffn_ln_gamma, L0_ffn_ln_beta, L0_ffn_spline_bases, L0_ffn_spline_slopes, L0_ffn_output_scale)
    return x

_drawn_inputs = setup_inputs


def setup_inputs(seed=0):
    import zlib

    import numpy as np

    out = dict(_drawn_inputs(seed))
    spreads = {'L0_attn_b_ba': (0.0, 0.8),
     'L0_attn_b_bb': (0.0, 0.8),
     'L0_attn_b_conv_q_b': (0.0, 0.331),
     'L0_attn_b_conv_k_b': (0.0, 0.293),
     'L0_attn_b_conv_v_b': (0.0, 0.282),
     'L0_attn_b_ln_w': (1.0, 0.6),
     'L0_attn_b_ln_b': (0.0, 0.332)}
    factors = {'L0_attn_a_b_out': 2.847,
     'L0_attn_b_Wa': 8.0,
     'L0_attn_b_Wb': 7.169,
     'L0_attn_b_Wg': 5.758,
     'L0_ffn_ln_gamma': 7.703,
     'L0_ffn_ln_beta': 6.083,
     'L0_ffn_spline_bases': 6.255,
     'L0_ffn_spline_slopes': 8.0,
     'L0_ffn_output_scale': 8.0}
    for name, (base, spread) in spreads.items():
        noise = np.random.default_rng([zlib.crc32(name.encode()), seed]).standard_normal(out[name].shape)
        drawn = base * np.exp(spread * noise) if base else spread * noise
        out[name] = jnp.asarray(drawn.astype(out[name].dtype))
    for name, factor in factors.items():
        out[name] = (out[name] * factor).astype(out[name].dtype)
    return out
```

```python
from contextlib import ExitStack

import numpy as np

import concourse.bass as bass
from concourse import mybir

F32 = mybir.dt.float32
BF16 = mybir.dt.bfloat16
ALU = mybir.AluOpType
ACT = mybir.ActivationFunctionType
AX = mybir.AxisListType

P = 128
SEQS, SEQ, C = 16, 256, 256
TPS = SEQ // P
TILES = SEQS * TPS
CT = C // P
HEADS, HD = 16, 16
HALF = HD // 2
SLOT = 32
UNITS = 12
EPS = 1e-5
MASKED = -1e30
ROUTES, SLICE, CLUSTER, GRID = 64, 4, 8, 16
TABW = 2 * SLICE * GRID + 3
FG = 4
FSTEPS = TILES // FG
FAR = 1e30
DH, DK = 16, 128
HG = 4
GROUPS = DH // HG
TAPS = 4
BLK = 32
PROBS = HG * TPS
KAPPA2 = 1.0 / DK
KAPPA = float(DK) ** -0.5


def past(count):
    return count + 1


class Chain:

    def __init__(self, eng, sem, base=0):
        self.eng, self.sem, self.base, self.n = eng, sem, base, 0

    def link(self, ins):
        self.n += 1
        ins.then_inc(self.sem, 1)
        self.eng.wait_ge(self.sem, self.base + self.n)


def program(nc, io, stop=99):
    ctx = ExitStack()
    with ctx:
        def sb(name, shape, dt=F32):
            return ctx.enter_context(nc.sbuf_tensor(name, shape, dt))

        def sem(name):
            return ctx.enter_context(nc.semaphore(name))

        bank = [ctx.enter_context(nc.psum_tensor(f"bank{i}", [P, 512], F32)) for i in range(8)]

        stream = sb("stream", [P, TILES, C])
        ident = sb("ident", [P, P])
        ones_row = sb("ones_row", [1, P])
        half_neg = sb("half_neg", [P, TILES])
        moments = sb("moments", [P, TILES, 2])
        rstd = sb("rstd", [P, TILES])
        stats = sb("stats", [P, 8, 6])
        mom8 = sb("mom8", [P, 8, 2])
        pad = sb("pad", [P, 1])

        xT_dram = nc.dram_tensor("xT_scratch", [SEQS, P, CT * SEQ], F32).ap()
        decay_dram = nc.dram_tensor("decay_scratch", [SEQS, DH, SEQ], F32).ap()

        loaded_x = sem("loaded_x")
        loaded_a = sem("loaded_a")
        consts = sem("consts")
        v_step = sem("v_step")
        p_step = sem("p_step")
        a_step = sem("a_step")
        stage_done = sem("stage_done")
        stored = sem("stored")

        stack_a = ExitStack()

        def sa(name, shape, dt=F32):
            return stack_a.enter_context(nc.sbuf_tensor(name, shape, dt))
        w_qkv = sa("w_qkv", [P, CT, 3 * C])
        w_out = sa("w_out", [P, CT, C])
        b_qkv = sa("b_qkv", [1, 3 * C])
        b_out = sa("b_out", [1, C])
        cosT = sa("cosT", [P, TPS, HALF])
        sinT = sa("sinT", [P, TPS, HALF])
        identb = sa("identb", [P, P], BF16)
        maskb = sa("maskb", [P, 2 * P], BF16)
        maskd = sa("maskd", [P, 4, P], BF16)
        masko = sa("masko", [P, 2, 2 * P], BF16)
        xn = sa("xn", [P, TPS, C])
        xT = sa("xT", [P, CT, SEQ])
        rope_t = sa("rope_t", [P, 4, TPS, 2 * HEADS * HALF])
        rot = sa("rot", [P, TPS, 2 * HEADS, SLOT])
        vx = sa("vx", [P, TPS, HEADS, HD + 1])
        qT = sa("qT", [P, 4, SEQ])
        kT = sa("kT", [P, 4, SEQ])
        row_max = sa("row_max", [P, 2, 4])
        prob = sa("prob", [P, 2, 512])
        probT = sa("probT", [P, 2, 512])
        rsum = sa("rsum", [P, TPS, HEADS])
        att = sa("att", [P, TPS, C])
        attT = sa("attT", [P, CT, SEQ])
        stack_a.close()

        stack_f = ExitStack()

        def sf(name, shape, dt=F32):
            return stack_f.enter_context(nc.sbuf_tensor(name, shape, dt))
        gam = sf("gam", [P, C])
        bet = sf("bet", [P, C])
        sl_all = sf("sl_all", [P, C, GRID])
        sl_sum = sf("sl_sum", [P, C])
        sl_sign = sf("sl_sign", [P, C])
        xf = sf("xf", [P, TILES, C])
        onehot = sf("onehot", [P, TILES, ROUTES])
        table = sf("table", [ROUTES, TABW])
        rank = sf("rank", [P, ROUTES])
        kgrid = sf("kgrid", [P, GRID + 1])
        ranki = sf("ranki", [P, ROUTES], mybir.dt.int32)
        kgridi = sf("kgridi", [P, GRID + 1], mybir.dt.int32)
        z = sf("z", [P, FG, C])
        fmom = sf("fmom", [P, FG, 2])
        fvar = sf("fvar", [P, FG])
        frs = sf("frs", [P, FG])
        fmom2 = sf("fmom2", [P, FG, 2])
        fvar2 = sf("fvar2", [P, FG])
        frs2 = sf("frs2", [P, FG])
        sgn = sf("sgn", [P, FG, C])
        tsc = sf("tsc", [P, FG, ROUTES])
        csc = sf("csc", [P, FG, CLUSTER])
        comp = sf("comp", [P, FG, ROUTES])
        best = sf("best", [P, FG])
        smin = sf("smin", [P, FG, ROUTES])
        smax = sf("smax", [P, FG, ROUTES])
        far = sf("far", [P, FG, ROUTES])
        run_min = sf("run_min", [P, FG, ROUTES])
        run_nmax = sf("run_nmax", [P, FG, ROUTES])
        ext = sf("ext", [ROUTES, 2])
        oh_fix = sf("oh_fix", [P, FG, ROUTES])
        ohT = sf("ohT", [ROUTES, FG, P])
        selr = sf("selr", [P, FG, TABW])
        pick = sf("pick", [P, FG, C])
        xs = sf("xs", [P, FG, SLICE])
        u16 = sf("u16", [P, FG, SLICE])
        ge = sf("ge", [P, FG * SLICE, GRID + 1])
        floor1 = sf("floor1", [P, FG * SLICE])
        gmask = sf("gmask", [P, FG, SLICE * GRID])
        bsel = sf("bsel", [P, FG * SLICE])
        ssel = sf("ssel", [P, FG * SLICE])
        tmpg = sf("tmpg", [P, FG, SLICE * GRID])
        delta = sf("delta", [P, FG, SLICE])
        stack_f.close()

        stack_c = ExitStack()

        def sc(name, shape, dt=F32):
            return stack_c.enter_context(nc.sbuf_tensor(name, shape, dt))
        w_ab = sc("w_ab", [P, CT, 2 * DH])
        b_ab = sc("b_ab", [1, 2 * DH])
        b_a = sc("b_a", [DH, 1])
        beta_k = sc("beta_k", [P, TILES, DH])
        beta_q = sc("beta_q", [P, TILES, DH])
        beta = sc("beta", [P, TILES, DH])
        gam_q = sc("gam_q", [P, TILES, DH])
        gam_k = sc("gam_k", [P, TILES, DH])
        ln_w = sc("ln_w", [P, 1])
        ln_b = sc("ln_b", [P, 1])
        conv_w = sc("conv_w", [P, 3, DH, TAPS])
        conv_b = sc("conv_b", [P, 3, DH])
        id_many = sc("id_many", [P, PROBS, P])
        id2c = sc("id2c", [P, BLK])
        cxn = sc("cxn", [P, TPS, C])
        cxT = sc("cxT", [P, CT, SEQ])
        alphaT = sc("alphaT", [DH, SEQ])
        alpha_z = sc("alpha_z", [DH, SEQ])
        alpha_r = sc("alpha_r", [DH, SEQ])
        gam_row = sc("gam_row", [DH, SEQ])
        gprev_row = sc("gprev_row", [DH, SEQ])
        w4 = sc("w4", [P, 4, CT, HG * DK])
        w_o = sc("w_o", [P, HG, C])
        cw = sc("cw", [P, 3, HG, TAPS])
        cb = sc("cb", [P, 3, HG])
        xTb = sc("xTb", [P, CT, SEQ])
        abc = sc("abc", [P, HG, SEQ])
        acc = sc("acc", [P, 3, HG, SEQ])
        kq = sc("kq", [P, HG, TPS, 2, P])
        vT = sc("vT", [P, HG, SEQ])
        gT = sc("gT", [P, HG, SEQ])
        vn = sc("vn", [P, TPS, HG, DK])
        kn = sc("kn", [P, HG, DK])
        dec = sc("dec", [P, HG, SEQ])
        LT = sc("LT", [P, TPS, HG, P])
        MT = sc("MT", [P, TPS, HG, P])
        BDL = sc("BDL", [P, TPS, HG, P])
        BDT = sc("BDT", [P, TPS, HG, P])
        BDN = sc("BDN", [P, TPS, HG, P])
        Cc = sc("Cc", [P, TPS, HG, BLK])
        Rc = sc("Rc", [P, TPS, HG, BLK])
        GT = sc("GT", [P, TPS, HG, P])
        y = sc("y", [P, HG, DK])
        r1 = sc("r1", [P, HG, DK])
        U = sc("U", [P, TPS, HG, DK])
        Uw = sc("Uw", [P, HG, DK])
        wgt = sc("wgt", [P, HG])
        S = sc("S", [P, HG, DK])
        oi = sc("oi", [P, HG, DK])
        o = sc("o", [P, TPS, HG, DK])
        ostat = sc("ostat", [P, PROBS, 6])
        omom = sc("omom", [P, PROBS, 2])
        ovar = sc("ovar", [P, PROBS])
        ors = sc("ors", [P, PROBS])
        oT = sc("oT", [P, TPS, HG, P])
        oG = sc("oG", [P, TPS, HG, P])
        stack_c.close()

        A = {k: sem("A_" + k) for k in (
            "xn", "xTp", "xT", "qkv", "rope", "v", "rotp", "qkT", "score", "shift", "exp", "pT",
            "probT", "av", "att", "attTp", "attT", "yout", "res", "var", "rstd")}
        R = {k: sem("R_" + k) for k in (
            "loaded", "var", "rs", "z", "added", "xf", "sign", "minT", "table", "pass1",
            "fix", "ohTp", "ohT", "selp", "sel", "pick0", "xs", "delta", "scat", "res", "cons")}
        Z = {k: sem("Z_" + k) for k in (
            "w", "wab", "xn", "xTp", "xT", "stored", "abp", "ab", "rows", "gamp", "gam", "cons",
            "var", "rstd",
            "wg", "xin", "abc", "proj", "tap", "conv", "silu", "gate", "vTp", "vn", "kq", "LM",
            "bdl", "t1", "X", "Rr", "Y", "Cev", "Tn", "bdn", "Gp", "Gev", "ap", "yv", "Up", "Uev",
            "Sp", "Sev", "KS", "QS", "r1", "oi", "Op", "oev", "ovar", "ors", "on", "oTp", "oT",
            "oG", "yout", "res", "dec")}

        block = ctx.enter_context(nc.Block())

        @block.sync
        def _(sp):
            for g in range(4):
                n = TILES // 4
                sp.dma_start(stream[:, g * n:(g + 1) * n, :],
                             io["x"][g * n * P:(g + 1) * n * P, :].rearrange("(n p) c -> p n c", p=P)
                             ).then_inc(loaded_x, 16)
            sp.dma_start(w_qkv[:], io["w_qkv"].rearrange("(k p) n -> p k n", p=P)).then_inc(loaded_a, 16)
            sp.dma_start(w_out[:], io["w_out"].rearrange("(k p) n -> p k n", p=P)).then_inc(loaded_a, 16)
            sp.dma_start(b_qkv[:], io["b_qkv"].rearrange("(a n) -> a n", a=1)).then_inc(loaded_a, 16)
            sp.dma_start(b_out[:], io["b_out"].rearrange("(a n) -> a n", a=1)).then_inc(loaded_a, 16)
            sp.dma_start(cosT[:], io["cos"].rearrange("(j p) n -> p j n", p=P)).then_inc(loaded_a, 16)
            sp.dma_start(sinT[:], io["sin"].rearrange("(j p) n -> p j n", p=P)).then_inc(loaded_a, 16)

            def routed_loads():
                row = io["slopes"].rearrange("(a r) j k -> a (r j) k", a=1)
                sp.dma_start(gam[:], io["gamma"].rearrange("(a n) -> a n", a=1).broadcast_to([P, C])).then_inc(R["loaded"], 16)
                sp.dma_start(bet[:], io["beta"].rearrange("(a n) -> a n", a=1).broadcast_to([P, C])).then_inc(R["loaded"], 16)
                sp.dma_start(sl_all[:], row.broadcast_to([P, C, GRID])).then_inc(R["loaded"], 16)
                w = SLICE * GRID
                sp.dma_start(table[:, 0:w], io["bases"].rearrange("r j k -> r (j k)")).then_inc(R["loaded"], 16)
                sp.dma_start(table[:, w:2 * w], io["slopes"].rearrange("r j k -> r (j k)")).then_inc(R["loaded"], 16)
                sp.dma_start(table[:, 2 * w:2 * w + 1], io["oscale"].rearrange("(r a) -> r a", a=1)).then_inc(R["loaded"], 16)

            sp.wait_ge(stage_done, 1)
            if stop > 1:
                routed_loads()
                sp.wait_ge(stage_done, 2)
            if stop > 2:
                sp.dma_start(w_ab[:, :, 0:DH], io["Wa"].rearrange("(k p) n -> p k n", p=P)).then_inc(Z["wab"], 16)
                sp.dma_start(w_ab[:, :, DH:], io["Wb"].rearrange("(k p) n -> p k n", p=P)).then_inc(Z["wab"], 16)
                sp.dma_start(b_ab[:, 0:DH], io["ba"].rearrange("(a n) -> a n", a=1)).then_inc(Z["wab"], 16)
                sp.dma_start(b_ab[:, DH:], io["bb"].rearrange("(a n) -> a n", a=1)).then_inc(Z["wab"], 16)
                sp.dma_start(b_a[:], io["ba"].rearrange("(n a) -> n a", a=1)).then_inc(Z["wab"], 16)
                sp.dma_start(ln_w[:], io["ln_w"].rearrange("(n a) -> n a", a=1)).then_inc(Z["wab"], 16)
                sp.dma_start(ln_b[:], io["ln_b"].rearrange("(n a) -> n a", a=1)).then_inc(Z["wab"], 16)
                for n, k in enumerate("qkv"):
                    sp.dma_start(conv_w[:, n], io[f"cw_{k}"]).then_inc(Z["wab"], 16)
                    sp.dma_start(conv_b[:, n], io[f"cb_{k}"]).then_inc(Z["wab"], 16)
                with sp.Fori(0, SEQS) as b:
                    sp.wait_ge(Z["xT"], past(2 * b + 2))
                    sp.dma_start(xT_dram[b], cxT[:].rearrange("p k t -> p (k t)")).then_inc(Z["stored"], 16)
                    sp.wait_ge(Z["rows"], past(b + 1))
                    sp.dma_start(decay_dram[b], alpha_z[:]).then_inc(Z["stored"], 16)
                sp.wait_ge(Z["stored"], past(32 * SEQS))
                with sp.Fori(0, GROUPS) as g:
                    sp.wait_ge(Z["yout"], past(SEQS * g))
                    for k, w in enumerate(("Wq", "Wk", "Wv", "Wg")):
                        sp.dma_start(w4[:, k], io[w].rearrange("(k p) n -> p k n", p=P)[:, :, bass.ds(g * HG * DK, HG * DK)]).then_inc(Z["wg"], 16)
                    sp.dma_start(w_o[:], io["Wo"].rearrange("(h p) n -> p h n", p=P)[:, bass.ds(g * HG, HG), :]).then_inc(Z["wg"], 16)
                    with sp.Fori(0, SEQS) as b:
                        n = g * SEQS + b
                        sp.wait_ge(Z["proj"], past(8 * n))
                        sp.dma_start(xTb[:].rearrange("p k t -> p (k t)"), xT_dram[b]).then_inc(Z["xin"], 16)
                        sp.wait_ge(Z["dec"], past(n))
                        row = decay_dram.rearrange("b (g h) t -> b g (h t)", g=GROUPS)[bass.ds(b, 1), bass.ds(g, 1), :]
                        sp.dma_start(abc[:].rearrange("p h t -> p (h t)"),
                                     row.rearrange("a b n -> (a b) n").broadcast_to([P, HG * SEQ])).then_inc(Z["abc"], 16)
                sp.wait_ge(stage_done, 3)
            if stop > 3:
                routed_loads()
                sp.wait_ge(stage_done, 4)
            for g in range(4):
                n = TILES // 4
                sp.dma_start(io["out"][g * n * P:(g + 1) * n * P, :].rearrange("(n p) c -> p n c", p=P),
                             stream[:, g * n:(g + 1) * n, :]).then_inc(stored, 16)
            sp.wait_ge(stored, 64)

        @block.gpsimd
        def _(pool):
            for signals in (A, R, Z):
                for signal in signals.values():
                    pool.sem_inc(signal, 1)
            ch = Chain(pool, p_step)
            ch.link(pool.memset(ident[:], 0.0))
            ch.link(pool.affine_select(out=ident[:], in_=ident[:], compare_op=ALU.not_equal, fill=1.0,
                                       base=0, pattern=[[-1, P]], channel_multiplier=1))
            pool.tensor_copy(identb[:], ident[:]).then_inc(consts, 1)
            pool.memset(ones_row[:], 1.0).then_inc(consts, 1)
            pool.memset(half_neg[:], -0.5).then_inc(consts, 1)
            ch.link(pool.memset(maskb[:], 0.0))
            ch.link(pool.affine_select(out=maskb[:, P:], in_=maskb[:, P:], compare_op=ALU.is_ge, fill=MASKED,
                                       base=0, pattern=[[-1, P]], channel_multiplier=1))
            for i in range(4):
                pool.tensor_copy(maskd[:, i], maskb[:, P:]).then_inc(consts, 1)
            for i in range(2):
                pool.tensor_copy(masko[:, i], maskb[:]).then_inc(consts, 1)
            pool.memset(rot[:], 0.0).then_inc(consts, 1)
            pool.memset(vx[:], 1.0).then_inc(consts, 1)
            n0 = ch.n
            pool.wait_ge(A["var"], past(1))
            pool.wait_ge(consts, 3)
            pool.tensor_tensor(rstd[:], rstd[:], half_neg[:], ALU.pow).then_inc(A["rstd"], 1)

            def routed(turn):
                pool.wait_ge(stage_done, 1 + 2 * turn)
                c1 = Chain(pool, p_step, pstep_base(turn))
                c1.link(pool.iota(ranki[:].rearrange("p (c i) -> p c i", c=CLUSTER), [[-P, CLUSTER], [-1, ROUTES // CLUSTER]],
                                  base=0, channel_multiplier=0))
                c1.link(pool.iota(kgridi[:], [[1, GRID + 1]], base=0, channel_multiplier=0))
                pool.tensor_copy(rank[:], ranki[:]).then_inc(R["cons"], 1)
                pool.tensor_copy(kgrid[:], kgridi[:]).then_inc(R["cons"], 1)
                pool.memset(run_min[:], 2 * FAR).then_inc(R["cons"], 1)
                pool.memset(run_nmax[:], 2 * FAR).then_inc(R["cons"], 1)
                with pool.Fori(0, FSTEPS) as s:
                    n = s + FSTEPS * turn
                    pool.wait_ge(R["var"], past(2 * n + 1))
                    pool.tensor_tensor(frs[:], fvar[:], half_neg[:, 0:FG], ALU.pow).then_inc(R["rs"], 1)
                    pool.wait_ge(R["z"], past(n + 1))
                    pool.tensor_tensor(stream[:, bass.ds(s * FG, FG), :], stream[:, bass.ds(s * FG, FG), :], z[:], ALU.add).then_inc(R["added"], 1)
                    pool.wait_ge(R["var"], past(2 * n + 2))
                    pool.tensor_tensor(frs2[:], fvar2[:], half_neg[:, 0:FG], ALU.pow).then_inc(R["rs"], 1)
                with pool.Fori(0, FSTEPS) as s:
                    n = s + FSTEPS * turn
                    pool.wait_ge(R["pass1"], past(turn + 1))
                    pool.wait_ge(R["ohTp"], past(n))
                    pool.wait_ge(R["res"], past(n))
                    pool.tensor_copy(oh_fix[:], onehot[:, bass.ds(s * FG, FG), :]).then_inc(R["fix"], 1)
                    pool.wait_ge(R["fix"], past(n + 1))
                    pool.tensor_tensor(pick[:].rearrange("p f (r j) -> p (f r) j", j=SLICE),
                                       xf[:, bass.ds(s * FG, FG), :].rearrange("p f (r j) -> p (f r) j", j=SLICE),
                                       oh_fix[:].rearrange("p f r -> p (f r)").unsqueeze(2).broadcast_to([P, FG * ROUTES, SLICE]),
                                       ALU.mult).then_inc(R["pick0"], 1)

            def pstep_base(turn):
                return n0 + 2 * turn

            if stop > 1:
                routed(0)
            if stop > 2:
                pool.wait_ge(stage_done, 2)
                base = n0 + 4
                cc = Chain(pool, p_step, base)
                for i in range(PROBS):
                    pool.tensor_copy(id_many[:, i], ident[:]).then_inc(Z["cons"], 1)
                for q in range(P // BLK):
                    qs = slice(q * BLK, (q + 1) * BLK)
                    pool.wait_ge(Z["cons"], past(PROBS + q))
                    pool.tensor_scalar(id2c[qs, :], ident[qs, q * BLK:(q + 1) * BLK], 2.0, 0.0, ALU.mult, ALU.add).then_inc(Z["cons"], 1)
                pool.wait_ge(Z["cons"], past(PROBS + P // BLK))
                for m in (BDL, BDT, BDN):
                    pool.memset(m[:], 0.0).then_inc(Z["cons"], 1)
                pool.tensor_copy(LT[:].rearrange("p c h t -> p (c h) t")[:, :, 0:1], id_many[:, :, 0:1]).then_inc(Z["cons"], 1)
                pool.wait_ge(Z["var"], past(1))
                pool.tensor_tensor(rstd[:], rstd[:], half_neg[:], ALU.pow).then_inc(Z["rstd"], 1)
                with pool.Fori(0, GROUPS * SEQS) as n:
                    pool.wait_ge(Z["ovar"], past(n + 1))
                    pool.tensor_tensor(ors[:], ovar[:], half_neg[:, 0:PROBS], ALU.pow).then_inc(Z["ors"], 1)
                    for c in range(TPS):
                        pool.wait_ge(Z["oT"], past(2 * n + c + 1))
                        pool.wait_ge(Z["gate"], past(2 * n + 2))
                        pool.wait_ge(Z["yout"], past(n))
                        pool.tensor_tensor(oG[:, c], oT[:, c], gT[:, :, c * P:(c + 1) * P], ALU.mult).then_inc(Z["oG"], 1)
            if stop > 3:
                routed(1)

        @block.scalar
        def _(act):
            act.wait_ge(consts, 11)
            with act.Fori(0, SEQS) as b:
                act.wait_ge(A["xTp"], past(b + 1))
                act.copy(xT[:].rearrange("p k t -> p (k t)"), bank[0][:]).then_inc(A["xT"], 1)
                for j in range(TPS):
                    act.wait_ge(A["qkv"], past(2 * b + 2))
                    act.copy(vx[:, j, :, 0:HD], bank[3][:, j * C:(j + 1) * C].rearrange("p (h d) -> p h d", d=HD)).then_inc(A["v"], 1)
                for m in range(4):
                    act.wait_ge(A["rotp"], past(4 * b + m + 1))
                    dst = (qT, kT)[m % 2]
                    act.copy(dst[:, :, (m // 2) * P:(m // 2 + 1) * P], bank[4 + m][:].rearrange("p (g t) -> p g t", g=4)).then_inc(A["qkT"], 1)
                for u in range(UNITS + 1):
                    if u < UNITS:
                        act.wait_ge(A["shift"], past(UNITS * b + u + 1))
                        act.activation(prob[:, u % 2], prob[:, u % 2], ACT.Exp, scale=float(HD) ** -0.5).then_inc(A["exp"], 1)
                    if u >= 1:
                        act.wait_ge(A["pT"], past(UNITS * b + u))
                        if u >= 3:
                            act.wait_ge(A["av"], past(UNITS * b + u - 2))
                        act.copy(probT[:, (u - 1) % 2], bank[6 + (u - 1) % 2][:]).then_inc(A["probT"], 1)
                act.wait_ge(A["attTp"], past(b + 1))
                act.copy(attT[:].rearrange("p k t -> p (k t)"), bank[0][:]).then_inc(A["attT"], 1)

            def routed(turn):
                with act.Fori(0, FSTEPS) as s:
                    n = s + FSTEPS * turn
                    act.wait_ge(R["xf"], past(n + 1))
                    act.activation(sgn[:], xf[:, bass.ds(s * FG, FG), :], ACT.Sign).then_inc(R["sign"], 1)
                with act.Fori(0, FSTEPS) as s:
                    n = s + FSTEPS * turn
                    act.wait_ge(R["ohTp"], past(n + 1))
                    act.copy(ohT[:].rearrange("r f t -> r (f t)"), bank[0][0:ROUTES, :]).then_inc(R["ohT"], 1)
                    act.wait_ge(R["selp"], past(n + 1))
                    act.wait_ge(R["delta"], past(n))
                    for h in range(2):
                        act.copy(selr[:, 2 * h:2 * h + 2, :], bank[1 + h][:].rearrange("p (i w) -> p i w", i=2)[:, :, 0:TABW]).then_inc(R["sel"], 1)

            if stop > 1:
                routed(0)
            if stop > 2:
                act.wait_ge(Z["wab"], past(16 * 13))
                with act.Fori(0, SEQS) as b:
                    act.wait_ge(Z["xTp"], past(b + 1))
                    act.wait_ge(Z["stored"], past(32 * b))
                    for k in range(CT):
                        act.copy(cxT[:, k], bank[0][:, k * SEQ:(k + 1) * SEQ]).then_inc(Z["xT"], 1)
                    act.wait_ge(Z["abp"], past(2 * b + 1))
                    act.activation(beta[:, bass.ds(2 * b, 2), :], bank[1][:, 0:2 * 2 * DH].rearrange("p (j n) -> p j n", j=2)[:, :, DH:], ACT.Sigmoid).then_inc(Z["ab"], 1)
                    act.wait_ge(Z["abp"], past(2 * b + 2))
                    act.wait_ge(Z["rows"], past(b))
                    act.activation(alphaT[:], bank[2][0:DH, 0:SEQ], ACT.Sigmoid, bias=b_a[:]).then_inc(Z["ab"], 1)
                    act.wait_ge(Z["gamp"], past(b + 1))
                    act.mul(gam_q[:, bass.ds(2 * b, 2), :], bank[3][:, 0:2 * DH].rearrange("p (j n) -> p j n", j=2), KAPPA).then_inc(Z["gam"], 1)
                    act.mul(gam_k[:, bass.ds(2 * b, 2), :], bank[3][:, 2 * DH:4 * DH].rearrange("p (j n) -> p j n", j=2), -KAPPA2).then_inc(Z["gam"], 1)
                with act.Fori(0, GROUPS) as g:
                    with act.Fori(0, SEQS) as b:
                        n = g * SEQS + b
                        for kind in range(3):
                            act.wait_ge(Z["proj"], past(8 * n + 2 * kind + 2))
                            act.wait_ge(Z["silu"], past(3 * n))
                            for i in range(HG):
                                act.activation(acc[:, kind, i], bank[2 * kind + i // 2][:, (i % 2) * SEQ:(i % 2 + 1) * SEQ], ACT.Identity,
                                               scale=conv_w[:, kind, bass.ds(g * HG + i, 1), TAPS - 1:TAPS].rearrange("p a b -> p (a b)"),
                                               bias=conv_b[:, kind, bass.ds(g * HG + i, 1)]).then_inc(Z["tap"], 1)
                        act.wait_ge(Z["oG"], past(2 * n))
                        for i in range(2):
                            act.wait_ge(Z["proj"], past(8 * n + 7 + i))
                            act.activation(gT[:, 2 * i:2 * i + 2, :].rearrange("p h t -> p (h t)"), bank[6 + i][:], ACT.Sigmoid).then_inc(Z["gate"], 1)
                        for kind in range(3):
                            act.wait_ge(Z["conv"], past(12 * n + 4 * kind + 4))
                            if kind < 2:
                                dst = kq[:, :, :, 1 - kind, :]
                                src = acc[:, kind].rearrange("p h (c t) -> p h c t", c=TPS)
                            else:
                                dst, src = vT[:], acc[:, kind]
                            act.activation(dst, src, ACT.Silu).then_inc(Z["silu"], 1)
                        for c in range(TPS):
                            act.wait_ge(Z["vTp"], past(3 * n + c + 1))
                            act.copy(vn[:, c].rearrange("p h v -> p (h v)"), bank[4 + c][:]).then_inc(Z["vn"], 1)
                        act.wait_ge(Z["vTp"], past(3 * n + 3))
                        act.copy(kn[:].rearrange("p h v -> p (h v)"), bank[6][:]).then_inc(Z["vn"], 1)
                        act.wait_ge(Z["X"], past(8 * n))
                        act.wait_ge(Z["LM"], past(2 * n + 2))
                        for q in range(P // BLK):
                            qs = slice(q * BLK, (q + 1) * BLK)
                            act.copy(BDL[qs, :, :, qs].rearrange("p c h t -> p (c h) t"),
                                     LT[qs, :, :, qs].rearrange("p c h t -> p (c h) t")).then_inc(Z["bdl"], 1)
                        for lev in range(4):
                            for c in range(TPS):
                                act.wait_ge(Z["Y"], past(8 * n + 2 * lev + c + 1))
                                act.copy(Cc[:, c].rearrange("p h t -> p (h t)"), bank[6 + c][:, 128:256]).then_inc(Z["Cev"], 1)
                        act.wait_ge(Z["Up"], past(2 * n + 1))
                        act.copy(U[:, 0].rearrange("p h v -> p (h v)"), bank[2][:]).then_inc(Z["Uev"], 1)
                        act.wait_ge(Z["Op"], past(2 * n + 1))
                        act.copy(o[:, 0].rearrange("p h v -> p (h v)"), bank[5][:]).then_inc(Z["oev"], 1)
                        act.wait_ge(Z["Sp"], past(n + 1))
                        act.copy(S[:].rearrange("p h v -> p (h v)"), bank[3][:]).then_inc(Z["Sev"], 1)
                        act.wait_ge(Z["QS"], past(n + 1))
                        for i in range(HG):
                            act.activation(oi[:, i], bank[6][:, i * DK:(i + 1) * DK], ACT.Copy,
                                           scale=gam_q[:, bass.ds(2 * b + 1, 1), bass.ds(g * HG + i, 1)].rearrange("p a b -> p (a b)")).then_inc(Z["oi"], 1)
                        act.wait_ge(Z["Up"], past(2 * n + 2))
                        act.copy(U[:, 1].rearrange("p h v -> p (h v)"), bank[2][:]).then_inc(Z["Uev"], 1)
                        for c in range(TPS):
                            act.wait_ge(Z["oTp"], past(2 * n + c + 1))
                            act.activation(oT[:, c].rearrange("p h t -> p (h t)"), bank[c][:], ACT.Identity,
                                           scale=ln_w[:], bias=ln_b[:]).then_inc(Z["oT"], 1)
            if stop > 3:
                routed(1)

        @block.vector
        def _(dve):
            ch = Chain(dve, v_step)
            base = 0

            def all_moments(eps_to, ready):
                with dve.Fori(0, TILES // 8) as t:
                    c = Chain(dve, v_step, base + 3 * t)
                    for i in range(8):
                        ins = dve.bn_stats(stats[:, i, :], stream[:, bass.ds(t * 8 + i, 1), :].rearrange("p a c -> p (a c)"))
                    c.link(ins)
                    dve.memset(pad[:], 0.0)
                    for i in range(8):
                        ins = dve.bn_aggr(mom8[:, i, :], stats[:, i, :])
                    c.link(ins)
                    c.link(dve.tensor_copy(moments[:, bass.ds(t * 8, 8), :], mom8[:]))
                dve.tensor_scalar(rstd[:], moments[:, :, 1], EPS, None, ALU.add).then_inc(ready, 1)
                return base + 3 * (TILES // 8)

            dve.wait_ge(loaded_x, 64)
            base = all_moments(rstd, A["var"])
            dve.wait_ge(A["rstd"], past(1))
            dve.wait_ge(consts, 11)
            dve.wait_ge(loaded_a, 96)
            PER_A = 7
            base_a = base
            with dve.Fori(0, SEQS) as b:
                c = Chain(dve, v_step, base_a + PER_A * b)
                for j in range(TPS):
                    dve.wait_ge(A["xTp"], past(b))
                    dve.tensor_scalar(xn[:, j], stream[:, bass.ds(2 * b + j, 1), :].rearrange("p a c -> p (a c)"),
                                      moments[:, bass.ds(2 * b + j, 1), 0:1].rearrange("p a c -> p (a c)"),
                                      rstd[:, bass.ds(2 * b + j, 1)], ALU.subtract, ALU.mult).then_inc(A["xn"], 1)
                for j in range(TPS):
                    dve.wait_ge(A["qkv"], past(2 * b + j + 1))
                    src = bank[1 + j][:].rearrange("p (h i two) -> p h i two", i=HALF, two=2)
                    cs = cosT[:, j:j + 1, :].broadcast_to([P, 2 * HEADS, HALF])
                    sn = sinT[:, j:j + 1, :].broadcast_to([P, 2 * HEADS, HALF])
                    t = [rope_t[:, m, j].rearrange("p (h i) -> p h i", i=HALF) for m in range(4)]
                    dve.tensor_tensor(t[0], src[:, :, :, 0], cs, ALU.mult)
                    dve.tensor_tensor(t[1], src[:, :, :, 1], sn, ALU.mult)
                    dve.tensor_tensor(t[2], src[:, :, :, 0], sn, ALU.mult)
                    c.link(dve.tensor_tensor(t[3], src[:, :, :, 1], cs, ALU.mult))
                    dve.wait_ge(A["rotp"], past(4 * b))
                    dve.tensor_tensor(rot[:, j, :, 0:HALF], t[0], t[1], ALU.subtract).then_inc(A["rope"], 1)
                    dve.tensor_tensor(rot[:, j, :, HALF:HD], t[2], t[3], ALU.add).then_inc(A["rope"], 1)
                for u in range(UNITS):
                    heads = 4 if u % 3 == 0 else 2
                    sc3 = bank[4 + u % 2][:].rearrange("p (h s) -> p h s", h=heads)
                    dve.wait_ge(A["score"], past(UNITS * b + u + 1))
                    dve.tensor_reduce(row_max[:, u % 2, 0:heads], sc3, AX.X, ALU.max).then_inc(A["res"], 1)
                    dve.wait_ge(A["res"], past(b * (UNITS + 1) + u + 1))
                    if u >= 2:
                        dve.wait_ge(A["pT"], past(UNITS * b + u - 1))
                    dve.tensor_tensor(prob[:, u % 2].rearrange("p (h s) -> p h s", h=heads), sc3,
                                      row_max[:, u % 2, 0:heads].unsqueeze(2).broadcast_to([P, heads, 512 // heads]),
                                      ALU.subtract).then_inc(A["shift"], 1)
                dve.wait_ge(A["av"], past(UNITS * b + UNITS))
                for j in range(TPS):
                    av = bank[(3, 1)[j]][:, 0:HEADS * (HD + 1)].rearrange("p (h d) -> p h d", d=HD + 1)
                    c.link(dve.reciprocal(rsum[:, j, :], av[:, :, HD]))
                    dve.tensor_tensor(att[:, j].rearrange("p (h d) -> p h d", d=HD), av[:, :, 0:HD],
                                      rsum[:, j, :].unsqueeze(2).broadcast_to([P, HEADS, HD]), ALU.mult).then_inc(A["att"], 1)
                dve.wait_ge(A["yout"], past(b + 1))
                x2 = stream[:, bass.ds(2 * b, 2), :].rearrange("p j c -> p (j c)")
                dve.tensor_tensor(x2, x2, bank[2][:], ALU.add).then_inc(A["res"], 1)
                for _ in range(PER_A - c.n):
                    c.link(dve.engine_nop() if False else dve.memset(stats[:, 0, :], 0.0))
            base = base_a + PER_A * SEQS
            dve.wait_ge(A["res"], past(SEQS * (UNITS + 1)))
            dve.sem_inc(stage_done, 1) if False else dve.memset(stats[:, 1, :], 0.0).then_inc(stage_done, 1)

            def routed(turn, base):
                dve.wait_ge(R["loaded"], past(96 * (turn + 1)))
                dve.wait_ge(R["cons"], past(4 * (turn + 1)))
                c = Chain(dve, v_step, base)
                c.link(dve.tensor_reduce(sl_sum[:], sl_all[:], AX.X, ALU.add))
                c.link(dve.tensor_scalar(sl_sign[:], sl_sum[:], 0.0, None, ALU.is_lt))
                c.link(dve.scalar_tensor_tensor(out=sl_sign[:], in0=sl_sum[:], scalar=0.0, in1=sl_sign[:],
                                                op0=ALU.is_gt, op1=ALU.subtract))
                base = base + c.n
                PER = 26
                with dve.Fori(0, FSTEPS) as s:
                    n = s + FSTEPS * turn
                    c = Chain(dve, v_step, base + PER * s)
                    xs4 = stream[:, bass.ds(s * FG, FG), :]
                    for i in range(FG):
                        ins = dve.bn_stats(stats[:, i, :], stream[:, bass.ds(s * FG + i, 1), :].rearrange("p a c -> p (a c)"))
                    c.link(ins)
                    dve.memset(pad[:], 0.0)
                    for i in range(FG):
                        ins = dve.bn_aggr(fmom[:, i, :], stats[:, i, :])
                    c.link(ins)
                    dve.tensor_scalar(fvar[:], fmom[:, :, 1], EPS, None, ALU.add).then_inc(R["var"], 1)
                    dve.wait_ge(R["rs"], past(2 * n + 1))
                    dve.wait_ge(R["added"], past(n))
                    for i in range(FG):
                        ins = dve.tensor_scalar(z[:, i], stream[:, bass.ds(s * FG + i, 1), :].rearrange("p a c -> p (a c)"),
                                                fmom[:, i, 0:1], frs[:, i:i + 1], ALU.subtract, ALU.mult)
                    ins.then_inc(R["z"], 1)
                    dve.wait_ge(R["z"], past(n + 1))
                    for i in range(FG):
                        ins = dve.bn_stats(stats[:, i, :], z[:, i])
                    c.link(ins)
                    dve.memset(pad[:], 0.0)
                    for i in range(FG):
                        ins = dve.bn_aggr(fmom2[:, i, :], stats[:, i, :])
                    c.link(ins)
                    dve.tensor_scalar(fvar2[:], fmom2[:, :, 1], EPS, None, ALU.add).then_inc(R["var"], 1)
                    dve.wait_ge(R["rs"], past(2 * n + 2))
                    xf4 = xf[:, bass.ds(s * FG, FG), :]
                    for i in range(FG):
                        ins = dve.tensor_scalar(z[:, i], z[:, i], fmom2[:, i, 0:1], frs2[:, i:i + 1], ALU.subtract, ALU.mult) \
                            if False else dve.tensor_scalar(xf[:, bass.ds(s * FG + i, 1), :].rearrange("p a c -> p (a c)"), z[:, i],
                                                            fmom2[:, i, 0:1], frs2[:, i:i + 1], ALU.subtract, ALU.mult)
                    c.link(ins)
                    c.link(dve.tensor_tensor(xf4, xf4, gam[:].unsqueeze(1).broadcast_to([P, FG, C]), ALU.mult))
                    dve.tensor_tensor(xf4, xf4, bet[:].unsqueeze(1).broadcast_to([P, FG, C]), ALU.add).then_inc(R["xf"], 1)
                    dve.wait_ge(R["xf"], past(n + 1))
                    dve.memset(pad[:], 0.0)
                    x4 = xf4.rearrange("p f (r j) -> p (f r) j", j=SLICE)
                    dve.tensor_reduce(smin[:].rearrange("p f r -> p (f r)"), x4, AX.X, ALU.min)
                    c.link(dve.tensor_reduce(smax[:].rearrange("p f r -> p (f r)"), x4, AX.X, ALU.max))
                    dve.wait_ge(R["sign"], past(n + 1))
                    c.link(dve.tensor_tensor(sgn[:], sgn[:], sl_sign[:].unsqueeze(1).broadcast_to([P, FG, C]), ALU.mult))
                    c.link(dve.tensor_reduce(tsc[:].rearrange("p f r -> p (f r)"), sgn[:].rearrange("p f (r j) -> p (f r) j", j=SLICE), AX.X, ALU.add))
                    c.link(dve.tensor_reduce(csc[:].rearrange("p f k -> p (f k)"), tsc[:].rearrange("p f (k i) -> p (f k) i", k=CLUSTER), AX.X, ALU.add))
                    c.link(dve.scalar_tensor_tensor(out=comp[:], in0=tsc[:], scalar=float(ROUTES // CLUSTER),
                                                    in1=rank[:].unsqueeze(1).broadcast_to([P, FG, ROUTES]), op0=ALU.mult, op1=ALU.add))
                    cm = comp[:].rearrange("p f (k i) -> p (f k) i", k=CLUSTER)
                    c.link(dve.scalar_tensor_tensor(out=cm, in0=csc[:].rearrange("p f k -> p (f k)").unsqueeze(2).broadcast_to([P, FG * CLUSTER, ROUTES // CLUSTER]),
                                                    scalar=float(P * CLUSTER), in1=cm, op0=ALU.mult, op1=ALU.add))
                    c.link(dve.tensor_reduce(best[:], comp[:], AX.X, ALU.max))
                    oh4 = onehot[:, bass.ds(s * FG, FG), :]
                    c.link(dve.tensor_tensor(oh4, comp[:], best[:].unsqueeze(2).broadcast_to([P, FG, ROUTES]), ALU.is_equal))
                    c.link(dve.tensor_scalar(far[:], oh4, -FAR, FAR, ALU.mult, ALU.add))
                    c.link(dve.tensor_tensor(smin[:], smin[:], far[:], ALU.add))
                    c.link(dve.tensor_tensor(smax[:], far[:], smax[:], ALU.subtract))
                    c.link(dve.tensor_tensor(run_min[:], run_min[:], smin[:], ALU.min))
                    c.link(dve.tensor_tensor(run_nmax[:], run_nmax[:], smax[:], ALU.min))
                    for _ in range(PER - c.n):
                        c.link(dve.memset(pad[:], 0.0))
                base = base + PER * FSTEPS
                dve.memset(pad[:], 0.0).then_inc(R["pass1"], 1)
                dve.wait_ge(R["minT"], past(2 * (turn + 1)))
                c = Chain(dve, v_step, base)
                c.link(dve.tensor_reduce(ext[:, 0:1], bank[3][0:ROUTES, :], AX.X, ALU.min))
                c.link(dve.tensor_reduce(ext[:, 1:2], bank[4][0:ROUTES, :], AX.X, ALU.min))
                w = 2 * SLICE * GRID
                c.link(dve.tensor_copy(table[:, w + 1:w + 2], ext[:, 0:1]))
                c.link(dve.tensor_tensor(ext[:, 0:1], ext[:, 0:1], ext[:, 1:2], ALU.add))
                c.link(dve.tensor_scalar(ext[:, 0:1], ext[:, 0:1], -1.0, 1e-8, ALU.mult, ALU.add))
                dve.reciprocal(table[:, w + 2:w + 3], ext[:, 0:1]).then_inc(R["table"], 1)
                base = base + c.n
                PER2 = 16
                with dve.Fori(0, FSTEPS) as s:
                    n = s + FSTEPS * turn
                    c = Chain(dve, v_step, base + PER2 * s)
                    dve.wait_ge(R["pick0"], past(n + 1))
                    c.link(dve.tensor_reduce(xs[:], pick[:].rearrange("p f (r j) -> p f j r", j=SLICE), AX.X, ALU.add))
                    dve.wait_ge(R["sel"], past(2 * n + 2))
                    mn = selr[:, :, w + 1:w + 2].broadcast_to([P, FG, SLICE])
                    rd = selr[:, :, w + 2:w + 3].broadcast_to([P, FG, SLICE])
                    osc = selr[:, :, w:w + 1].broadcast_to([P, FG, SLICE])
                    c.link(dve.tensor_tensor(xs[:], xs[:], mn, ALU.subtract))
                    c.link(dve.tensor_tensor(xs[:], xs[:], rd, ALU.mult))
                    c.link(dve.tensor_scalar(xs[:], xs[:], 0.0, 1.0 - 1e-6, ALU.max, ALU.min))
                    c.link(dve.tensor_scalar(u16[:], xs[:], float(GRID), None, ALU.mult))
                    uf = u16[:].rearrange("p f j -> p (f j)")
                    c.link(dve.tensor_tensor(ge[:], uf.unsqueeze(2).broadcast_to([P, FG * SLICE, GRID + 1]),
                                             kgrid[:].unsqueeze(1).broadcast_to([P, FG * SLICE, GRID + 1]), ALU.is_ge))
                    c.link(dve.tensor_reduce(floor1[:], ge[:], AX.X, ALU.add))
                    gm = gmask[:].rearrange("p f (j k) -> p (f j) k", k=GRID)
                    c.link(dve.tensor_tensor(gm, ge[:, :, 0:GRID], ge[:, :, 1:GRID + 1], ALU.subtract))
                    hw = SLICE * GRID
                    tg = tmpg[:].rearrange("p f (j k) -> p (f j) k", k=GRID)
                    c.link(dve.tensor_tensor(tmpg[:], gmask[:], selr[:, :, 0:hw], ALU.mult))
                    c.link(dve.tensor_reduce(bsel[:], tg, AX.X, ALU.add))
                    c.link(dve.tensor_tensor(tmpg[:], gmask[:], selr[:, :, hw:2 * hw], ALU.mult))
                    c.link(dve.tensor_reduce(ssel[:], tg, AX.X, ALU.add))
                    c.link(dve.scalar_tensor_tensor(out=uf, in0=uf, scalar=1.0, in1=floor1[:], op0=ALU.add, op1=ALU.subtract)
                           if False else dve.tensor_scalar(floor1[:], floor1[:], -1.0, None, ALU.add))
                    c.link(dve.tensor_tensor(uf, uf, floor1[:], ALU.subtract))
                    c.link(dve.tensor_tensor(ssel[:], ssel[:], uf, ALU.mult))
                    c.link(dve.tensor_tensor(bsel[:], bsel[:], ssel[:], ALU.add))
                    dve.tensor_tensor(delta[:], bsel[:].rearrange("p (f j) -> p f j", j=SLICE), osc, ALU.mult).then_inc(R["delta"], 1)
                    dve.wait_ge(R["delta"], past(n + 1))
                    pk = pick[:].rearrange("p f (r j) -> p f r j", j=SLICE)
                    dve.tensor_tensor(pk, oh_fix[:].unsqueeze(3).broadcast_to([P, FG, ROUTES, SLICE]),
                                      delta[:].unsqueeze(2).broadcast_to([P, FG, ROUTES, SLICE]), ALU.mult).then_inc(R["scat"], 1)
                    dve.wait_ge(R["scat"], past(n + 1))
                    xs4 = stream[:, bass.ds(s * FG, FG), :]
                    dve.tensor_tensor(xs4, xs4, pick[:], ALU.add).then_inc(R["res"], 1)
                    assert c.n == PER2, c.n
                dve.wait_ge(R["res"], past(FSTEPS * (turn + 1)))
                dve.memset(pad[:], 0.0).then_inc(stage_done, 1)
                return base + PER2 * FSTEPS

            if stop > 1:
                base = routed(0, base)
            if stop > 2:
                dve.wait_ge(stage_done, 2)
                base = all_moments(rstd, Z["var"])
                dve.wait_ge(Z["rstd"], past(1))
                PER_P = 4
                base_p = base
                with dve.Fori(0, SEQS) as b:
                    c = Chain(dve, v_step, base_p + PER_P * b)
                    for j in range(TPS):
                        dve.wait_ge(Z["xTp"], past(b))
                        dve.tensor_scalar(cxn[:, j], stream[:, bass.ds(2 * b + j, 1), :].rearrange("p a c -> p (a c)"),
                                          moments[:, bass.ds(2 * b + j, 1), 0:1].rearrange("p a c -> p (a c)"),
                                          rstd[:, bass.ds(2 * b + j, 1)], ALU.subtract, ALU.mult).then_inc(Z["xn"], 1)
                    dve.wait_ge(Z["ab"], past(2 * b + 2))
                    dve.wait_ge(Z["stored"], past(32 * b))
                    dve.wait_ge(Z["gamp"], past(b))
                    c.link(dve.tensor_copy(alpha_z[:], alphaT[:]))
                    c.link(dve.memset(alpha_z[:, 0:SEQ:P], 0.0))
                    c.link(dve.tensor_tensor(alpha_r[:], alphaT[:], alpha_z[:], ALU.subtract))
                    c.link(dve.tensor_tensor_scan(gam_row[:], alpha_z[:], alpha_r[:], 0.0, ALU.mult, ALU.add))
                    dve.memset(gprev_row[:, 0:SEQ:P], 1.0)
                    dve.tensor_copy(gprev_row[:].rearrange("h (c t) -> h c t", c=TPS)[:, :, 1:P],
                                    gam_row[:].rearrange("h (c t) -> h c t", c=TPS)[:, :, 0:P - 1]).then_inc(Z["rows"], 1)
                base = base_p + PER_P * SEQS
                dve.wait_ge(Z["ab"], past(2 * SEQS))
                c = Chain(dve, v_step, base)
                dve.tensor_scalar(beta_k[:], beta[:], KAPPA2, None, ALU.mult)
                c.link(dve.tensor_scalar(beta_q[:], beta[:], KAPPA, None, ALU.mult))
                base = base + c.n
                dve.wait_ge(Z["cons"], past(PROBS + 4 + 4))
                PER_C = 12 * 3 + 2 + 40
                with dve.Fori(0, GROUPS) as g:
                    with dve.Fori(0, SEQS) as b:
                        n = g * SEQS + b
                        c = Chain(dve, v_step, base + PER_C * n)
                        for kind in range(3):
                            for i in range(HG):
                                dve.wait_ge(Z["tap"], past(12 * n + 4 * kind + 2 * (i // 2) + 2))
                                pj = bank[2 * kind + i // 2][:, (i % 2) * SEQ:(i % 2 + 1) * SEQ]
                                for tap in range(1, TAPS):
                                    wcol = conv_w[:, kind, bass.ds(g * HG + i, 1), TAPS - 1 - tap:TAPS - tap].rearrange("p a b -> p (a b)")
                                    ins = dve.scalar_tensor_tensor(out=acc[:, kind, i, tap:], in0=pj[:, 0:SEQ - tap], scalar=wcol,
                                                                   in1=acc[:, kind, i, tap:], op0=ALU.mult, op1=ALU.add)
                                    if tap < TAPS - 1:
                                        c.link(ins)
                                    else:
                                        ins.then_inc(Z["conv"], 1)
                        dve.wait_ge(Z["abc"], past(16 * n + 16))
                        dve.tensor_tensor_scan(dec[:].rearrange("p h t -> p (h t)"), abc[:].rearrange("p h t -> p (h t)"),
                                               id_many[:].rearrange("p n t -> p (n t)"), 0.0, ALU.mult, ALU.add).then_inc(Z["dec"], 1)
                        dve.wait_ge(Z["dec"], past(n + 1))
                        for tc in range(TPS):
                            dve.wait_ge(Z["kq"], past(2 * n + tc + 1))
                            dve.wait_ge(Z["Gp"], past(2 * n))
                            for i in range(HG):
                                src = bank[2 * tc + i // 2][:, (i % 2) * 2 * P:(i % 2 + 1) * 2 * P]
                                bk = beta_k[:, bass.ds(2 * b + tc, 1), bass.ds(g * HG + i, 1)].rearrange("p a b -> p (a b)")
                                bq = beta_q[:, bass.ds(2 * b + tc, 1), bass.ds(g * HG + i, 1)].rearrange("p a b -> p (a b)")
                                dve.scalar_tensor_tensor(out=LT[:, tc, i, 1:P], in0=src[:, 1:P], scalar=bk,
                                                         in1=dec[:, i, tc * P:tc * P + P - 1], op0=ALU.mult, op1=ALU.mult)
                                ins = dve.scalar_tensor_tensor(out=MT[:, tc, i, :], in0=src[:, P:2 * P], scalar=bq,
                                                               in1=dec[:, i, tc * P:(tc + 1) * P], op0=ALU.mult, op1=ALU.mult)
                            c.link(ins)
                            dve.tensor_tensor(LT[:, tc, :, 1:P], LT[:, tc, :, 1:P], id_many[:, 0:HG, 1:P], ALU.add).then_inc(Z["LM"], 1)
                        dve.wait_ge(Z["LM"], past(2 * n + 2))
                        dve.wait_ge(Z["Up"], past(2 * n))
                        for q in range(P // BLK):
                            qs = slice(q * BLK, (q + 1) * BLK)
                            qc = slice(q * BLK, (q + 1) * BLK)
                            c_ = LT[qs, :, :, qc].rearrange("p c h t -> p (c h) t")
                            ins = dve.tensor_tensor(BDT[qs, :, :, qc].rearrange("p c h t -> p (c h) t"),
                                                    id2c[qs, :].unsqueeze(1).broadcast_to([BLK, PROBS, BLK]), c_, ALU.subtract)
                            c.link(ins)
                        for q in range(P // BLK):
                            qs = slice(q * BLK, (q + 1) * BLK)
                            c.link(dve.transpose(Cc[qs].rearrange("p c h t -> p (c h) t"), BDT[qs, :, :, qs].rearrange("p c h t -> p (c h) t")))
                        dve.memset(pad[:], 0.0).then_inc(Z["t1"], 1)
                        for lev in range(4):
                            for tc in range(TPS):
                                dve.wait_ge(Z["X"], past(8 * n + 2 * lev + tc + 1))
                                dve.tensor_tensor(Rc[:, tc], id2c[:].unsqueeze(1).broadcast_to([P, HG, BLK]),
                                                  bank[6 + tc][:, 0:HG * BLK].rearrange("p (h t) -> p h t", t=BLK), ALU.subtract).then_inc(Z["Rr"], 1)
                            for tc in range(TPS):
                                dve.wait_ge(Z["Cev"], past(8 * n + 2 * lev + tc + 1))
                                for q in range(P // BLK):
                                    qs = slice(q * BLK, (q + 1) * BLK)
                                    ins = dve.transpose(BDT[qs, tc, :, qs], Cc[qs, tc])
                                ins.then_inc(Z["Tn"], 1)
                        for q in range(P // BLK):
                            qs = slice(q * BLK, (q + 1) * BLK)
                            ins = dve.tensor_copy(BDN[qs, :, :, qs].rearrange("p c h t -> p (c h) t"), Cc[qs].rearrange("p c h t -> p (c h) t"))
                        ins.then_inc(Z["bdn"], 1)
                        for tc in range(TPS):
                            dve.wait_ge(Z["Gp"], past(2 * n + tc + 1))
                            dve.tensor_tensor(GT[:, tc], id_many[:, 0:HG], bank[tc][:].rearrange("p (h t) -> p h t", h=HG), ALU.subtract).then_inc(Z["Gev"], 1)
                        for tc in range(TPS):
                            if tc == 0:
                                rhs = vn[:, 0]
                            else:
                                dve.wait_ge(Z["KS"], past(n + 1))
                                dve.wait_ge(Z["vn"], past(3 * n + 2))
                                for i in range(HG):
                                    gk = gam_k[:, bass.ds(2 * b + 1, 1), bass.ds(g * HG + i, 1)].rearrange("p a b -> p (a b)")
                                    ins = dve.scalar_tensor_tensor(out=r1[:, i], in0=bank[4][:, i * DK:(i + 1) * DK], scalar=gk,
                                                                   in1=vn[:, 1, i], op0=ALU.mult, op1=ALU.add)
                                ins.then_inc(Z["r1"], 1)
                                dve.wait_ge(Z["r1"], past(n + 1))
                                rhs = r1[:]
                            for sw in range(3):
                                dve.wait_ge(Z["ap"], past(6 * n + 3 * tc + sw + 1))
                                dve.tensor_tensor(y[:], rhs, bank[7][:].rearrange("p (h v) -> p h v", h=HG), ALU.add).then_inc(Z["yv"], 1)
                            if tc == 0:
                                c.link(dve.tensor_tensor(wgt[:], dec[:, :, P - 1], beta[:, bass.ds(2 * b, 1), bass.ds(g * HG, HG)].rearrange("p a b -> p (a b)"), ALU.mult))
                                dve.wait_ge(Z["Uev"], past(2 * n + 1))
                                dve.tensor_tensor(Uw[:], U[:, 0], wgt[:].unsqueeze(2).broadcast_to([P, HG, DK]), ALU.mult).then_inc(Z["Uev"], 0) if False else \
                                    c.link(dve.tensor_tensor(Uw[:], U[:, 0], wgt[:].unsqueeze(2).broadcast_to([P, HG, DK]), ALU.mult))
                                dve.memset(pad[:], 0.0).then_inc(Z["on"], 1)
                        dve.wait_ge(Z["Op"], past(2 * n + 2))
                        dve.wait_ge(Z["oi"], past(4 * n + 4))
                        dve.tensor_tensor(o[:, 1], oi[:], bank[5][:].rearrange("p (h v) -> p h v", h=HG), ALU.add).then_inc(Z["oev"], 1)
                        dve.wait_ge(Z["oev"], past(2 * n + 2))
                        of = o[:].rearrange("p c h v -> p (c h) v")
                        for m in range(PROBS):
                            ins = dve.bn_stats(ostat[:, m], of[:, m])
                        c.link(ins)
                        dve.memset(pad[:], 0.0)
                        for m in range(PROBS):
                            ins = dve.bn_aggr(omom[:, m], ostat[:, m])
                        c.link(ins)
                        dve.tensor_scalar(ovar[:], omom[:, :, 1], EPS, None, ALU.add).then_inc(Z["ovar"], 1)
                        dve.wait_ge(Z["ors"], past(n + 1))
                        for m in range(PROBS):
                            ins = dve.tensor_scalar(of[:, m], of[:, m], omom[:, m, 0:1], ors[:, m:m + 1], ALU.subtract, ALU.mult)
                        ins.then_inc(Z["on"], 1)
                        dve.wait_ge(Z["yout"], past(n + 1))
                        x2 = stream[:, bass.ds(2 * b, 2), :].rearrange("p j c -> p (j c)")
                        dve.tensor_tensor(x2, x2, bank[3][:], ALU.add).then_inc(Z["res"], 1)
                        for _ in range(PER_C - c.n):
                            c.link(dve.memset(pad[:], 0.0))
                base = base + PER_C * GROUPS * SEQS
                dve.wait_ge(Z["res"], past(GROUPS * SEQS))
                dve.memset(pad[:], 0.0).then_inc(stage_done, 1)
            if stop > 3:
                base = routed(1, base)

        @block.tensor
        def _(pe):
            pe.wait_ge(loaded_a, 96)
            pe.wait_ge(consts, 11)
            with pe.Fori(0, SEQS) as b:
                pe.wait_ge(A["xn"], past(2 * b + 2))
                pe.wait_ge(A["attT"], past(b))
                for k in range(CT):
                    for j in range(TPS):
                        mm = pe.transpose(bank[0][:, k * SEQ + j * P:k * SEQ + (j + 1) * P], xn[:, j, k * P:(k + 1) * P], ident[:])
                mm.then_inc(A["xTp"], 1)
                pe.wait_ge(A["xT"], past(b + 1))
                pe.wait_ge(A["att"], past(2 * b))
                pe.wait_ge(A["res"], past(b * (UNITS + 1)))
                for j in range(TPS):
                    for dst, lo, hi in ((bank[1 + j][:], 0, 2 * C), (bank[3][:, j * C:(j + 1) * C], 2 * C, 3 * C)):
                        pe.matmul(dst, ones_row[:], b_qkv[:, lo:hi], start=True, stop=False)
                        for k in range(CT):
                            mm = pe.matmul(dst, xT[:, k, j * P:(j + 1) * P], w_qkv[:, k, lo:hi], start=False, stop=(k == CT - 1))
                    mm.then_inc(A["qkv"], 1)
                for m in range(4):
                    j, qk = m // 2, m % 2
                    pe.wait_ge(A["rope"], past(4 * b + 2 * j + 2))
                    for g in range(4):
                        h0 = qk * HEADS + 4 * g
                        mm = pe.transpose(bank[4 + m][:, g * P:(g + 1) * P],
                                          rot[:, j, h0:h0 + 4, :].rearrange("p h d -> p (h d)"), ident[:])
                    mm.then_inc(A["rotp"], 1)
                pe.wait_ge(A["qkT"], past(4 * b + 4))

                def heads_of(u):
                    r, part = u // 3, u % 3
                    return [(g, r) for g in (range(4) if part == 0 else (2 * (part - 1), 2 * (part - 1) + 1))], (0 if part == 0 else 1)

                def scores(u):
                    hs, j = heads_of(u)
                    bk = bank[4 + u % 2]
                    if u >= 2:
                        pe.wait_ge(A["shift"], past(UNITS * b + u - 1))
                    pe.matmul(bk[:], identb[:], (maskd if j == 0 else masko)[:].rearrange("p a s -> p (a s)"), start=True, stop=True)
                    w = (j + 1) * P
                    for m, (g, r) in enumerate(hs):
                        pr = slice(SLOT * r, SLOT * r + HD)
                        mm = pe.matmul(bk[:, m * w:(m + 1) * w], qT[pr, g, j * P:(j + 1) * P], kT[pr, g, 0:w], start=False,
                                       stop=True, skip_group_check=True)
                    mm.then_inc(A["score"], 1)

                def weigh(u):
                    pe.wait_ge(A["exp"], past(UNITS * b + u + 1))
                    if u >= 2:
                        pe.wait_ge(A["probT"], past(UNITS * b + u - 1))
                    for m in range(4):
                        mm = pe.transpose(bank[6 + u % 2][:, m * P:(m + 1) * P], prob[:, u % 2, m * P:(m + 1) * P], ident[:])
                    mm.then_inc(A["pT"], 1)

                def apply(u):
                    hs, j = heads_of(u)
                    pe.wait_ge(A["probT"], past(UNITS * b + u + 1))
                    if u == 0:
                        pe.wait_ge(A["v"], past(2 * b + 2))
                    for m, (g, r) in enumerate(hs):
                        h = 4 * g + r
                        for st in range(j + 1):
                            mm = pe.matmul(bank[(3, 1)[j]][:, h * (HD + 1):(h + 1) * (HD + 1)],
                                           probT[:, u % 2, (m * (j + 1) + st) * P:(m * (j + 1) + st + 1) * P], vx[:, st, h, :],
                                           start=(st == 0), stop=(st == j))
                    mm.then_inc(A["av"], 1)

                for u in range(UNITS + 2):
                    if u < UNITS:
                        scores(u)
                    if 1 <= u <= UNITS:
                        weigh(u - 1)
                    if u >= 2:
                        apply(u - 2)
                pe.wait_ge(A["att"], past(2 * b + 2))
                for k in range(CT):
                    for j in range(TPS):
                        mm = pe.transpose(bank[0][:, k * SEQ + j * P:k * SEQ + (j + 1) * P], att[:, j, k * P:(k + 1) * P], ident[:])
                mm.then_inc(A["attTp"], 1)
                pe.wait_ge(A["attT"], past(b + 1))
                for j in range(TPS):
                    dst = bank[2][:, j * C:(j + 1) * C]
                    pe.matmul(dst, ones_row[:], b_out[:], start=True, stop=False)
                    for k in range(CT):
                        mm = pe.matmul(dst, attT[:, k, j * P:(j + 1) * P], w_out[:, k, :], start=False, stop=(k == CT - 1))
                mm.then_inc(A["yout"], 1)

            def routed(turn):
                pe.wait_ge(R["pass1"], past(turn + 1))
                for m, src in enumerate((run_min, run_nmax)):
                    for i in range(FG):
                        mm = pe.transpose(bank[3 + m][0:ROUTES, i * P:(i + 1) * P], src[:, i, :], ident[:])
                    mm.then_inc(R["minT"], 1)
                pe.wait_ge(R["table"], past(turn + 1))
                with pe.Fori(0, FSTEPS) as s:
                    n = s + FSTEPS * turn
                    pe.wait_ge(R["fix"], past(n + 1))
                    pe.transpose(bank[0][:, 0:P], ident[:], ident[:])
                    for i in range(FG):
                        mm = pe.transpose(bank[0][0:ROUTES, i * P:(i + 1) * P], oh_fix[:, i, :], ident[:])
                    mm.then_inc(R["ohTp"], 1)
                    pe.wait_ge(R["ohT"], past(n + 1))
                    pe.wait_ge(R["sel"], past(2 * n))
                    for i in range(FG):
                        mm = pe.matmul(bank[1 + i // 2][:, (i % 2) * 256:(i % 2) * 256 + TABW], ohT[:, i, :], table[:], start=True, stop=True)
                    mm.then_inc(R["selp"], 1)

            if stop > 1:
                routed(0)
            if stop > 2:
                pe.wait_ge(Z["wab"], past(16 * 13))
                with pe.Fori(0, SEQS) as b:
                    pe.wait_ge(Z["xn"], past(2 * b + 2))
                    for k in range(CT):
                        for j in range(TPS):
                            mm = pe.transpose(bank[0][:, k * SEQ + j * P:k * SEQ + (j + 1) * P], cxn[:, j, k * P:(k + 1) * P], ident[:])
                    mm.then_inc(Z["xTp"], 1)
                    pe.wait_ge(Z["xT"], past(2 * b + 2))
                    for j in range(TPS):
                        dst = bank[1][:, j * 2 * DH:(j + 1) * 2 * DH]
                        pe.matmul(dst, ones_row[:], b_ab[:], start=True, stop=False)
                        for k in range(CT):
                            mm = pe.matmul(dst, cxT[:, k, j * P:(j + 1) * P], w_ab[:, k, :], start=False, stop=(k == CT - 1))
                    mm.then_inc(Z["abp"], 1)
                    for k in range(CT):
                        mm = pe.matmul(bank[2][0:DH, 0:SEQ], w_ab[:, k, 0:DH], cxT[:, k, :], start=(k == 0), stop=(k == CT - 1))
                    mm.then_inc(Z["abp"], 1)
                    pe.wait_ge(Z["rows"], past(b + 1))
                    pe.wait_ge(Z["gam"], past(2 * b))
                    pe.transpose(bank[3][:, 0:P], ident[:], ident[:])
                    for m, src in enumerate((gam_row, gprev_row)):
                        for j in range(TPS):
                            mm = pe.transpose(bank[3][:, (2 * m + j) * DH:(2 * m + j + 1) * DH], src[:, j * P:(j + 1) * P], ident[0:DH, 0:DH])
                    mm.then_inc(Z["gamp"], 1)
                pe.wait_ge(Z["ab"], past(2 * SEQS))
                pe.wait_ge(Z["gam"], past(2 * SEQS))
                with pe.Fori(0, GROUPS) as g:
                    with pe.Fori(0, SEQS) as b:
                        n = g * SEQS + b
                        pe.wait_ge(Z["wg"], past(80 * g + 80))
                        pe.wait_ge(Z["xin"], past(16 * n + 16))
                        pe.wait_ge(Z["res"], past(n))
                        for m in range(8):
                            for i in range(2):
                                h = 2 * (m % 2) + i
                                for k in range(CT):
                                    mm = pe.matmul(bank[m][:, i * SEQ:(i + 1) * SEQ], w4[:, m // 2, k, h * DK:(h + 1) * DK], xTb[:, k, :],
                                                   start=(k == 0), stop=(k == CT - 1))
                            mm.then_inc(Z["proj"], 1)
                        pe.wait_ge(Z["silu"], past(3 * n + 2))
                        pe.wait_ge(Z["conv"], past(12 * n + 8))
                        for c in range(TPS):
                            for i in range(HG):
                                mm = pe.matmul(bank[2 * c + i // 2][:, (i % 2) * 2 * P:(i % 2 + 1) * 2 * P], kq[:, i, c, 0, :],
                                               kq[:, i, c].rearrange("p a t -> p (a t)"), start=True, stop=True)
                            mm.then_inc(Z["kq"], 1)
                        pe.wait_ge(Z["silu"], past(3 * n + 3))
                        for c in range(TPS):
                            for i in range(HG):
                                mm = pe.transpose(bank[4 + c][:, i * DK:(i + 1) * DK], vT[:, i, c * P:(c + 1) * P], ident[:])
                            mm.then_inc(Z["vTp"], 1)
                        pe.wait_ge(Z["gate"], past(2 * n + 2))
                        for i in range(HG):
                            mm = pe.transpose(bank[6][:, i * DK:(i + 1) * DK], kq[:, i, 0, 0, :], ident[:])
                        mm.then_inc(Z["vTp"], 1)
                        pe.wait_ge(Z["vn"], past(3 * n + 3))
                        pe.wait_ge(Z["bdl"], past(4 * n + 4))
                        pe.wait_ge(Z["t1"], past(n + 1))
                        for lev in range(4):
                            for c in range(TPS):
                                if lev:
                                    pe.wait_ge(Z["Cev"], past(8 * n + 2 * lev - 1 + c))
                                for i in range(HG):
                                    mm = pe.matmul(bank[6 + c][:, i * BLK:(i + 1) * BLK], BDL[:, c, i], Cc[:, c, i], start=True, stop=True)
                                mm.then_inc(Z["X"], 1)
                            for c in range(TPS):
                                pe.wait_ge(Z["Rr"], past(8 * n + 2 * lev + c + 1))
                                if lev:
                                    pe.wait_ge(Z["Tn"], past(8 * n + 2 * lev - 1 + c))
                                for i in range(HG):
                                    mm = pe.matmul(bank[6 + c][:, 128 + i * BLK:128 + (i + 1) * BLK], BDT[:, c, i], Rc[:, c, i], start=True, stop=True)
                                mm.then_inc(Z["Y"], 1)
                        pe.wait_ge(Z["bdn"], past(n + 1))
                        for c in range(TPS):
                            for i in range(HG):
                                mm = pe.matmul(bank[c][:, i * P:(i + 1) * P], BDN[:, c, i], LT[:, c, i], start=True, stop=True)
                            mm.then_inc(Z["Gp"], 1)

                        def solve(c, rhs):
                            for sw in range(3):
                                src = rhs if sw == 0 else y
                                if sw:
                                    pe.wait_ge(Z["yv"], past(6 * n + 3 * c + sw))
                                for i in range(HG):
                                    mm = pe.matmul(bank[7][:, i * DK:(i + 1) * DK], GT[:, c, i], src[:, i], start=True, stop=True)
                                mm.then_inc(Z["ap"], 1)
                            pe.wait_ge(Z["yv"], past(6 * n + 3 * c + 3))
                            for i in range(HG):
                                mm = pe.matmul(bank[2][:, i * DK:(i + 1) * DK], BDT[:, c, i], y[:, i], start=True, stop=True)
                            mm.then_inc(Z["Up"], 1)

                        pe.wait_ge(Z["Gev"], past(2 * n + 1))
                        pe.wait_ge(Z["Tn"], past(8 * n + 8))
                        solve(0, vn[:, 0])
                        pe.wait_ge(Z["Uev"], past(2 * n + 1))
                        for i in range(HG):
                            mm = pe.matmul(bank[5][:, i * DK:(i + 1) * DK], MT[:, 0, i], U[:, 0, i], start=True, stop=True)
                        mm.then_inc(Z["Op"], 1)
                        pe.wait_ge(Z["on"], past(2 * n + 1))
                        for i in range(HG):
                            mm = pe.matmul(bank[3][:, i * DK:(i + 1) * DK], kn[:, i], Uw[:, i], start=True, stop=True)
                        mm.then_inc(Z["Sp"], 1)
                        pe.wait_ge(Z["Sev"], past(n + 1))
                        for a, sg in ((0, "KS"), (1, "QS")):
                            for i in range(HG):
                                mm = pe.matmul(bank[4 + 2 * a][:, i * DK:(i + 1) * DK], kq[:, i, 1, a, :], S[:, i], start=True, stop=True)
                            mm.then_inc(Z[sg], 1)
                        pe.wait_ge(Z["r1"], past(n + 1))
                        pe.wait_ge(Z["Gev"], past(2 * n + 2))
                        solve(1, r1)
                        pe.wait_ge(Z["Uev"], past(2 * n + 2))
                        pe.wait_ge(Z["oev"], past(2 * n + 1))
                        for i in range(HG):
                            mm = pe.matmul(bank[5][:, i * DK:(i + 1) * DK], MT[:, 1, i], U[:, 1, i], start=True, stop=True)
                        mm.then_inc(Z["Op"], 1)
                        pe.wait_ge(Z["on"], past(2 * n + 2))
                        for c in range(TPS):
                            for i in range(HG):
                                mm = pe.transpose(bank[c][:, i * P:(i + 1) * P], o[:, c, i], ident[:])
                            mm.then_inc(Z["oTp"], 1)
                        for c in range(TPS):
                            pe.wait_ge(Z["oG"], past(2 * n + c + 1))
                            for i in range(HG):
                                mm = pe.matmul(bank[3][:, c * C:(c + 1) * C], oG[:, c, i], w_o[:, i], start=(i == 0), stop=(i == HG - 1))
                        mm.then_inc(Z["yout"], 1)
            if stop > 3:
                routed(1)


def kernel(**inputs):
    import concourse.bacc as bacc
    from concourse.bass_utils import run_bass_kernel_spmd

    a, d, f = "L0_attn_a_", "L0_attn_b_", "L0_ffn_"
    nc = bacc.Bacc("TRN2", target_bir_lowering=False, num_devices=1)
    theta = (np.float32(10000.0) ** (-np.arange(HALF, dtype=np.float32) / np.float32(HALF))).astype(np.float32)
    angle = np.arange(SEQ, dtype=np.float32)[:, None] * theta[None, :]
    get = {k: np.asarray(v) for k, v in inputs.items()}
    arrays = {
        "x": get[a + "x"].reshape(-1, C), "w_qkv": get[a + "w_qkv"].T, "w_out": get[a + "w_out"].T,
        "b_qkv": get[a + "b_qkv"], "b_out": get[a + "b_out"], "cos": np.cos(angle), "sin": np.sin(angle),
        "gamma": get[f + "ln_gamma"], "beta": get[f + "ln_beta"], "bases": get[f + "spline_bases"],
        "slopes": get[f + "spline_slopes"], "oscale": get[f + "output_scale"],
        "ln_w": get[d + "ln_w"], "ln_b": get[d + "ln_b"], "ba": get[d + "ba"], "bb": get[d + "bb"],
        "Wa": get[d + "Wa"], "Wb": get[d + "Wb"], "Wq": get[d + "Wq"], "Wk": get[d + "Wk"],
        "Wv": get[d + "Wv"], "Wg": get[d + "Wg"], "Wo": get[d + "Wo"],
    }
    for k in "qkv":
        arrays[f"cw_{k}"] = get[d + f"conv_{k}_w"].reshape(DH, DK, TAPS).transpose(1, 0, 2)
        arrays[f"cb_{k}"] = get[d + f"conv_{k}_b"].reshape(DH, DK).T
    arrays = {k: np.ascontiguousarray(v) for k, v in arrays.items()}
    io = {k: nc.dram_tensor(f"in_{k}", v.shape, mybir.dt.from_np(v.dtype), kind="ExternalInput").ap() for k, v in arrays.items()}
    io["out"] = nc.dram_tensor("out", [SEQS * SEQ, C], F32, kind="ExternalOutput").ap()
    program(nc, io)
    r = run_bass_kernel_spmd(nc, [{f"in_{k}": v for k, v in arrays.items()}], core_ids=[0])
    return r.results[0]["out"].reshape(SEQS, SEQ, C)
```

```python
from contextlib import ExitStack

import numpy as np

import concourse.bass as bass
from concourse import mybir

F32 = mybir.dt.float32
BF16 = mybir.dt.bfloat16
ALU = mybir.AluOpType
ACT = mybir.ActivationFunctionType
AX = mybir.AxisListType

P = 128
SEQS, SEQ, C = 16, 256, 256
TPS = SEQ // P
TILES = SEQS * TPS
CT = C // P
HEADS, HD = 16, 16
HALF = HD // 2
SLOT = 32
UNITS = 12
EPS = 1e-5
MASKED = -1e30
ROUTES, SLICE, CLUSTER, GRID = 64, 4, 8, 16
TABW = 2 * SLICE * GRID + 3
FG = 4
FSTEPS = TILES // FG
FAR = 1e30
DH, DK = 16, 128
HG = 4
GROUPS = DH // HG
TAPS = 4
BLK = 32
PROBS = HG * TPS
KAPPA2 = 1.0 / DK
KAPPA = float(DK) ** -0.5


def past(count):
    return count + 1


STEPS = GROUPS * SEQS


def pipeline(eng, slot):
    slot(0, None, 0)
    with eng.Fori(0, (STEPS - 2) // 2) as m:
        slot(2 * m + 1, 2 * m, 1)
        slot(2 * m + 2, 2 * m + 1, 0)
    slot(STEPS - 1, STEPS - 2, 1)
    slot(None, STEPS - 1, 0)


class Chain:

    def __init__(self, eng, sem, base=0):
        self.eng, self.sem, self.base, self.n = eng, sem, base, 0

    def mark(self, ins):
        self.n += 1
        ins.then_inc(self.sem, 1)
        return self.n

    def wait(self, n):
        self.eng.wait_ge(self.sem, self.base + n)

    def link(self, ins):
        self.n += 1
        ins.then_inc(self.sem, 1)
        self.eng.wait_ge(self.sem, self.base + self.n)


def program(nc, io, stop=99):
    ctx = ExitStack()
    with ctx:
        def sb(name, shape, dt=F32):
            return ctx.enter_context(nc.sbuf_tensor(name, shape, dt))

        def sem(name):
            return ctx.enter_context(nc.semaphore(name))

        bank = [ctx.enter_context(nc.psum_tensor(f"bank{i}", [P, 512], F32)) for i in range(8)]

        stream = sb("stream", [P, TILES, C])
        ident = sb("ident", [P, P])
        ones_row = sb("ones_row", [1, P])
        half_neg = sb("half_neg", [P, TILES])
        moments = sb("moments", [P, TILES, 2])
        rstd = sb("rstd", [P, TILES])
        stats = sb("stats", [P, 8, 6])
        mom8 = sb("mom8", [P, 8, 2])
        pad = sb("pad", [P, 1])

        xT_dram = nc.dram_tensor("xT_scratch", [SEQS, P, CT * SEQ], F32).ap()
        decay_dram = nc.dram_tensor("decay_scratch", [SEQS, DH, SEQ], F32).ap()

        loaded_x = sem("loaded_x")
        loaded_a = sem("loaded_a")
        consts = sem("consts")
        v_step = sem("v_step")
        p_step = sem("p_step")
        a_step = sem("a_step")
        stage_done = sem("stage_done")
        stored = sem("stored")

        stack_a = ExitStack()

        def sa(name, shape, dt=F32):
            return stack_a.enter_context(nc.sbuf_tensor(name, shape, dt))
        w_qkv = sa("w_qkv", [P, CT, 3 * C])
        w_out = sa("w_out", [P, CT, C])
        b_qkv = sa("b_qkv", [1, 3 * C])
        b_out = sa("b_out", [1, C])
        cosT = sa("cosT", [P, TPS, HALF])
        sinT = sa("sinT", [P, TPS, HALF])
        identb = sa("identb", [P, P], BF16)
        maskb = sa("maskb", [P, 2 * P], BF16)
        maskd = sa("maskd", [P, 4, P], BF16)
        masko = sa("masko", [P, 2, 2 * P], BF16)
        xn = sa("xn", [P, TPS, C])
        xT = sa("xT", [P, CT, SEQ])
        rope_t = sa("rope_t", [P, 4, TPS, 2 * HEADS * HALF])
        rot = sa("rot", [P, TPS, 2 * HEADS, SLOT])
        vx = sa("vx", [P, TPS, HEADS, HD + 1])
        qT = sa("qT", [P, 4, SEQ])
        kT = sa("kT", [P, 4, SEQ])
        row_max = sa("row_max", [P, 2, 4])
        prob = sa("prob", [P, 2, 512])
        probT = sa("probT", [P, 2, 512])
        rsum = sa("rsum", [P, TPS, HEADS])
        att = sa("att", [P, TPS, C])
        attT = sa("attT", [P, CT, SEQ])
        stack_a.close()

        stack_f = ExitStack()

        def sf(name, shape, dt=F32):
            return stack_f.enter_context(nc.sbuf_tensor(name, shape, dt))
        gam = sf("gam", [P, C])
        bet = sf("bet", [P, C])
        sl_all = sf("sl_all", [P, C, GRID])
        sl_sum = sf("sl_sum", [P, C])
        sl_sign = sf("sl_sign", [P, C])
        xf = sf("xf", [P, TILES, C])
        onehot = sf("onehot", [P, TILES, ROUTES])
        table = sf("table", [ROUTES, TABW])
        rank = sf("rank", [P, ROUTES])
        kgrid = sf("kgrid", [P, GRID + 1])
        ranki = sf("ranki", [P, ROUTES], mybir.dt.int32)
        kgridi = sf("kgridi", [P, GRID + 1], mybir.dt.int32)
        z = sf("z", [P, FG, C])
        fmom = sf("fmom", [P, FG, 2])
        fvar = sf("fvar", [P, FG])
        frs = sf("frs", [P, FG])
        fmom2 = sf("fmom2", [P, FG, 2])
        fvar2 = sf("fvar2", [P, FG])
        frs2 = sf("frs2", [P, FG])
        sgn = sf("sgn", [P, FG, C])
        tsc = sf("tsc", [P, FG, ROUTES])
        csc = sf("csc", [P, FG, CLUSTER])
        comp = sf("comp", [P, FG, ROUTES])
        best = sf("best", [P, FG])
        smin = sf("smin", [P, FG, ROUTES])
        smax = sf("smax", [P, FG, ROUTES])
        far = sf("far", [P, FG, ROUTES])
        run_min = sf("run_min", [P, FG, ROUTES])
        run_nmax = sf("run_nmax", [P, FG, ROUTES])
        ext = sf("ext", [ROUTES, 2])
        oh_fix = sf("oh_fix", [P, FG, ROUTES])
        ohT = sf("ohT", [ROUTES, FG, P])
        selr = sf("selr", [P, FG, TABW])
        pick = sf("pick", [P, FG, C])
        xs = sf("xs", [P, FG, SLICE])
        u16 = sf("u16", [P, FG, SLICE])
        ge = sf("ge", [P, FG * SLICE, GRID + 1])
        floor1 = sf("floor1", [P, FG * SLICE])
        gmask = sf("gmask", [P, FG, SLICE * GRID])
        bsel = sf("bsel", [P, FG * SLICE])
        ssel = sf("ssel", [P, FG * SLICE])
        tmpg = sf("tmpg", [P, FG, SLICE * GRID])
        delta = sf("delta", [P, FG, SLICE])
        stack_f.close()

        stack_c = ExitStack()

        def sc(name, shape, dt=F32):
            return stack_c.enter_context(nc.sbuf_tensor(name, shape, dt))
        w_ab = sc("w_ab", [P, CT, 2 * DH])
        b_ab = sc("b_ab", [1, 2 * DH])
        b_a = sc("b_a", [DH, 1])
        beta_k = sc("beta_k", [P, TILES, DH])
        beta_q = sc("beta_q", [P, TILES, DH])
        beta = sc("beta", [P, TILES, DH])
        gam_q = sc("gam_q", [P, TILES, DH])
        gam_k = sc("gam_k", [P, TILES, DH])
        ln_w = sc("ln_w", [P, 1])
        ln_b = sc("ln_b", [P, 1])
        conv_w = sc("conv_w", [P, 3, DH, TAPS])
        conv_b = sc("conv_b", [P, 3, DH])
        id_many = sc("id_many", [P, PROBS, P])
        id2c = sc("id2c", [P, BLK])
        cxn = sc("cxn", [P, TPS, C])
        cxT = sc("cxT", [P, CT, SEQ])
        alphaT = sc("alphaT", [DH, SEQ])
        alpha_z = sc("alpha_z", [DH, SEQ])
        alpha_r = sc("alpha_r", [DH, SEQ])
        gam_row = sc("gam_row", [DH, SEQ])
        gprev_row = sc("gprev_row", [DH, SEQ])
        w4 = sc("w4", [P, 4, CT, HG * DK])
        w_o = sc("w_o", [P, HG, C])
        xTb = sc("xTb", [P, CT, SEQ])
        abc = sc("abc", [P, HG, SEQ])
        acc = sc("acc", [P, 3, HG, SEQ])
        vT = sc("vT", [P, HG, SEQ])
        dec = sc("dec", [P, HG, SEQ])
        LT = sc("LT", [P, TPS, HG, P])
        BDL = sc("BDL", [P, TPS, HG, P])
        BDN = sc("BDN", [P, TPS, HG, P])
        Cc = sc("Cc", [P, TPS, HG, BLK])
        Rc = sc("Rc", [P, TPS, HG, BLK])
        two = range(2)
        kq = [sc(f"kq{i}", [P, HG, TPS, 2, P]) for i in two]
        gT = [sc(f"gT{i}", [P, HG, SEQ]) for i in two]
        vn = [sc(f"vn{i}", [P, TPS, HG, DK]) for i in two]
        kn = [sc(f"kn{i}", [P, HG, DK]) for i in two]
        MT = [sc(f"MT{i}", [P, TPS, HG, P]) for i in two]
        BDT = [sc(f"BDT{i}", [P, TPS, HG, P]) for i in two]
        GT = [sc(f"GT{i}", [P, TPS, HG, P]) for i in two]
        wgt = [sc(f"wgt{i}", [P, HG]) for i in two]
        y = sc("y", [P, HG, DK])
        r1 = sc("r1", [P, HG, DK])
        U = sc("U", [P, TPS, HG, DK])
        Uw = sc("Uw", [P, HG, DK])
        S = sc("S", [P, HG, DK])
        oi = sc("oi", [P, HG, DK])
        o = sc("o", [P, TPS, HG, DK])
        ostat = sc("ostat", [P, PROBS, 6])
        omom = sc("omom", [P, PROBS, 2])
        ovar = sc("ovar", [P, PROBS])
        ors = sc("ors", [P, PROBS])
        oT = sc("oT", [P, TPS, HG, P])
        oG = sc("oG", [P, TPS, HG, P])
        stack_c.close()

        A = {k: sem("A_" + k) for k in (
            "xn", "xTp", "xT", "qkv", "rope", "v", "rotp", "qkT", "score", "shift", "exp", "pT",
            "probT", "av", "att", "attTp", "attT", "yout", "res", "var", "rstd")}
        R = {k: sem("R_" + k) for k in (
            "loaded", "var", "rs", "z", "added", "xf", "sign", "minT", "table", "pass1",
            "fix", "ohTp", "ohT", "selp", "sel", "pick0", "xs", "delta", "scat", "res", "cons")}
        Z = {k: sem("Z_" + k) for k in (
            "w", "wab", "xn", "xTp", "xT", "stored", "abp", "ab", "rows", "gamp", "gam", "cons",
            "var", "rstd",
            "wg", "wo", "xin", "abc", "proj", "tap", "conv", "silu", "gate", "vTp", "vn", "kq", "LM", "wgt", "Uw", "read",
            "bdl", "t1", "X", "Rr", "Y", "Cev", "Tn", "bdn", "Gp", "Gev", "ap", "yv", "Up", "Uev",
            "Sp", "Sev", "KS", "QS", "r1", "oi", "Op", "oev", "ovar", "ors", "on", "oTp", "oT",
            "oG", "yout", "res", "dec")}

        block = ctx.enter_context(nc.Block())

        @block.sync
        def _(sp):
            for g in range(4):
                n = TILES // 4
                sp.dma_start(stream[:, g * n:(g + 1) * n, :],
                             io["x"][g * n * P:(g + 1) * n * P, :].rearrange("(n p) c -> p n c", p=P)
                             ).then_inc(loaded_x, 16)
            sp.dma_start(w_qkv[:], io["w_qkv"].rearrange("(k p) n -> p k n", p=P)).then_inc(loaded_a, 16)
            sp.dma_start(w_out[:], io["w_out"].rearrange("(k p) n -> p k n", p=P)).then_inc(loaded_a, 16)
            sp.dma_start(b_qkv[:], io["b_qkv"].rearrange("(a n) -> a n", a=1)).then_inc(loaded_a, 16)
            sp.dma_start(b_out[:], io["b_out"].rearrange("(a n) -> a n", a=1)).then_inc(loaded_a, 16)
            sp.dma_start(cosT[:], io["cos"].rearrange("(j p) n -> p j n", p=P)).then_inc(loaded_a, 16)
            sp.dma_start(sinT[:], io["sin"].rearrange("(j p) n -> p j n", p=P)).then_inc(loaded_a, 16)

            def routed_loads():
                row = io["slopes"].rearrange("(a r) j k -> a (r j) k", a=1)
                sp.dma_start(gam[:], io["gamma"].rearrange("(a n) -> a n", a=1).broadcast_to([P, C])).then_inc(R["loaded"], 16)
                sp.dma_start(bet[:], io["beta"].rearrange("(a n) -> a n", a=1).broadcast_to([P, C])).then_inc(R["loaded"], 16)
                sp.dma_start(sl_all[:], row.broadcast_to([P, C, GRID])).then_inc(R["loaded"], 16)
                w = SLICE * GRID
                sp.dma_start(table[:, 0:w], io["bases"].rearrange("r j k -> r (j k)")).then_inc(R["loaded"], 16)
                sp.dma_start(table[:, w:2 * w], io["slopes"].rearrange("r j k -> r (j k)")).then_inc(R["loaded"], 16)
                sp.dma_start(table[:, 2 * w:2 * w + 1], io["oscale"].rearrange("(r a) -> r a", a=1)).then_inc(R["loaded"], 16)

            sp.wait_ge(stage_done, 1)
            if stop > 1:
                routed_loads()
                sp.wait_ge(stage_done, 2)
            if stop > 2:
                sp.dma_start(w_ab[:, :, 0:DH], io["Wa"].rearrange("(k p) n -> p k n", p=P)).then_inc(Z["wab"], 16)
                sp.dma_start(w_ab[:, :, DH:], io["Wb"].rearrange("(k p) n -> p k n", p=P)).then_inc(Z["wab"], 16)
                sp.dma_start(b_ab[:, 0:DH], io["ba"].rearrange("(a n) -> a n", a=1)).then_inc(Z["wab"], 16)
                sp.dma_start(b_ab[:, DH:], io["bb"].rearrange("(a n) -> a n", a=1)).then_inc(Z["wab"], 16)
                sp.dma_start(b_a[:], io["ba"].rearrange("(n a) -> n a", a=1)).then_inc(Z["wab"], 16)
                sp.dma_start(ln_w[:], io["ln_w"].rearrange("(n a) -> n a", a=1)).then_inc(Z["wab"], 16)
                sp.dma_start(ln_b[:], io["ln_b"].rearrange("(n a) -> n a", a=1)).then_inc(Z["wab"], 16)
                for n, k in enumerate("kqv"):
                    sp.dma_start(conv_w[:, n], io[f"cw_{k}"]).then_inc(Z["wab"], 16)
                    sp.dma_start(conv_b[:, n], io[f"cb_{k}"]).then_inc(Z["wab"], 16)
                with sp.Fori(0, SEQS) as b:
                    sp.wait_ge(Z["xT"], past(2 * b + 2))
                    sp.dma_start(xT_dram[b], cxT[:].rearrange("p k t -> p (k t)")).then_inc(Z["stored"], 16)
                    sp.wait_ge(Z["rows"], past(b + 1))
                    sp.dma_start(decay_dram[b], alpha_z[:]).then_inc(Z["stored"], 16)
                sp.wait_ge(Z["stored"], past(32 * SEQS))
                def token_loads(n):
                    sp.wait_ge(Z["proj"], past(8 * n))
                    sp.dma_start(xTb[:].rearrange("p k t -> p (k t)"), xT_dram[n % SEQS]).then_inc(Z["xin"], 16)
                    sp.wait_ge(Z["dec"], past(n))
                    row = decay_dram.rearrange("b (g h) t -> b g (h t)", g=GROUPS)[bass.ds(n % SEQS, 1), bass.ds(n // SEQS, 1), :]
                    sp.dma_start(abc[:].rearrange("p h t -> p (h t)"),
                                 row.rearrange("a b n -> (a b) n").broadcast_to([P, HG * SEQ])).then_inc(Z["abc"], 16)

                with sp.Fori(0, GROUPS) as g:
                    sp.wait_ge(Z["proj"], past(8 * SEQS * g))
                    for k, w in enumerate(("Wk", "Wq", "Wv", "Wg")):
                        sp.dma_start(w4[:, k], io[w].rearrange("(k p) n -> p k n", p=P)[:, :, bass.ds(g * HG * DK, HG * DK)]).then_inc(Z["wg"], 16)
                    token_loads(g * SEQS)
                    sp.wait_ge(Z["yout"], past(SEQS * g))
                    sp.dma_start(w_o[:], io["Wo"].rearrange("(h p) n -> p h n", p=P)[:, bass.ds(g * HG, HG), :]).then_inc(Z["wo"], 16)
                    with sp.Fori(1, SEQS) as b:
                        token_loads(g * SEQS + b)
                sp.wait_ge(stage_done, 3)
            if stop > 3:
                routed_loads()
                sp.wait_ge(stage_done, 4)
            for g in range(4):
                n = TILES // 4
                sp.dma_start(io["out"][g * n * P:(g + 1) * n * P, :].rearrange("(n p) c -> p n c", p=P),
                             stream[:, g * n:(g + 1) * n, :]).then_inc(stored, 16)
            sp.wait_ge(stored, 64)

        @block.gpsimd
        def _(pool):
            for signals in (A, R, Z):
                for signal in signals.values():
                    pool.sem_inc(signal, 1)
            ch = Chain(pool, p_step)
            ch.link(pool.memset(ident[:], 0.0))
            ch.link(pool.affine_select(out=ident[:], in_=ident[:], compare_op=ALU.not_equal, fill=1.0,
                                       base=0, pattern=[[-1, P]], channel_multiplier=1))
            pool.tensor_copy(identb[:], ident[:]).then_inc(consts, 1)
            pool.memset(ones_row[:], 1.0).then_inc(consts, 1)
            pool.memset(half_neg[:], -0.5).then_inc(consts, 1)
            ch.link(pool.memset(maskb[:], 0.0))
            ch.link(pool.affine_select(out=maskb[:, P:], in_=maskb[:, P:], compare_op=ALU.is_ge, fill=MASKED,
                                       base=0, pattern=[[-1, P]], channel_multiplier=1))
            for i in range(4):
                pool.tensor_copy(maskd[:, i], maskb[:, P:]).then_inc(consts, 1)
            for i in range(2):
                pool.tensor_copy(masko[:, i], maskb[:]).then_inc(consts, 1)
            pool.memset(rot[:], 0.0).then_inc(consts, 1)
            pool.memset(vx[:], 1.0).then_inc(consts, 1)
            n0 = ch.n
            pool.wait_ge(A["var"], past(1))
            pool.wait_ge(consts, 3)
            pool.tensor_tensor(rstd[:], rstd[:], half_neg[:], ALU.pow).then_inc(A["rstd"], 1)

            def routed(turn):
                pool.wait_ge(stage_done, 1 + 2 * turn)
                c1 = Chain(pool, p_step, pstep_base(turn))
                c1.link(pool.iota(ranki[:].rearrange("p (c i) -> p c i", c=CLUSTER), [[-P, CLUSTER], [-1, ROUTES // CLUSTER]],
                                  base=0, channel_multiplier=0))
                c1.link(pool.iota(kgridi[:], [[1, GRID + 1]], base=0, channel_multiplier=0))
                pool.tensor_copy(rank[:], ranki[:]).then_inc(R["cons"], 1)
                pool.tensor_copy(kgrid[:], kgridi[:]).then_inc(R["cons"], 1)
                pool.memset(run_min[:], 2 * FAR).then_inc(R["cons"], 1)
                pool.memset(run_nmax[:], 2 * FAR).then_inc(R["cons"], 1)
                with pool.Fori(0, FSTEPS) as s:
                    n = s + FSTEPS * turn
                    pool.wait_ge(R["var"], past(2 * n + 1))
                    pool.tensor_tensor(frs[:], fvar[:], half_neg[:, 0:FG], ALU.pow).then_inc(R["rs"], 1)
                    pool.wait_ge(R["z"], past(n + 1))
                    pool.tensor_tensor(stream[:, bass.ds(s * FG, FG), :], stream[:, bass.ds(s * FG, FG), :], z[:], ALU.add).then_inc(R["added"], 1)
                    pool.wait_ge(R["var"], past(2 * n + 2))
                    pool.tensor_tensor(frs2[:], fvar2[:], half_neg[:, 0:FG], ALU.pow).then_inc(R["rs"], 1)
                with pool.Fori(0, FSTEPS) as s:
                    n = s + FSTEPS * turn
                    pool.wait_ge(R["pass1"], past(turn + 1))
                    pool.wait_ge(R["ohTp"], past(n))
                    pool.wait_ge(R["res"], past(n))
                    pool.tensor_copy(oh_fix[:], onehot[:, bass.ds(s * FG, FG), :]).then_inc(R["fix"], 1)
                    pool.wait_ge(R["fix"], past(n + 1))
                    pool.tensor_tensor(pick[:].rearrange("p f (r j) -> p (f r) j", j=SLICE),
                                       xf[:, bass.ds(s * FG, FG), :].rearrange("p f (r j) -> p (f r) j", j=SLICE),
                                       oh_fix[:].rearrange("p f r -> p (f r)").unsqueeze(2).broadcast_to([P, FG * ROUTES, SLICE]),
                                       ALU.mult).then_inc(R["pick0"], 1)

            def pstep_base(turn):
                return n0 + 2 * turn

            if stop > 1:
                routed(0)
            if stop > 2:
                pool.wait_ge(stage_done, 2)
                base = n0 + 4
                cc = Chain(pool, p_step, base)
                for i in range(PROBS):
                    pool.tensor_copy(id_many[:, i], ident[:]).then_inc(Z["cons"], 1)
                for q in range(P // BLK):
                    qs = slice(q * BLK, (q + 1) * BLK)
                    pool.wait_ge(Z["cons"], past(PROBS + q))
                    pool.tensor_scalar(id2c[qs, :], ident[qs, q * BLK:(q + 1) * BLK], 2.0, 0.0, ALU.mult, ALU.add).then_inc(Z["cons"], 1)
                pool.wait_ge(Z["cons"], past(PROBS + P // BLK))
                for m in (BDL, BDT[0], BDT[1], BDN):
                    pool.memset(m[:], 0.0).then_inc(Z["cons"], 1)
                pool.tensor_copy(LT[:].rearrange("p c h t -> p (c h) t")[:, :, 0:1], id_many[:, :, 0:1]).then_inc(Z["cons"], 1)
                pool.wait_ge(Z["var"], past(1))
                pool.tensor_tensor(rstd[:], rstd[:], half_neg[:], ALU.pow).then_inc(Z["rstd"], 1)
                def slot(f, n, fp):
                    if n is None:
                        return
                    pool.wait_ge(Z["ovar"], past(n + 1))
                    pool.tensor_tensor(ors[:], ovar[:], half_neg[:, 0:PROBS], ALU.pow).then_inc(Z["ors"], 1)
                    for c in range(TPS):
                        pool.wait_ge(Z["gate"], past(2 * n + 2))
                        pool.wait_ge(Z["yout"], past(n))
                        pool.wait_ge(Z["oT"], past(2 * n + c + 1))
                        pool.tensor_tensor(oG[:, c], oT[:, c], gT[1 - fp][:, :, c * P:(c + 1) * P], ALU.mult).then_inc(Z["oG"], 1)

                pipeline(pool, slot)
            if stop > 3:
                routed(1)

        @block.scalar
        def _(act):
            act.wait_ge(consts, 11)
            with act.Fori(0, SEQS) as b:
                act.wait_ge(A["xTp"], past(b + 1))
                act.copy(xT[:].rearrange("p k t -> p (k t)"), bank[0][:]).then_inc(A["xT"], 1)
                for j in range(TPS):
                    act.wait_ge(A["qkv"], past(2 * b + 2))
                    act.copy(vx[:, j, :, 0:HD], bank[3][:, j * C:(j + 1) * C].rearrange("p (h d) -> p h d", d=HD)).then_inc(A["v"], 1)
                for m in range(4):
                    act.wait_ge(A["rotp"], past(4 * b + m + 1))
                    dst = (qT, kT)[m % 2]
                    act.copy(dst[:, :, (m // 2) * P:(m // 2 + 1) * P], bank[4 + m][:].rearrange("p (g t) -> p g t", g=4)).then_inc(A["qkT"], 1)
                for u in range(UNITS + 1):
                    if u < UNITS:
                        act.wait_ge(A["shift"], past(UNITS * b + u + 1))
                        act.activation(prob[:, u % 2], prob[:, u % 2], ACT.Exp, scale=float(HD) ** -0.5).then_inc(A["exp"], 1)
                    if u >= 1:
                        act.wait_ge(A["pT"], past(UNITS * b + u))
                        if u >= 3:
                            act.wait_ge(A["av"], past(UNITS * b + u - 2))
                        act.copy(probT[:, (u - 1) % 2], bank[6 + (u - 1) % 2][:]).then_inc(A["probT"], 1)
                act.wait_ge(A["attTp"], past(b + 1))
                act.copy(attT[:].rearrange("p k t -> p (k t)"), bank[0][:]).then_inc(A["attT"], 1)

            def routed(turn):
                with act.Fori(0, FSTEPS) as s:
                    n = s + FSTEPS * turn
                    act.wait_ge(R["xf"], past(n + 1))
                    act.activation(sgn[:], xf[:, bass.ds(s * FG, FG), :], ACT.Sign).then_inc(R["sign"], 1)
                with act.Fori(0, FSTEPS) as s:
                    n = s + FSTEPS * turn
                    act.wait_ge(R["ohTp"], past(n + 1))
                    act.copy(ohT[:].rearrange("r f t -> r (f t)"), bank[0][0:ROUTES, :]).then_inc(R["ohT"], 1)
                    act.wait_ge(R["selp"], past(n + 1))
                    act.wait_ge(R["delta"], past(n))
                    for h in range(2):
                        act.copy(selr[:, 2 * h:2 * h + 2, :], bank[1 + h][:].rearrange("p (i w) -> p i w", i=2)[:, :, 0:TABW]).then_inc(R["sel"], 1)

            if stop > 1:
                routed(0)
            if stop > 2:
                act.wait_ge(Z["wab"], past(16 * 13))
                with act.Fori(0, SEQS) as b:
                    act.wait_ge(Z["xTp"], past(b + 1))
                    act.wait_ge(Z["stored"], past(32 * b))
                    for k in range(CT):
                        act.copy(cxT[:, k], bank[0][:, k * SEQ:(k + 1) * SEQ]).then_inc(Z["xT"], 1)
                    act.wait_ge(Z["abp"], past(2 * b + 1))
                    act.activation(beta[:, bass.ds(2 * b, 2), :], bank[1][:, 0:2 * 2 * DH].rearrange("p (j n) -> p j n", j=2)[:, :, DH:], ACT.Sigmoid).then_inc(Z["ab"], 1)
                    act.wait_ge(Z["abp"], past(2 * b + 2))
                    act.wait_ge(Z["rows"], past(b))
                    act.activation(alphaT[:], bank[2][0:DH, 0:SEQ], ACT.Sigmoid, bias=b_a[:]).then_inc(Z["ab"], 1)
                    act.wait_ge(Z["gamp"], past(b + 1))
                    act.mul(gam_q[:, bass.ds(2 * b, 2), :], bank[3][:, 0:2 * DH].rearrange("p (j n) -> p j n", j=2), KAPPA).then_inc(Z["gam"], 1)
                    act.mul(gam_k[:, bass.ds(2 * b, 2), :], bank[3][:, 2 * DH:4 * DH].rearrange("p (j n) -> p j n", j=2), -KAPPA2).then_inc(Z["gam"], 1)
                def slot(f, n, fp):
                    bp = 1 - fp

                    def tap(u):
                        kind, pair = u // 2, u % 2
                        act.wait_ge(Z["silu"], past(3 * f))
                        act.wait_ge(Z["proj"], past(8 * f + u + 1))
                        for i in (2 * pair, 2 * pair + 1):
                            h = (f // SEQS) * HG + i
                            act.activation(acc[:, kind, i], bank[u % 3][:, (i % 2) * SEQ:(i % 2 + 1) * SEQ], ACT.Identity,
                                           scale=conv_w[:, kind, bass.ds(h, 1), TAPS - 1:TAPS].rearrange("p a b -> p (a b)"),
                                           bias=conv_b[:, kind, bass.ds(h, 1)]).then_inc(Z["tap"], 1)

                    def silu(kind):
                        act.wait_ge(Z["conv"], past(12 * f + 4 * kind + 4))
                        if kind < 2:
                            act.wait_ge(Z["QS"], past(f - 1) if not isinstance(f, int) or f > 1 else past(0))
                            act.activation(kq[fp][:, :, :, kind, :], acc[:, kind].rearrange("p h (c t) -> p h c t", c=TPS), ACT.Silu).then_inc(Z["silu"], 1)
                        else:
                            act.wait_ge(Z["vTp"], past(3 * f))
                            act.activation(vT[:], acc[:, kind], ACT.Silu).then_inc(Z["silu"], 1)

                    def gate(i):
                        act.wait_ge(Z["oG"], past(2 * f - 2) if not isinstance(f, int) or f > 1 else past(0))
                        act.wait_ge(Z["proj"], past(8 * f + 7 + i))
                        act.activation(gT[fp][:, 2 * i:2 * i + 2, :].rearrange("p h t -> p (h t)"), bank[(6 + i) % 3][:], ACT.Sigmoid).then_inc(Z["gate"], 1)

                    def tokens_major(m):
                        act.wait_ge(Z["vTp"], past(3 * f + m + 1))
                        dst = vn[fp][:, m] if m < TPS else kn[fp][:]
                        act.copy(dst.rearrange("p h v -> p (h v)"), bank[(12 + m) % 3][:]).then_inc(Z["vn"], 1)

                    def diagonal():
                        act.wait_ge(Z["X"], past(8 * f))
                        act.wait_ge(Z["LM"], past(2 * f + 2))
                        for q in range(P // BLK):
                            qs = slice(q * BLK, (q + 1) * BLK)
                            act.copy(BDL[qs, :, :, qs].rearrange("p c h t -> p (c h) t"),
                                     LT[qs, :, :, qs].rearrange("p c h t -> p (c h) t")).then_inc(Z["bdl"], 1)

                    def blocks(lev, c):
                        act.wait_ge(Z["Y"], past(8 * f + 2 * lev + c + 1))
                        act.copy(Cc[:, c].rearrange("p h t -> p (h t)"), bank[3 + c][:, 128:256]).then_inc(Z["Cev"], 1)

                    def updates(c):
                        act.wait_ge(Z["Up"], past(2 * n + c + 1))
                        act.copy(U[:, c].rearrange("p h v -> p (h v)"), bank[6][:]).then_inc(Z["Uev"], 1)

                    def first_out():
                        act.wait_ge(Z["Op"], past(2 * n + 1))
                        act.copy(o[:, 0].rearrange("p h v -> p (h v)"), bank[7][:]).then_inc(Z["oev"], 1)

                    def state():
                        act.wait_ge(Z["Sp"], past(n + 1))
                        act.copy(S[:].rearrange("p h v -> p (h v)"), bank[5][:]).then_inc(Z["Sev"], 1)

                    def from_state():
                        act.wait_ge(Z["QS"], past(n + 1))
                        for i in range(HG):
                            act.activation(oi[:, i], bank[5][:, i * DK:(i + 1) * DK], ACT.Copy,
                                           scale=gam_q[:, bass.ds(2 * (n % SEQS) + 1, 1), bass.ds((n // SEQS) * HG + i, 1)].rearrange("p a b -> p (a b)")).then_inc(Z["oi"], 1)

                    def affine(c):
                        act.wait_ge(Z["oTp"], past(2 * n + c + 1))
                        act.activation(oT[:, c].rearrange("p h t -> p (h t)"), bank[5 + c][:], ACT.Identity,
                                       scale=ln_w[:], bias=ln_b[:]).then_inc(Z["oT"], 1)

                    front, back = f is not None, n is not None
                    if front:
                        tap(0), tap(1), tap(2), tap(3)
                    if back:
                        updates(0)
                    if front:
                        tap(4)
                    if back:
                        state()
                        first_out()
                    if front:
                        tap(5)
                    if back:
                        from_state()
                    if front:
                        silu(0), silu(1), silu(2)
                        gate(0), gate(1)
                        tokens_major(0), tokens_major(1), tokens_major(2)
                    if back:
                        updates(1)
                    if front:
                        diagonal()
                        blocks(0, 0), blocks(0, 1), blocks(1, 0), blocks(1, 1)
                    if back:
                        affine(0), affine(1)
                    if front:
                        blocks(2, 0), blocks(2, 1), blocks(3, 0), blocks(3, 1)

                pipeline(act, slot)
            if stop > 3:
                routed(1)

        @block.vector
        def _(dve):
            ch = Chain(dve, v_step)
            base = 0

            def all_moments(eps_to, ready):
                with dve.Fori(0, TILES // 8) as t:
                    c = Chain(dve, v_step, base + 3 * t)
                    for i in range(8):
                        ins = dve.bn_stats(stats[:, i, :], stream[:, bass.ds(t * 8 + i, 1), :].rearrange("p a c -> p (a c)"))
                    c.link(ins)
                    dve.memset(pad[:], 0.0)
                    for i in range(8):
                        ins = dve.bn_aggr(mom8[:, i, :], stats[:, i, :])
                    c.link(ins)
                    c.link(dve.tensor_copy(moments[:, bass.ds(t * 8, 8), :], mom8[:]))
                dve.tensor_scalar(rstd[:], moments[:, :, 1], EPS, None, ALU.add).then_inc(ready, 1)
                return base + 3 * (TILES // 8)

            dve.wait_ge(loaded_x, 64)
            base = all_moments(rstd, A["var"])
            dve.wait_ge(A["rstd"], past(1))
            dve.wait_ge(consts, 11)
            dve.wait_ge(loaded_a, 96)
            PER_A = 7
            base_a = base
            with dve.Fori(0, SEQS) as b:
                c = Chain(dve, v_step, base_a + PER_A * b)
                for j in range(TPS):
                    dve.wait_ge(A["xTp"], past(b))
                    dve.tensor_scalar(xn[:, j], stream[:, bass.ds(2 * b + j, 1), :].rearrange("p a c -> p (a c)"),
                                      moments[:, bass.ds(2 * b + j, 1), 0:1].rearrange("p a c -> p (a c)"),
                                      rstd[:, bass.ds(2 * b + j, 1)], ALU.subtract, ALU.mult).then_inc(A["xn"], 1)
                for j in range(TPS):
                    dve.wait_ge(A["qkv"], past(2 * b + j + 1))
                    src = bank[1 + j][:].rearrange("p (h i two) -> p h i two", i=HALF, two=2)
                    cs = cosT[:, j:j + 1, :].broadcast_to([P, 2 * HEADS, HALF])
                    sn = sinT[:, j:j + 1, :].broadcast_to([P, 2 * HEADS, HALF])
                    t = [rope_t[:, m, j].rearrange("p (h i) -> p h i", i=HALF) for m in range(4)]
                    dve.tensor_tensor(t[0], src[:, :, :, 0], cs, ALU.mult)
                    dve.tensor_tensor(t[1], src[:, :, :, 1], sn, ALU.mult)
                    dve.tensor_tensor(t[2], src[:, :, :, 0], sn, ALU.mult)
                    c.link(dve.tensor_tensor(t[3], src[:, :, :, 1], cs, ALU.mult))
                    dve.wait_ge(A["rotp"], past(4 * b))
                    dve.tensor_tensor(rot[:, j, :, 0:HALF], t[0], t[1], ALU.subtract).then_inc(A["rope"], 1)
                    dve.tensor_tensor(rot[:, j, :, HALF:HD], t[2], t[3], ALU.add).then_inc(A["rope"], 1)
                for u in range(UNITS):
                    heads = 4 if u % 3 == 0 else 2
                    sc3 = bank[4 + u % 2][:].rearrange("p (h s) -> p h s", h=heads)
                    dve.wait_ge(A["score"], past(UNITS * b + u + 1))
                    dve.tensor_reduce(row_max[:, u % 2, 0:heads], sc3, AX.X, ALU.max).then_inc(A["res"], 1)
                    dve.wait_ge(A["res"], past(b * (UNITS + 1) + u + 1))
                    if u >= 2:
                        dve.wait_ge(A["pT"], past(UNITS * b + u - 1))
                    dve.tensor_tensor(prob[:, u % 2].rearrange("p (h s) -> p h s", h=heads), sc3,
                                      row_max[:, u % 2, 0:heads].unsqueeze(2).broadcast_to([P, heads, 512 // heads]),
                                      ALU.subtract).then_inc(A["shift"], 1)
                dve.wait_ge(A["av"], past(UNITS * b + UNITS))
                for j in range(TPS):
                    av = bank[(3, 1)[j]][:, 0:HEADS * (HD + 1)].rearrange("p (h d) -> p h d", d=HD + 1)
                    c.link(dve.reciprocal(rsum[:, j, :], av[:, :, HD]))
                    dve.tensor_tensor(att[:, j].rearrange("p (h d) -> p h d", d=HD), av[:, :, 0:HD],
                                      rsum[:, j, :].unsqueeze(2).broadcast_to([P, HEADS, HD]), ALU.mult).then_inc(A["att"], 1)
                dve.wait_ge(A["yout"], past(b + 1))
                x2 = stream[:, bass.ds(2 * b, 2), :].rearrange("p j c -> p (j c)")
                dve.tensor_tensor(x2, x2, bank[2][:], ALU.add).then_inc(A["res"], 1)
                for _ in range(PER_A - c.n):
                    c.link(dve.engine_nop() if False else dve.memset(stats[:, 0, :], 0.0))
            base = base_a + PER_A * SEQS
            dve.wait_ge(A["res"], past(SEQS * (UNITS + 1)))
            dve.sem_inc(stage_done, 1) if False else dve.memset(stats[:, 1, :], 0.0).then_inc(stage_done, 1)

            def routed(turn, base):
                dve.wait_ge(R["loaded"], past(96 * (turn + 1)))
                dve.wait_ge(R["cons"], past(4 * (turn + 1)))
                c = Chain(dve, v_step, base)
                c.link(dve.tensor_reduce(sl_sum[:], sl_all[:], AX.X, ALU.add))
                c.link(dve.tensor_scalar(sl_sign[:], sl_sum[:], 0.0, None, ALU.is_lt))
                c.link(dve.scalar_tensor_tensor(out=sl_sign[:], in0=sl_sum[:], scalar=0.0, in1=sl_sign[:],
                                                op0=ALU.is_gt, op1=ALU.subtract))
                base = base + c.n
                PER = 26
                with dve.Fori(0, FSTEPS) as s:
                    n = s + FSTEPS * turn
                    c = Chain(dve, v_step, base + PER * s)
                    xs4 = stream[:, bass.ds(s * FG, FG), :]
                    for i in range(FG):
                        ins = dve.bn_stats(stats[:, i, :], stream[:, bass.ds(s * FG + i, 1), :].rearrange("p a c -> p (a c)"))
                    c.link(ins)
                    dve.memset(pad[:], 0.0)
                    for i in range(FG):
                        ins = dve.bn_aggr(fmom[:, i, :], stats[:, i, :])
                    c.link(ins)
                    dve.tensor_scalar(fvar[:], fmom[:, :, 1], EPS, None, ALU.add).then_inc(R["var"], 1)
                    dve.wait_ge(R["rs"], past(2 * n + 1))
                    dve.wait_ge(R["added"], past(n))
                    for i in range(FG):
                        ins = dve.tensor_scalar(z[:, i], stream[:, bass.ds(s * FG + i, 1), :].rearrange("p a c -> p (a c)"),
                                                fmom[:, i, 0:1], frs[:, i:i + 1], ALU.subtract, ALU.mult)
                    ins.then_inc(R["z"], 1)
                    dve.wait_ge(R["z"], past(n + 1))
                    for i in range(FG):
                        ins = dve.bn_stats(stats[:, i, :], z[:, i])
                    c.link(ins)
                    dve.memset(pad[:], 0.0)
                    for i in range(FG):
                        ins = dve.bn_aggr(fmom2[:, i, :], stats[:, i, :])
                    c.link(ins)
                    dve.tensor_scalar(fvar2[:], fmom2[:, :, 1], EPS, None, ALU.add).then_inc(R["var"], 1)
                    dve.wait_ge(R["rs"], past(2 * n + 2))
                    xf4 = xf[:, bass.ds(s * FG, FG), :]
                    for i in range(FG):
                        ins = dve.tensor_scalar(z[:, i], z[:, i], fmom2[:, i, 0:1], frs2[:, i:i + 1], ALU.subtract, ALU.mult) \
                            if False else dve.tensor_scalar(xf[:, bass.ds(s * FG + i, 1), :].rearrange("p a c -> p (a c)"), z[:, i],
                                                            fmom2[:, i, 0:1], frs2[:, i:i + 1], ALU.subtract, ALU.mult)
                    c.link(ins)
                    c.link(dve.tensor_tensor(xf4, xf4, gam[:].unsqueeze(1).broadcast_to([P, FG, C]), ALU.mult))
                    dve.tensor_tensor(xf4, xf4, bet[:].unsqueeze(1).broadcast_to([P, FG, C]), ALU.add).then_inc(R["xf"], 1)
                    dve.wait_ge(R["xf"], past(n + 1))
                    dve.memset(pad[:], 0.0)
                    x4 = xf4.rearrange("p f (r j) -> p (f r) j", j=SLICE)
                    dve.tensor_reduce(smin[:].rearrange("p f r -> p (f r)"), x4, AX.X, ALU.min)
                    c.link(dve.tensor_reduce(smax[:].rearrange("p f r -> p (f r)"), x4, AX.X, ALU.max))
                    dve.wait_ge(R["sign"], past(n + 1))
                    c.link(dve.tensor_tensor(sgn[:], sgn[:], sl_sign[:].unsqueeze(1).broadcast_to([P, FG, C]), ALU.mult))
                    c.link(dve.tensor_reduce(tsc[:].rearrange("p f r -> p (f r)"), sgn[:].rearrange("p f (r j) -> p (f r) j", j=SLICE), AX.X, ALU.add))
                    c.link(dve.tensor_reduce(csc[:].rearrange("p f k -> p (f k)"), tsc[:].rearrange("p f (k i) -> p (f k) i", k=CLUSTER), AX.X, ALU.add))
                    c.link(dve.scalar_tensor_tensor(out=comp[:], in0=tsc[:], scalar=float(ROUTES // CLUSTER),
                                                    in1=rank[:].unsqueeze(1).broadcast_to([P, FG, ROUTES]), op0=ALU.mult, op1=ALU.add))
                    cm = comp[:].rearrange("p f (k i) -> p (f k) i", k=CLUSTER)
                    c.link(dve.scalar_tensor_tensor(out=cm, in0=csc[:].rearrange("p f k -> p (f k)").unsqueeze(2).broadcast_to([P, FG * CLUSTER, ROUTES // CLUSTER]),
                                                    scalar=float(P * CLUSTER), in1=cm, op0=ALU.mult, op1=ALU.add))
                    c.link(dve.tensor_reduce(best[:], comp[:], AX.X, ALU.max))
                    oh4 = onehot[:, bass.ds(s * FG, FG), :]
                    c.link(dve.tensor_tensor(oh4, comp[:], best[:].unsqueeze(2).broadcast_to([P, FG, ROUTES]), ALU.is_equal))
                    c.link(dve.tensor_scalar(far[:], oh4, -FAR, FAR, ALU.mult, ALU.add))
                    c.link(dve.tensor_tensor(smin[:], smin[:], far[:], ALU.add))
                    c.link(dve.tensor_tensor(smax[:], far[:], smax[:], ALU.subtract))
                    c.link(dve.tensor_tensor(run_min[:], run_min[:], smin[:], ALU.min))
                    c.link(dve.tensor_tensor(run_nmax[:], run_nmax[:], smax[:], ALU.min))
                    for _ in range(PER - c.n):
                        c.link(dve.memset(pad[:], 0.0))
                base = base + PER * FSTEPS
                dve.memset(pad[:], 0.0).then_inc(R["pass1"], 1)
                dve.wait_ge(R["minT"], past(2 * (turn + 1)))
                c = Chain(dve, v_step, base)
                c.link(dve.tensor_reduce(ext[:, 0:1], bank[3][0:ROUTES, :], AX.X, ALU.min))
                c.link(dve.tensor_reduce(ext[:, 1:2], bank[4][0:ROUTES, :], AX.X, ALU.min))
                w = 2 * SLICE * GRID
                c.link(dve.tensor_copy(table[:, w + 1:w + 2], ext[:, 0:1]))
                c.link(dve.tensor_tensor(ext[:, 0:1], ext[:, 0:1], ext[:, 1:2], ALU.add))
                c.link(dve.tensor_scalar(ext[:, 0:1], ext[:, 0:1], -1.0, 1e-8, ALU.mult, ALU.add))
                dve.reciprocal(table[:, w + 2:w + 3], ext[:, 0:1]).then_inc(R["table"], 1)
                base = base + c.n
                PER2 = 16
                with dve.Fori(0, FSTEPS) as s:
                    n = s + FSTEPS * turn
                    c = Chain(dve, v_step, base + PER2 * s)
                    dve.wait_ge(R["pick0"], past(n + 1))
                    c.link(dve.tensor_reduce(xs[:], pick[:].rearrange("p f (r j) -> p f j r", j=SLICE), AX.X, ALU.add))
                    dve.wait_ge(R["sel"], past(2 * n + 2))
                    mn = selr[:, :, w + 1:w + 2].broadcast_to([P, FG, SLICE])
                    rd = selr[:, :, w + 2:w + 3].broadcast_to([P, FG, SLICE])
                    osc = selr[:, :, w:w + 1].broadcast_to([P, FG, SLICE])
                    c.link(dve.tensor_tensor(xs[:], xs[:], mn, ALU.subtract))
                    c.link(dve.tensor_tensor(xs[:], xs[:], rd, ALU.mult))
                    c.link(dve.tensor_scalar(xs[:], xs[:], 0.0, 1.0 - 1e-6, ALU.max, ALU.min))
                    c.link(dve.tensor_scalar(u16[:], xs[:], float(GRID), None, ALU.mult))
                    uf = u16[:].rearrange("p f j -> p (f j)")
                    c.link(dve.tensor_tensor(ge[:], uf.unsqueeze(2).broadcast_to([P, FG * SLICE, GRID + 1]),
                                             kgrid[:].unsqueeze(1).broadcast_to([P, FG * SLICE, GRID + 1]), ALU.is_ge))
                    c.link(dve.tensor_reduce(floor1[:], ge[:], AX.X, ALU.add))
                    gm = gmask[:].rearrange("p f (j k) -> p (f j) k", k=GRID)
                    c.link(dve.tensor_tensor(gm, ge[:, :, 0:GRID], ge[:, :, 1:GRID + 1], ALU.subtract))
                    hw = SLICE * GRID
                    tg = tmpg[:].rearrange("p f (j k) -> p (f j) k", k=GRID)
                    c.link(dve.tensor_tensor(tmpg[:], gmask[:], selr[:, :, 0:hw], ALU.mult))
                    c.link(dve.tensor_reduce(bsel[:], tg, AX.X, ALU.add))
                    c.link(dve.tensor_tensor(tmpg[:], gmask[:], selr[:, :, hw:2 * hw], ALU.mult))
                    c.link(dve.tensor_reduce(ssel[:], tg, AX.X, ALU.add))
                    c.link(dve.scalar_tensor_tensor(out=uf, in0=uf, scalar=1.0, in1=floor1[:], op0=ALU.add, op1=ALU.subtract)
                           if False else dve.tensor_scalar(floor1[:], floor1[:], -1.0, None, ALU.add))
                    c.link(dve.tensor_tensor(uf, uf, floor1[:], ALU.subtract))
                    c.link(dve.tensor_tensor(ssel[:], ssel[:], uf, ALU.mult))
                    c.link(dve.tensor_tensor(bsel[:], bsel[:], ssel[:], ALU.add))
                    dve.tensor_tensor(delta[:], bsel[:].rearrange("p (f j) -> p f j", j=SLICE), osc, ALU.mult).then_inc(R["delta"], 1)
                    dve.wait_ge(R["delta"], past(n + 1))
                    pk = pick[:].rearrange("p f (r j) -> p f r j", j=SLICE)
                    dve.tensor_tensor(pk, oh_fix[:].unsqueeze(3).broadcast_to([P, FG, ROUTES, SLICE]),
                                      delta[:].unsqueeze(2).broadcast_to([P, FG, ROUTES, SLICE]), ALU.mult).then_inc(R["scat"], 1)
                    dve.wait_ge(R["scat"], past(n + 1))
                    xs4 = stream[:, bass.ds(s * FG, FG), :]
                    dve.tensor_tensor(xs4, xs4, pick[:], ALU.add).then_inc(R["res"], 1)
                    assert c.n == PER2, c.n
                dve.wait_ge(R["res"], past(FSTEPS * (turn + 1)))
                dve.memset(pad[:], 0.0).then_inc(stage_done, 1)
                return base + PER2 * FSTEPS

            if stop > 1:
                base = routed(0, base)
            if stop > 2:
                dve.wait_ge(stage_done, 2)
                base = all_moments(rstd, Z["var"])
                dve.wait_ge(Z["rstd"], past(1))
                PER_P = 4
                base_p = base
                with dve.Fori(0, SEQS) as b:
                    c = Chain(dve, v_step, base_p + PER_P * b)
                    for j in range(TPS):
                        dve.wait_ge(Z["xTp"], past(b))
                        dve.tensor_scalar(cxn[:, j], stream[:, bass.ds(2 * b + j, 1), :].rearrange("p a c -> p (a c)"),
                                          moments[:, bass.ds(2 * b + j, 1), 0:1].rearrange("p a c -> p (a c)"),
                                          rstd[:, bass.ds(2 * b + j, 1)], ALU.subtract, ALU.mult).then_inc(Z["xn"], 1)
                    dve.wait_ge(Z["ab"], past(2 * b + 2))
                    dve.wait_ge(Z["stored"], past(32 * b))
                    dve.wait_ge(Z["gamp"], past(b))
                    c.link(dve.tensor_copy(alpha_z[:], alphaT[:]))
                    c.link(dve.memset(alpha_z[:, 0:SEQ:P], 0.0))
                    c.link(dve.tensor_tensor(alpha_r[:], alphaT[:], alpha_z[:], ALU.subtract))
                    c.link(dve.tensor_tensor_scan(gam_row[:], alpha_z[:], alpha_r[:], 0.0, ALU.mult, ALU.add))
                    dve.memset(gprev_row[:, 0:SEQ:P], 1.0)
                    dve.tensor_copy(gprev_row[:].rearrange("h (c t) -> h c t", c=TPS)[:, :, 1:P],
                                    gam_row[:].rearrange("h (c t) -> h c t", c=TPS)[:, :, 0:P - 1]).then_inc(Z["rows"], 1)
                base = base_p + PER_P * SEQS
                dve.wait_ge(Z["ab"], past(2 * SEQS))
                c = Chain(dve, v_step, base)
                dve.tensor_scalar(beta_k[:], beta[:], KAPPA2, None, ALU.mult)
                c.link(dve.tensor_scalar(beta_q[:], beta[:], KAPPA, None, ALU.mult))
                base = base + c.n
                dve.wait_ge(Z["cons"], past(PROBS + 4 + 5))
                PER_C = 33
                first = [None]

                def slot(f, n, fp):
                    bp = 1 - fp
                    if isinstance(f, int) and f == 0:
                        c = Chain(dve, v_step, base)
                    else:
                        c = Chain(dve, v_step, base + first[0] + PER_C * ((f if f is not None else n + 1) - 1))
                    quads = [slice(q * BLK, (q + 1) * BLK) for q in range(P // BLK)]
                    if f is not None:
                        fb, fg = f % SEQS, f // SEQS
                    if n is not None:
                        nb, ng = n % SEQS, n // SEQS

                    def conv(u):
                        kind, pair = u // 2, u % 2
                        dve.wait_ge(Z["tap"], past(12 * f + 2 * u + 2))
                        last = {}
                        for t in range(1, TAPS):
                            for i in (2 * pair, 2 * pair + 1):
                                pj = bank[u % 3][:, (i % 2) * SEQ:(i % 2 + 1) * SEQ]
                                wcol = conv_w[:, kind, bass.ds(fg * HG + i, 1), TAPS - 1 - t:TAPS - t].rearrange("p a b -> p (a b)")
                                if t > 1:
                                    c.wait(last[i])
                                ins = dve.scalar_tensor_tensor(out=acc[:, kind, i, t:], in0=pj[:, 0:SEQ - t], scalar=wcol,
                                                               in1=acc[:, kind, i, t:], op0=ALU.mult, op1=ALU.add)
                                if t < TAPS - 1:
                                    last[i] = c.mark(ins)
                                else:
                                    ins.then_inc(Z["conv"], 1)

                    def decays():
                        dve.wait_ge(Z["abc"], past(16 * f + 16))
                        dve.tensor_tensor_scan(dec[:].rearrange("p h t -> p (h t)"), abc[:].rearrange("p h t -> p (h t)"),
                                               id_many[:].rearrange("p n t -> p (n t)"), 0.0, ALU.mult, ALU.add).then_inc(Z["dec"], 1)
                        dve.wait_ge(Z["dec"], past(f + 1))
                        dve.tensor_tensor(wgt[fp][:], dec[:, :, P - 1], beta[:, bass.ds(2 * fb, 1), bass.ds(fg * HG, HG)].rearrange("p a b -> p (a b)"),
                                          ALU.mult).then_inc(Z["wgt"], 1)

                    def products(u):
                        tc, pair = u // 2, u % 2
                        dve.wait_ge(Z["Gp"], past(2 * f))
                        dve.wait_ge(Z["kq"], past(4 * f + u + 1))
                        for i in (2 * pair, 2 * pair + 1):
                            src = bank[(8 + u) % 3][:, (i % 2) * 2 * P:(i % 2 + 1) * 2 * P]
                            bk = beta_k[:, bass.ds(2 * fb + tc, 1), bass.ds(fg * HG + i, 1)].rearrange("p a b -> p (a b)")
                            bq = beta_q[:, bass.ds(2 * fb + tc, 1), bass.ds(fg * HG + i, 1)].rearrange("p a b -> p (a b)")
                            dve.scalar_tensor_tensor(out=LT[:, tc, i, 1:P], in0=src[:, 1:P], scalar=bk,
                                                     in1=dec[:, i, tc * P:tc * P + P - 1], op0=ALU.mult, op1=ALU.mult)
                            ins = dve.scalar_tensor_tensor(out=MT[fp][:, tc, i, :], in0=src[:, P:2 * P], scalar=bq,
                                                           in1=dec[:, i, tc * P:(tc + 1) * P], op0=ALU.mult, op1=ALU.mult)
                        ins.then_inc(Z["read"], 1)
                        if pair:
                            dve.wait_ge(Z["read"], past(4 * f + u + 1))
                            dve.tensor_tensor(LT[:, tc, :, 1:P], LT[:, tc, :, 1:P], id_many[:, 0:HG, 1:P], ALU.add).then_inc(Z["LM"], 1)

                    def start_inverse():
                        dve.wait_ge(Z["LM"], past(2 * f + 2))
                        for qs in quads:
                            ins = dve.tensor_tensor(BDT[fp][qs, :, :, qs].rearrange("p c h t -> p (c h) t"),
                                                    id2c[qs, :].unsqueeze(1).broadcast_to([BLK, PROBS, BLK]),
                                                    LT[qs, :, :, qs].rearrange("p c h t -> p (c h) t"), ALU.subtract)
                            c.mark(ins)
                        for m, qs in enumerate(quads):
                            c.wait(c.n - 3)
                            ins = dve.transpose(Cc[qs].rearrange("p c h t -> p (c h) t"), BDT[fp][qs, :, :, qs].rearrange("p c h t -> p (c h) t"))
                            if m < 3:
                                c.mark(ins)
                            else:
                                ins.then_inc(Z["t1"], 1)

                    def refine(lev, tc):
                        dve.wait_ge(Z["X"], past(8 * f + 2 * lev + tc + 1))
                        dve.tensor_tensor(Rc[:, tc], id2c[:].unsqueeze(1).broadcast_to([P, HG, BLK]),
                                          bank[3 + tc][:, 0:HG * BLK].rearrange("p (h t) -> p h t", t=BLK), ALU.subtract).then_inc(Z["Rr"], 1)

                    def turn(lev, tc):
                        dve.wait_ge(Z["Cev"], past(8 * f + 2 * lev + tc + 1))
                        for qs in quads:
                            ins = dve.transpose(BDT[fp][qs, tc, :, qs], Cc[qs, tc])
                        ins.then_inc(Z["Tn"], 1)

                    def plain_blocks():
                        for qs in quads:
                            ins = dve.tensor_copy(BDN[qs, :, :, qs].rearrange("p c h t -> p (c h) t"), Cc[qs].rearrange("p c h t -> p (c h) t"))
                        ins.then_inc(Z["bdn"], 1)

                    def off_blocks(tc):
                        dve.wait_ge(Z["Gp"], past(2 * f + tc + 1))
                        dve.tensor_tensor(GT[fp][:, tc], id_many[:, 0:HG], bank[3 + tc][:].rearrange("p (h t) -> p h t", h=HG), ALU.subtract).then_inc(Z["Gev"], 1)

                    def sweep(tc, k):
                        dve.wait_ge(Z["ap"], past(6 * n + 3 * tc + k + 1))
                        dve.tensor_tensor(y[:], vn[bp][:, 0] if tc == 0 else r1[:], bank[5][:].rearrange("p (h v) -> p h v", h=HG), ALU.add).then_inc(Z["yv"], 1)

                    def weighted():
                        dve.wait_ge(Z["wgt"], past(n + 1))
                        dve.wait_ge(Z["Uev"], past(2 * n + 1))
                        dve.tensor_tensor(Uw[:], U[:, 0], wgt[bp][:].unsqueeze(2).broadcast_to([P, HG, DK]), ALU.mult).then_inc(Z["Uw"], 1)

                    def second_rhs():
                        dve.wait_ge(Z["KS"], past(n + 1))
                        for i in range(HG):
                            gk = gam_k[:, bass.ds(2 * nb + 1, 1), bass.ds(ng * HG + i, 1)].rearrange("p a b -> p (a b)")
                            ins = dve.scalar_tensor_tensor(out=r1[:, i], in0=bank[6][:, i * DK:(i + 1) * DK], scalar=gk,
                                                           in1=vn[bp][:, 1, i], op0=ALU.mult, op1=ALU.add)
                        ins.then_inc(Z["r1"], 1)
                        dve.wait_ge(Z["r1"], past(n + 1))

                    of = o[:].rearrange("p c h v -> p (c h) v")

                    def moments_of_out():
                        dve.wait_ge(Z["Op"], past(2 * n + 2))
                        dve.wait_ge(Z["oi"], past(4 * n + 4))
                        dve.tensor_tensor(o[:, 1], oi[:], bank[7][:].rearrange("p (h v) -> p h v", h=HG), ALU.add).then_inc(Z["oev"], 1)
                        dve.wait_ge(Z["oev"], past(2 * n + 2))
                        for m in range(PROBS):
                            ins = dve.bn_stats(ostat[:, m], of[:, m])
                        c.link(ins)
                        dve.memset(pad[:], 0.0)
                        for m in range(PROBS):
                            ins = dve.bn_aggr(omom[:, m], ostat[:, m])
                        c.link(ins)
                        dve.tensor_scalar(ovar[:], omom[:, :, 1], EPS, None, ALU.add).then_inc(Z["ovar"], 1)

                    def normalise():
                        dve.wait_ge(Z["ors"], past(n + 1))
                        for m in range(PROBS):
                            ins = dve.tensor_scalar(of[:, m], of[:, m], omom[:, m, 0:1], ors[:, m:m + 1], ALU.subtract, ALU.mult)
                        ins.then_inc(Z["on"], 1)

                    def residual():
                        dve.wait_ge(Z["yout"], past(n + 1))
                        x2 = stream[:, bass.ds(2 * nb, 2), :].rearrange("p j c -> p (j c)")
                        dve.tensor_tensor(x2, x2, bank[7][:], ALU.add).then_inc(Z["res"], 1)

                    front, back = f is not None, n is not None
                    for u in range(6):
                        if front:
                            conv(u)
                        if back:
                            (lambda: sweep(0, 0), lambda: sweep(0, 1), lambda: sweep(0, 2), lambda: None, weighted, second_rhs)[u]()
                    if front:
                        decays()
                    if back:
                        sweep(1, 0)
                        sweep(1, 1)
                    if front:
                        products(0)
                        products(1)
                    if back:
                        sweep(1, 2)
                    if front:
                        products(2)
                        products(3)
                        start_inverse()
                    if back:
                        moments_of_out()
                    if front:
                        refine(0, 0), refine(0, 1)
                    if back:
                        normalise()
                    if front:
                        turn(0, 0), turn(0, 1)
                        for lev in (1, 2):
                            refine(lev, 0), refine(lev, 1), turn(lev, 0), turn(lev, 1)
                    if back:
                        residual()
                    if front:
                        refine(3, 0), refine(3, 1), turn(3, 0), turn(3, 1)
                        plain_blocks()
                        off_blocks(0), off_blocks(1)
                    if isinstance(f, int) and f == 0:
                        first[0] = c.n
                    elif front:
                        assert c.n == PER_C, c.n

                pipeline(dve, slot)
                base = base + first[0] + PER_C * (STEPS - 1) + 2
                dve.wait_ge(Z["res"], past(GROUPS * SEQS))
                dve.memset(pad[:], 0.0).then_inc(stage_done, 1)
            if stop > 3:
                base = routed(1, base)

        @block.tensor
        def _(pe):
            pe.wait_ge(loaded_a, 96)
            pe.wait_ge(consts, 11)
            with pe.Fori(0, SEQS) as b:
                pe.wait_ge(A["xn"], past(2 * b + 2))
                pe.wait_ge(A["attT"], past(b))
                for k in range(CT):
                    for j in range(TPS):
                        mm = pe.transpose(bank[0][:, k * SEQ + j * P:k * SEQ + (j + 1) * P], xn[:, j, k * P:(k + 1) * P], ident[:])
                mm.then_inc(A["xTp"], 1)
                pe.wait_ge(A["xT"], past(b + 1))
                pe.wait_ge(A["att"], past(2 * b))
                pe.wait_ge(A["res"], past(b * (UNITS + 1)))
                for j in range(TPS):
                    for dst, lo, hi in ((bank[1 + j][:], 0, 2 * C), (bank[3][:, j * C:(j + 1) * C], 2 * C, 3 * C)):
                        pe.matmul(dst, ones_row[:], b_qkv[:, lo:hi], start=True, stop=False)
                        for k in range(CT):
                            mm = pe.matmul(dst, xT[:, k, j * P:(j + 1) * P], w_qkv[:, k, lo:hi], start=False, stop=(k == CT - 1))
                    mm.then_inc(A["qkv"], 1)
                for m in range(4):
                    j, qk = m // 2, m % 2
                    pe.wait_ge(A["rope"], past(4 * b + 2 * j + 2))
                    for g in range(4):
                        h0 = qk * HEADS + 4 * g
                        mm = pe.transpose(bank[4 + m][:, g * P:(g + 1) * P],
                                          rot[:, j, h0:h0 + 4, :].rearrange("p h d -> p (h d)"), ident[:])
                    mm.then_inc(A["rotp"], 1)
                pe.wait_ge(A["qkT"], past(4 * b + 4))

                def heads_of(u):
                    r, part = u // 3, u % 3
                    return [(g, r) for g in (range(4) if part == 0 else (2 * (part - 1), 2 * (part - 1) + 1))], (0 if part == 0 else 1)

                def scores(u):
                    hs, j = heads_of(u)
                    bk = bank[4 + u % 2]
                    if u >= 2:
                        pe.wait_ge(A["shift"], past(UNITS * b + u - 1))
                    pe.matmul(bk[:], identb[:], (maskd if j == 0 else masko)[:].rearrange("p a s -> p (a s)"), start=True, stop=True)
                    w = (j + 1) * P
                    for m, (g, r) in enumerate(hs):
                        pr = slice(SLOT * r, SLOT * r + HD)
                        mm = pe.matmul(bk[:, m * w:(m + 1) * w], qT[pr, g, j * P:(j + 1) * P], kT[pr, g, 0:w], start=False,
                                       stop=True, skip_group_check=True)
                    mm.then_inc(A["score"], 1)

                def weigh(u):
                    pe.wait_ge(A["exp"], past(UNITS * b + u + 1))
                    if u >= 2:
                        pe.wait_ge(A["probT"], past(UNITS * b + u - 1))
                    for m in range(4):
                        mm = pe.transpose(bank[6 + u % 2][:, m * P:(m + 1) * P], prob[:, u % 2, m * P:(m + 1) * P], ident[:])
                    mm.then_inc(A["pT"], 1)

                def apply(u):
                    hs, j = heads_of(u)
                    pe.wait_ge(A["probT"], past(UNITS * b + u + 1))
                    if u == 0:
                        pe.wait_ge(A["v"], past(2 * b + 2))
                    for m, (g, r) in enumerate(hs):
                        h = 4 * g + r
                        for st in range(j + 1):
                            mm = pe.matmul(bank[(3, 1)[j]][:, h * (HD + 1):(h + 1) * (HD + 1)],
                                           probT[:, u % 2, (m * (j + 1) + st) * P:(m * (j + 1) + st + 1) * P], vx[:, st, h, :],
                                           start=(st == 0), stop=(st == j))
                    mm.then_inc(A["av"], 1)

                for u in range(UNITS + 2):
                    if u < UNITS:
                        scores(u)
                    if 1 <= u <= UNITS:
                        weigh(u - 1)
                    if u >= 2:
                        apply(u - 2)
                pe.wait_ge(A["att"], past(2 * b + 2))
                for k in range(CT):
                    for j in range(TPS):
                        mm = pe.transpose(bank[0][:, k * SEQ + j * P:k * SEQ + (j + 1) * P], att[:, j, k * P:(k + 1) * P], ident[:])
                mm.then_inc(A["attTp"], 1)
                pe.wait_ge(A["attT"], past(b + 1))
                for j in range(TPS):
                    dst = bank[2][:, j * C:(j + 1) * C]
                    pe.matmul(dst, ones_row[:], b_out[:], start=True, stop=False)
                    for k in range(CT):
                        mm = pe.matmul(dst, attT[:, k, j * P:(j + 1) * P], w_out[:, k, :], start=False, stop=(k == CT - 1))
                mm.then_inc(A["yout"], 1)

            def routed(turn):
                pe.wait_ge(R["pass1"], past(turn + 1))
                for m, src in enumerate((run_min, run_nmax)):
                    for i in range(FG):
                        mm = pe.transpose(bank[3 + m][0:ROUTES, i * P:(i + 1) * P], src[:, i, :], ident[:])
                    mm.then_inc(R["minT"], 1)
                pe.wait_ge(R["table"], past(turn + 1))
                with pe.Fori(0, FSTEPS) as s:
                    n = s + FSTEPS * turn
                    pe.wait_ge(R["fix"], past(n + 1))
                    pe.transpose(bank[0][:, 0:P], ident[:], ident[:])
                    for i in range(FG):
                        mm = pe.transpose(bank[0][0:ROUTES, i * P:(i + 1) * P], oh_fix[:, i, :], ident[:])
                    mm.then_inc(R["ohTp"], 1)
                    pe.wait_ge(R["ohT"], past(n + 1))
                    pe.wait_ge(R["sel"], past(2 * n))
                    for i in range(FG):
                        mm = pe.matmul(bank[1 + i // 2][:, (i % 2) * 256:(i % 2) * 256 + TABW], ohT[:, i, :], table[:], start=True, stop=True)
                    mm.then_inc(R["selp"], 1)

            if stop > 1:
                routed(0)
            if stop > 2:
                pe.wait_ge(Z["wab"], past(16 * 13))
                with pe.Fori(0, SEQS) as b:
                    pe.wait_ge(Z["xn"], past(2 * b + 2))
                    for k in range(CT):
                        for j in range(TPS):
                            mm = pe.transpose(bank[0][:, k * SEQ + j * P:k * SEQ + (j + 1) * P], cxn[:, j, k * P:(k + 1) * P], ident[:])
                    mm.then_inc(Z["xTp"], 1)
                    pe.wait_ge(Z["xT"], past(2 * b + 2))
                    for j in range(TPS):
                        dst = bank[1][:, j * 2 * DH:(j + 1) * 2 * DH]
                        pe.matmul(dst, ones_row[:], b_ab[:], start=True, stop=False)
                        for k in range(CT):
                            mm = pe.matmul(dst, cxT[:, k, j * P:(j + 1) * P], w_ab[:, k, :], start=False, stop=(k == CT - 1))
                    mm.then_inc(Z["abp"], 1)
                    for k in range(CT):
                        mm = pe.matmul(bank[2][0:DH, 0:SEQ], w_ab[:, k, 0:DH], cxT[:, k, :], start=(k == 0), stop=(k == CT - 1))
                    mm.then_inc(Z["abp"], 1)
                    pe.wait_ge(Z["rows"], past(b + 1))
                    pe.wait_ge(Z["gam"], past(2 * b))
                    pe.transpose(bank[3][:, 0:P], ident[:], ident[:])
                    for m, src in enumerate((gam_row, gprev_row)):
                        for j in range(TPS):
                            mm = pe.transpose(bank[3][:, (2 * m + j) * DH:(2 * m + j + 1) * DH], src[:, j * P:(j + 1) * P], ident[0:DH, 0:DH])
                    mm.then_inc(Z["gamp"], 1)
                pe.wait_ge(Z["ab"], past(2 * SEQS))
                pe.wait_ge(Z["gam"], past(2 * SEQS))
                def slot(f, n, fp):
                    bp = 1 - fp

                    def ring_free(u):
                        if u >= 3:
                            v, s_ = u - 3, f
                        else:
                            v, s_ = u + 12, f - 1
                            if isinstance(f, int) and f == 0:
                                return
                        if v < 6:
                            pe.wait_ge(Z["conv"], past(12 * s_ + 2 * v + 2))
                        elif v < 8:
                            pe.wait_ge(Z["gate"], past(2 * s_ + v - 5))
                        elif v < 12:
                            c, pair = (v - 8) // 2, (v - 8) % 2
                            pe.wait_ge(Z["read"], past(4 * s_ + v - 7))
                        else:
                            pe.wait_ge(Z["vn"], past(3 * s_ + v - 11))

                    def proj(u):
                        if u == 0:
                            pe.wait_ge(Z["wg"], past(64 * (f // SEQS) + 64))
                            pe.wait_ge(Z["xin"], past(16 * f + 16))
                        ring_free(u)
                        for i in range(2):
                            h = 2 * (u % 2) + i
                            for k in range(CT):
                                mm = pe.matmul(bank[u % 3][:, i * SEQ:(i + 1) * SEQ], w4[:, u // 2, k, h * DK:(h + 1) * DK], xTb[:, k, :],
                                               start=(k == 0), stop=(k == CT - 1))
                        mm.then_inc(Z["proj"], 1)

                    def products(u):
                        c, pair = u // 2, u % 2
                        pe.wait_ge(Z["silu"], past(3 * f + 2))
                        ring_free(8 + u)
                        for i in (2 * pair, 2 * pair + 1):
                            mm = pe.matmul(bank[(8 + u) % 3][:, (i % 2) * 2 * P:(i % 2 + 1) * 2 * P], kq[fp][:, i, c, 0, :],
                                           kq[fp][:, i, c].rearrange("p a t -> p (a t)"), start=True, stop=True)
                        mm.then_inc(Z["kq"], 1)

                    def tokens_major(m):
                        pe.wait_ge(Z["silu"], past(3 * f + 3))
                        ring_free(12 + m)
                        for i in range(HG):
                            src = vT[:, i, m * P:(m + 1) * P] if m < TPS else kq[fp][:, i, 0, 0, :]
                            mm = pe.transpose(bank[(12 + m) % 3][:, i * DK:(i + 1) * DK], src, ident[:])
                        mm.then_inc(Z["vTp"], 1)

                    def residue(lev, c):
                        if lev:
                            pe.wait_ge(Z["Cev"], past(8 * f + 2 * lev - 1 + c))
                        else:
                            pe.wait_ge(Z["Gev"], past(2 * f))
                            pe.wait_ge(Z["bdl"], past(4 * f + 4))
                            pe.wait_ge(Z["t1"], past(f + 1))
                        for i in range(HG):
                            mm = pe.matmul(bank[3 + c][:, i * BLK:(i + 1) * BLK], BDL[:, c, i], Cc[:, c, i], start=True, stop=True)
                        mm.then_inc(Z["X"], 1)

                    def improve(lev, c):
                        pe.wait_ge(Z["Rr"], past(8 * f + 2 * lev + c + 1))
                        if lev:
                            pe.wait_ge(Z["Tn"], past(8 * f + 2 * lev - 1 + c))
                        for i in range(HG):
                            mm = pe.matmul(bank[3 + c][:, 128 + i * BLK:128 + (i + 1) * BLK], BDT[fp][:, c, i], Rc[:, c, i], start=True, stop=True)
                        mm.then_inc(Z["Y"], 1)

                    def off_blocks(c):
                        pe.wait_ge(Z["bdn"], past(f + 1))
                        for i in range(HG):
                            mm = pe.matmul(bank[3 + c][:, i * P:(i + 1) * P], BDN[:, c, i], LT[:, c, i], start=True, stop=True)
                        mm.then_inc(Z["Gp"], 1)

                    def sweep(c, k):
                        if k == 0:
                            pe.wait_ge(Z["Gev"], past(2 * n + c + 1))
                            if c == 0:
                                pe.wait_ge(Z["vn"], past(3 * n + 1))
                            else:
                                pe.wait_ge(Z["oi"], past(4 * n + 4))
                                pe.wait_ge(Z["r1"], past(n + 1))
                        else:
                            pe.wait_ge(Z["yv"], past(6 * n + 3 * c + k))
                        src = y if k else (r1, vn[bp][:, 0])[c == 0]
                        for i in range(HG):
                            mm = pe.matmul(bank[5][:, i * DK:(i + 1) * DK], GT[bp][:, c, i], src[:, i], start=True, stop=True)
                        mm.then_inc(Z["ap"], 1)

                    def updates(c):
                        pe.wait_ge(Z["yv"], past(6 * n + 3 * c + 3))
                        for i in range(HG):
                            mm = pe.matmul(bank[6][:, i * DK:(i + 1) * DK], BDT[bp][:, c, i], y[:, i], start=True, stop=True)
                        mm.then_inc(Z["Up"], 1)

                    def outputs(c):
                        pe.wait_ge(Z["Uev"], past(2 * n + c + 1))
                        if c == 0:
                            pe.wait_ge(Z["res"], past(n))
                        else:
                            pe.wait_ge(Z["oev"], past(2 * n + 1))
                        for i in range(HG):
                            mm = pe.matmul(bank[7][:, i * DK:(i + 1) * DK], MT[bp][:, c, i], U[:, c, i], start=True, stop=True)
                        mm.then_inc(Z["Op"], 1)

                    def state():
                        pe.wait_ge(Z["Uw"], past(n + 1))
                        for i in range(HG):
                            mm = pe.matmul(bank[5][:, i * DK:(i + 1) * DK], kn[bp][:, i], Uw[:, i], start=True, stop=True)
                        mm.then_inc(Z["Sp"], 1)

                    def from_state():
                        pe.wait_ge(Z["Sev"], past(n + 1))
                        for a, sg in ((0, "KS"), (1, "QS")):
                            for i in range(HG):
                                mm = pe.matmul(bank[6 - a][:, i * DK:(i + 1) * DK], kq[bp][:, i, 1, a, :], S[:, i], start=True, stop=True)
                            mm.then_inc(Z[sg], 1)

                    def outT(c):
                        pe.wait_ge(Z["on"], past(n + 1))
                        for i in range(HG):
                            mm = pe.transpose(bank[5 + c][:, i * P:(i + 1) * P], o[:, c, i], ident[:])
                        mm.then_inc(Z["oTp"], 1)

                    def project_out():
                        pe.wait_ge(Z["wo"], past(16 * (n // SEQS) + 16))
                        for c in range(TPS):
                            pe.wait_ge(Z["oG"], past(2 * n + c + 1))
                            for i in range(HG):
                                mm = pe.matmul(bank[7][:, c * C:(c + 1) * C], oG[:, c, i], w_o[:, i], start=(i == 0), stop=(i == HG - 1))
                        mm.then_inc(Z["yout"], 1)

                    front, back = f is not None, n is not None
                    behind = (lambda: sweep(0, 0), lambda: sweep(0, 1), lambda: sweep(0, 2), lambda: updates(0),
                              lambda: outputs(0), state, from_state, lambda: sweep(1, 0))
                    for u in range(8):
                        if front:
                            proj(u)
                        if back:
                            behind[u]()
                    if back:
                        sweep(1, 1)
                    if front:
                        products(0), products(1)
                    if back:
                        sweep(1, 2)
                    if front:
                        products(2), products(3)
                    if back:
                        updates(1)
                    if front:
                        tokens_major(0), tokens_major(1), tokens_major(2)
                    if back:
                        outputs(1)
                    if front:
                        for lev in range(4):
                            residue(lev, 0), residue(lev, 1)
                            improve(lev, 0), improve(lev, 1)
                            if back and lev == 1:
                                outT(0), outT(1)
                            if back and lev == 2:
                                project_out()
                        off_blocks(0), off_blocks(1)
                    else:
                        outT(0), outT(1)
                        project_out()

                pipeline(pe, slot)
            if stop > 3:
                routed(1)


def kernel(**inputs):
    import concourse.bacc as bacc
    from concourse.bass_utils import run_bass_kernel_spmd

    a, d, f = "L0_attn_a_", "L0_attn_b_", "L0_ffn_"
    nc = bacc.Bacc("TRN2", target_bir_lowering=False, num_devices=1)
    theta = (np.float32(10000.0) ** (-np.arange(HALF, dtype=np.float32) / np.float32(HALF))).astype(np.float32)
    angle = np.arange(SEQ, dtype=np.float32)[:, None] * theta[None, :]
    get = {k: np.asarray(v) for k, v in inputs.items()}
    arrays = {
        "x": get[a + "x"].reshape(-1, C), "w_qkv": get[a + "w_qkv"].T, "w_out": get[a + "w_out"].T,
        "b_qkv": get[a + "b_qkv"], "b_out": get[a + "b_out"], "cos": np.cos(angle), "sin": np.sin(angle),
        "gamma": get[f + "ln_gamma"], "beta": get[f + "ln_beta"], "bases": get[f + "spline_bases"],
        "slopes": get[f + "spline_slopes"], "oscale": get[f + "output_scale"],
        "ln_w": get[d + "ln_w"], "ln_b": get[d + "ln_b"], "ba": get[d + "ba"], "bb": get[d + "bb"],
        "Wa": get[d + "Wa"], "Wb": get[d + "Wb"], "Wq": get[d + "Wq"], "Wk": get[d + "Wk"],
        "Wv": get[d + "Wv"], "Wg": get[d + "Wg"], "Wo": get[d + "Wo"],
    }
    for k in "qkv":
        arrays[f"cw_{k}"] = get[d + f"conv_{k}_w"].reshape(DH, DK, TAPS).transpose(1, 0, 2)
        arrays[f"cb_{k}"] = get[d + f"conv_{k}_b"].reshape(DH, DK).T
    arrays = {k: np.ascontiguousarray(v) for k, v in arrays.items()}
    io = {k: nc.dram_tensor(f"in_{k}", v.shape, mybir.dt.from_np(v.dtype), kind="ExternalInput").ap() for k, v in arrays.items()}
    io["out"] = nc.dram_tensor("out", [SEQS * SEQ, C], F32, kind="ExternalOutput").ap()
    program(nc, io)
    r = run_bass_kernel_spmd(nc, [{f"in_{k}": v for k, v in arrays.items()}], core_ids=[0])
    return r.results[0]["out"].reshape(SEQS, SEQ, C)
```

```python
from contextlib import ExitStack

import numpy as np

import concourse.bass as bass
from concourse import mybir

F32 = mybir.dt.float32
BF16 = mybir.dt.bfloat16
ALU = mybir.AluOpType
ACT = mybir.ActivationFunctionType
AX = mybir.AxisListType

P = 128
SEQS, SEQ, C = 16, 256, 256
TPS = SEQ // P
TILES = SEQS * TPS
CT = C // P
HEADS, HD = 16, 16
HALF = HD // 2
SLOT = 32
UNITS = 12
SCORE_BANKS = (4, 5, 0, 2)
ROT_BANKS = (6, 7, 0, 3)
EPS = 1e-5
MASKED = -1e30
ROUTES, SLICE, CLUSTER, GRID = 64, 4, 8, 16
TABW = 2 * SLICE * GRID + 3
FG = 4
FSTEPS = TILES // FG
FAR = 1e30
DH, DK = 16, 128
HG = 4
GROUPS = DH // HG
TAPS = 4
BLK = 32
PROBS = HG * TPS
KAPPA2 = 1.0 / DK
KAPPA = float(DK) ** -0.5


def past(count):
    return count + 1


STEPS = GROUPS * SEQS


RING = {"proj": (0, 1, 2, 3, 4, 5, 8, 11), "products": (6, 7, 9, 10), "tokens_major": (12, 13, 14)}


def sequences(eng, head, body):
    head(0, 0), head(0, 1)
    with eng.Fori(0, SEQS - 1) as b:
        body(b, head)
    body(SEQS - 1, None)


def pipeline(eng, slot):
    slot(0, None, None, 0)
    slot(1, 0, None, 1)
    with eng.Fori(1, STEPS // 2) as m:
        slot(2 * m, 2 * m - 1, 2 * m - 2, 0)
        slot(2 * m + 1, 2 * m, 2 * m - 1, 1)
    slot(None, STEPS - 1, STEPS - 2, 0)
    slot(None, None, STEPS - 1, 1)


class Chain:

    def __init__(self, eng, sem, base=0):
        self.eng, self.sem, self.base, self.n = eng, sem, base, 0

    def mark(self, ins):
        self.n += 1
        ins.then_inc(self.sem, 1)
        return self.n

    def wait(self, n):
        self.eng.wait_ge(self.sem, self.base + n)

    def link(self, ins):
        self.n += 1
        ins.then_inc(self.sem, 1)
        self.eng.wait_ge(self.sem, self.base + self.n)


def program(nc, io):
    ctx = ExitStack()
    with ctx:
        def sb(name, shape, dt=F32):
            return ctx.enter_context(nc.sbuf_tensor(name, shape, dt))

        def sem(name):
            return ctx.enter_context(nc.semaphore(name))

        bank = [ctx.enter_context(nc.psum_tensor(f"bank{i}", [P, 512], F32)) for i in range(8)]

        stream = sb("stream", [P, TILES, C])
        ident = sb("ident", [P, P])
        ones_row = sb("ones_row", [1, P])
        half_neg = sb("half_neg", [P, TILES])
        moments = sb("moments", [P, TILES, 2])
        rstd = sb("rstd", [P, TILES])
        stats = sb("stats", [P, 8, 6])
        mom8 = sb("mom8", [P, 8, 2])
        pad = sb("pad", [P, 1])

        xT_dram = nc.dram_tensor("xT_scratch", [SEQS, P, CT * SEQ], F32).ap()
        decay_dram = nc.dram_tensor("decay_scratch", [SEQS, DH, SEQ], F32).ap()

        loaded_x = sem("loaded_x")
        loaded_a = sem("loaded_a")
        consts = sem("consts")
        v_step = sem("v_step")
        p_step = sem("p_step")
        a_step = sem("a_step")
        stage_done = sem("stage_done")
        stored = sem("stored")

        stack_a = ExitStack()

        def sa(name, shape, dt=F32):
            return stack_a.enter_context(nc.sbuf_tensor(name, shape, dt))
        w_qkv = sa("w_qkv", [P, CT, 3 * C])
        w_out = sa("w_out", [P, CT, C])
        b_qkv = sa("b_qkv", [1, 3 * C])
        b_out = sa("b_out", [1, C])
        cosT = sa("cosT", [P, TPS, HALF])
        sinT = sa("sinT", [P, TPS, HALF])
        identb = sa("identb", [P, P], BF16)
        maskb = sa("maskb", [P, 2 * P], BF16)
        maskd = sa("maskd", [P, 4, P], BF16)
        masko = sa("masko", [P, 2, 2 * P], BF16)
        xn = sa("xn", [P, TPS, C])
        xT = sa("xT", [P, CT, SEQ])
        rope_t = sa("rope_t", [P, 4, TPS, 2 * HEADS * HALF])
        rot = sa("rot", [P, TPS, 2 * HEADS, SLOT])
        vx = sa("vx", [P, TPS, HEADS, HD + 1])
        qT = sa("qT", [P, 4, 4, SEQ])
        kT = sa("kT", [P, 4, SEQ])
        row_max = sa("row_max", [P, 2, 4])
        prob = sa("prob", [P, 4, 512])
        probT = sa("probT", [P, 4, 512])
        rsum = sa("rsum", [P, TPS, HEADS])
        att = sa("att", [P, TPS, C])
        attT = sa("attT", [P, CT, SEQ])
        stack_a.close()

        stack_f = ExitStack()

        def sf(name, shape, dt=F32):
            return stack_f.enter_context(nc.sbuf_tensor(name, shape, dt))
        gam = sf("gam", [P, C])
        bet = sf("bet", [P, C])
        sl_all = sf("sl_all", [P, C, GRID])
        sl_sum = sf("sl_sum", [P, C])
        sl_sign = sf("sl_sign", [P, C])
        xf = sf("xf", [P, TILES, C])
        onehot = sf("onehot", [P, TILES, ROUTES])
        table = sf("table", [ROUTES, TABW])
        rank = sf("rank", [P, ROUTES])
        kgrid = sf("kgrid", [P, GRID + 1])
        ranki = sf("ranki", [P, ROUTES], mybir.dt.int32)
        kgridi = sf("kgridi", [P, GRID + 1], mybir.dt.int32)
        z = sf("z", [P, FG, C])
        fmom = sf("fmom", [P, FG, 2])
        fvar = sf("fvar", [P, FG])
        frs = sf("frs", [P, FG])
        fmom2 = sf("fmom2", [P, FG, 2])
        fvar2 = sf("fvar2", [P, FG])
        frs2 = sf("frs2", [P, FG])
        sgn = sf("sgn", [P, FG, C])
        tsc = sf("tsc", [P, FG, ROUTES])
        csc = sf("csc", [P, FG, CLUSTER])
        comp = sf("comp", [P, FG, ROUTES])
        best = sf("best", [P, FG])
        smin = sf("smin", [P, FG, ROUTES])
        smax = sf("smax", [P, FG, ROUTES])
        far = sf("far", [P, FG, ROUTES])
        run_min = sf("run_min", [P, FG, ROUTES])
        run_nmax = sf("run_nmax", [P, FG, ROUTES])
        ext = sf("ext", [ROUTES, 2])
        oh_fix = sf("oh_fix", [P, FG, ROUTES])
        ohT = sf("ohT", [ROUTES, FG, P])
        selr = sf("selr", [P, FG, TABW])
        pick = sf("pick", [P, FG, C])
        xs = sf("xs", [P, FG, SLICE])
        u16 = sf("u16", [P, FG, SLICE])
        ge = sf("ge", [P, FG * SLICE, GRID + 1])
        floor1 = sf("floor1", [P, FG * SLICE])
        gmask = sf("gmask", [P, FG, SLICE * GRID])
        bsel = sf("bsel", [P, FG * SLICE])
        ssel = sf("ssel", [P, FG * SLICE])
        tmpg = sf("tmpg", [P, FG, SLICE * GRID])
        delta = sf("delta", [P, FG, SLICE])
        stack_f.close()

        stack_c = ExitStack()

        def sc(name, shape, dt=F32):
            return stack_c.enter_context(nc.sbuf_tensor(name, shape, dt))
        w_ab = sc("w_ab", [P, CT, 2 * DH])
        b_ab = sc("b_ab", [1, 2 * DH])
        b_a = sc("b_a", [DH, 1])
        beta_k = sc("beta_k", [P, TILES, DH])
        beta_q = sc("beta_q", [P, TILES, DH])
        beta = sc("beta", [P, TILES, DH])
        gam_q = sc("gam_q", [P, TILES, DH])
        gam_k = sc("gam_k", [P, TILES, DH])
        ln_w = sc("ln_w", [P, 1])
        ln_b = sc("ln_b", [P, 1])
        conv_w = sc("conv_w", [P, 3, DH, TAPS])
        conv_b = sc("conv_b", [P, 3, DH])
        id_many = sc("id_many", [P, PROBS, P])
        id1c = sc("id1c", [P, BLK])
        id2c = sc("id2c", [P, BLK])
        shifted = sc("shifted", [P, 2, 2, SEQ])
        cxn, cxT = shifted[:, 0], shifted[:, 1]
        alphaT = sc("alphaT", [DH, SEQ])
        alpha_z = sc("alpha_z", [DH, SEQ])
        alpha_r = sc("alpha_r", [DH, SEQ])
        gam_row = sc("gam_row", [DH, SEQ])
        gprev_row = sc("gprev_row", [DH, SEQ])
        w4 = sc("w4", [P, 4, CT, HG * DK])
        w_o = sc("w_o", [P, HG, C])
        xTb = sc("xTb", [P, CT, SEQ])
        abc = sc("abc", [P, HG, SEQ])
        acc = sc("acc", [P, 3, HG, SEQ])
        vT = sc("vT", [P, HG, SEQ])
        dec = sc("dec", [P, HG, SEQ])
        LT = sc("LT", [P, TPS, HG, P])
        BDL = sc("BDL", [P, TPS, HG, P])
        BDN = sc("BDN", [P, TPS, HG, P])
        PT = sc("PT", [P, TPS, HG, 2, BLK])
        two = range(2)
        kq = [sc(f"kq{i}", [P, HG, TPS, 2, P]) for i in two]
        gT = [sc(f"gT{i}", [P, HG, SEQ]) for i in two]
        vn = [sc(f"vn{i}", [P, TPS, HG, DK]) for i in two]
        kn = [sc(f"kn{i}", [P, HG, DK]) for i in two]
        MT = [sc(f"MT{i}", [P, TPS, HG, P]) for i in two]
        BDT = [sc(f"BDT{i}", [P, TPS, HG, P]) for i in two]
        GT = [sc(f"GT{i}", [P, TPS, HG, P]) for i in two]
        wgt = [sc(f"wgt{i}", [P, HG]) for i in two]
        y = sc("y", [P, HG, DK])
        r1 = sc("r1", [P, HG, DK])
        U = sc("U", [P, TPS, HG, DK])
        Uw = sc("Uw", [P, HG, DK])
        S = sc("S", [P, HG, DK])
        oi = sc("oi", [P, HG, DK])
        o = sc("o", [P, TPS, HG, DK])
        ostat = sc("ostat", [P, PROBS, 6])
        omom = sc("omom", [P, PROBS, 2])
        ovar = sc("ovar", [P, PROBS])
        ors = sc("ors", [P, PROBS])
        oT = sc("oT", [P, TPS, HG, P])
        oG = sc("oG", [P, TPS, HG, P])
        stack_c.close()

        def powers_of(lev, c):
            half = bank[3 + c][:, (lev % 2) * 256:(lev % 2) * 256 + 2 * HG * BLK]
            return half.rearrange("p (h a t) -> p h a t", h=HG, a=2)

        A = {k: sem("A_" + k) for k in (
            "xn", "xTp", "xT", "qkv", "rope", "v", "rotp", "qkT", "score", "shift", "exp", "pT",
            "probT", "av", "att", "attTp", "attT", "yout", "res", "var", "rstd")}
        R = {k: sem("R_" + k) for k in (
            "loaded", "var", "rs", "z", "added", "xf", "sign", "minT", "table", "pass1",
            "fix", "ohTp", "ohT", "selp", "sel", "pick0", "xs", "delta", "scat", "res", "cons")}
        Z = {k: sem("Z_" + k) for k in (
            "w", "wab", "xn", "xTp", "xT", "stored", "abp", "ab", "rows", "gamp", "gam", "cons",
            "var", "rstd",
            "wg", "wo", "xin", "abc", "proj", "tap", "conv", "silu", "gate", "vTp", "vn", "kq", "LM", "wgt", "Uw", "read",
            "bdl", "t1", "summed", "P1", "X", "Rr", "Y", "Cev", "Tn", "bdn", "Gp", "Gev", "ap", "yv", "Up", "Uev",
            "Sp", "Sev", "KS", "QS", "r1", "oi", "Op", "oev", "ovar", "ors", "on", "oTp", "oT",
            "oG", "yout", "res", "dec")}

        block = ctx.enter_context(nc.Block())

        @block.sync
        def _(sp):
            for g in range(4):
                n = TILES // 4
                sp.dma_start(stream[:, g * n:(g + 1) * n, :],
                             io["x"][g * n * P:(g + 1) * n * P, :].rearrange("(n p) c -> p n c", p=P)
                             ).then_inc(loaded_x, 16)
            sp.dma_start(w_qkv[:], io["w_qkv"].rearrange("(k p) n -> p k n", p=P)).then_inc(loaded_a, 16)
            sp.dma_start(w_out[:], io["w_out"].rearrange("(k p) n -> p k n", p=P)).then_inc(loaded_a, 16)
            sp.dma_start(b_qkv[:], io["b_qkv"].rearrange("(a n) -> a n", a=1)).then_inc(loaded_a, 16)
            sp.dma_start(b_out[:], io["b_out"].rearrange("(a n) -> a n", a=1)).then_inc(loaded_a, 16)
            sp.dma_start(cosT[:], io["cos"].rearrange("(j p) n -> p j n", p=P)).then_inc(loaded_a, 16)
            sp.dma_start(sinT[:], io["sin"].rearrange("(j p) n -> p j n", p=P)).then_inc(loaded_a, 16)

            def routed_loads():
                row = io["slopes"].rearrange("(a r) j k -> a (r j) k", a=1)
                sp.dma_start(gam[:], io["gamma"].rearrange("(a n) -> a n", a=1).broadcast_to([P, C])).then_inc(R["loaded"], 16)
                sp.dma_start(bet[:], io["beta"].rearrange("(a n) -> a n", a=1).broadcast_to([P, C])).then_inc(R["loaded"], 16)
                sp.dma_start(sl_all[:], row.broadcast_to([P, C, GRID])).then_inc(R["loaded"], 16)
                w = SLICE * GRID
                sp.dma_start(table[:, 0:w], io["bases"].rearrange("r j k -> r (j k)")).then_inc(R["loaded"], 16)
                sp.dma_start(table[:, w:2 * w], io["slopes"].rearrange("r j k -> r (j k)")).then_inc(R["loaded"], 16)
                sp.dma_start(table[:, 2 * w:2 * w + 1], io["oscale"].rearrange("(r a) -> r a", a=1)).then_inc(R["loaded"], 16)

            sp.wait_ge(stage_done, 1)
            routed_loads()
            sp.wait_ge(stage_done, 2)
            sp.dma_start(w_ab[:, :, 0:DH], io["Wa"].rearrange("(k p) n -> p k n", p=P)).then_inc(Z["wab"], 16)
            sp.dma_start(w_ab[:, :, DH:], io["Wb"].rearrange("(k p) n -> p k n", p=P)).then_inc(Z["wab"], 16)
            sp.dma_start(b_ab[:, 0:DH], io["ba"].rearrange("(a n) -> a n", a=1)).then_inc(Z["wab"], 16)
            sp.dma_start(b_ab[:, DH:], io["bb"].rearrange("(a n) -> a n", a=1)).then_inc(Z["wab"], 16)
            sp.dma_start(b_a[:], io["ba"].rearrange("(n a) -> n a", a=1)).then_inc(Z["wab"], 16)
            sp.dma_start(ln_w[:], io["ln_w"].rearrange("(n a) -> n a", a=1)).then_inc(Z["wab"], 16)
            sp.dma_start(ln_b[:], io["ln_b"].rearrange("(n a) -> n a", a=1)).then_inc(Z["wab"], 16)
            for n, k in enumerate("kqv"):
                sp.dma_start(conv_w[:, n], io[f"cw_{k}"]).then_inc(Z["wab"], 16)
                sp.dma_start(conv_b[:, n], io[f"cb_{k}"]).then_inc(Z["wab"], 16)
            with sp.Fori(0, SEQS) as b:
                sp.wait_ge(Z["xT"], past(2 * b + 2))
                sp.dma_start(xT_dram[b], cxT[:].rearrange("p k t -> p (k t)")).then_inc(Z["stored"], 16)
                sp.wait_ge(Z["rows"], past(b + 1))
                sp.dma_start(decay_dram[b], alpha_z[:]).then_inc(Z["stored"], 16)
            sp.wait_ge(Z["stored"], past(32 * SEQS))
            def token_loads(n):
                sp.wait_ge(Z["proj"], past(8 * n))
                sp.dma_start(xTb[:].rearrange("p k t -> p (k t)"), xT_dram[n % SEQS]).then_inc(Z["xin"], 16)
                sp.wait_ge(Z["dec"], past(n))
                row = decay_dram.rearrange("b (g h) t -> b g (h t)", g=GROUPS)[bass.ds(n % SEQS, 1), bass.ds(n // SEQS, 1), :]
                sp.dma_start(abc[:].rearrange("p h t -> p (h t)"),
                             row.rearrange("a b n -> (a b) n").broadcast_to([P, HG * SEQ])).then_inc(Z["abc"], 16)

            with sp.Fori(0, GROUPS) as g:
                sp.wait_ge(Z["proj"], past(8 * SEQS * g))
                for k, w in enumerate(("Wk", "Wq", "Wv", "Wg")):
                    sp.dma_start(w4[:, k], io[w].rearrange("(k p) n -> p k n", p=P)[:, :, bass.ds(g * HG * DK, HG * DK)]).then_inc(Z["wg"], 16)
                token_loads(g * SEQS)
                token_loads(g * SEQS + 1)
                sp.wait_ge(Z["yout"], past(SEQS * g))
                sp.dma_start(w_o[:], io["Wo"].rearrange("(h p) n -> p h n", p=P)[:, bass.ds(g * HG, HG), :]).then_inc(Z["wo"], 16)
                with sp.Fori(2, SEQS) as b:
                    token_loads(g * SEQS + b)
            sp.wait_ge(stage_done, 3)
            routed_loads()
            sp.wait_ge(stage_done, 4)
            for g in range(4):
                n = TILES // 4
                sp.dma_start(io["out"][g * n * P:(g + 1) * n * P, :].rearrange("(n p) c -> p n c", p=P),
                             stream[:, g * n:(g + 1) * n, :]).then_inc(stored, 16)
            sp.wait_ge(stored, 64)

        @block.gpsimd
        def _(pool):
            for signals in (A, R, Z):
                for signal in signals.values():
                    pool.sem_inc(signal, 1)
            ch = Chain(pool, p_step)
            ch.link(pool.memset(ident[:], 0.0))
            ch.link(pool.affine_select(out=ident[:], in_=ident[:], compare_op=ALU.not_equal, fill=1.0,
                                       base=0, pattern=[[-1, P]], channel_multiplier=1))
            pool.tensor_copy(identb[:], ident[:]).then_inc(consts, 1)
            pool.memset(ones_row[:], 1.0).then_inc(consts, 1)
            pool.memset(half_neg[:], -0.5).then_inc(consts, 1)
            ch.link(pool.memset(maskb[:], 0.0))
            ch.link(pool.affine_select(out=maskb[:, P:], in_=maskb[:, P:], compare_op=ALU.is_ge, fill=MASKED,
                                       base=0, pattern=[[-1, P]], channel_multiplier=1))
            for i in range(4):
                pool.tensor_copy(maskd[:, i], maskb[:, P:]).then_inc(consts, 1)
            for i in range(2):
                pool.tensor_copy(masko[:, i], maskb[:]).then_inc(consts, 1)
            pool.memset(rot[:], 0.0).then_inc(consts, 1)
            pool.memset(qT[:], 0.0).then_inc(consts, 1)
            pool.memset(vx[:], 1.0).then_inc(consts, 1)
            n0 = ch.n
            pool.wait_ge(A["var"], past(1))
            pool.wait_ge(consts, 3)
            pool.tensor_tensor(rstd[:], rstd[:], half_neg[:], ALU.pow).then_inc(A["rstd"], 1)

            def routed(turn):
                pool.wait_ge(stage_done, 1 + 2 * turn)
                c1 = Chain(pool, p_step, pstep_base(turn))
                c1.link(pool.iota(ranki[:].rearrange("p (c i) -> p c i", c=CLUSTER), [[-P, CLUSTER], [-1, ROUTES // CLUSTER]],
                                  base=0, channel_multiplier=0))
                c1.link(pool.iota(kgridi[:], [[1, GRID + 1]], base=0, channel_multiplier=0))
                pool.tensor_copy(rank[:], ranki[:]).then_inc(R["cons"], 1)
                pool.tensor_copy(kgrid[:], kgridi[:]).then_inc(R["cons"], 1)
                pool.memset(run_min[:], 2 * FAR).then_inc(R["cons"], 1)
                pool.memset(run_nmax[:], 2 * FAR).then_inc(R["cons"], 1)
                with pool.Fori(0, FSTEPS) as s:
                    n = s + FSTEPS * turn
                    pool.wait_ge(R["var"], past(2 * n + 1))
                    pool.tensor_tensor(frs[:], fvar[:], half_neg[:, 0:FG], ALU.pow).then_inc(R["rs"], 1)
                    pool.wait_ge(R["z"], past(n + 1))
                    pool.tensor_tensor(stream[:, bass.ds(s * FG, FG), :], stream[:, bass.ds(s * FG, FG), :], z[:], ALU.add).then_inc(R["added"], 1)
                    pool.wait_ge(R["var"], past(2 * n + 2))
                    pool.tensor_tensor(frs2[:], fvar2[:], half_neg[:, 0:FG], ALU.pow).then_inc(R["rs"], 1)
                with pool.Fori(0, FSTEPS) as s:
                    n = s + FSTEPS * turn
                    pool.wait_ge(R["pass1"], past(turn + 1))
                    pool.wait_ge(R["ohTp"], past(n))
                    pool.wait_ge(R["res"], past(n))
                    pool.tensor_copy(oh_fix[:], onehot[:, bass.ds(s * FG, FG), :]).then_inc(R["fix"], 1)
                    pool.wait_ge(R["fix"], past(n + 1))
                    pool.tensor_tensor(pick[:].rearrange("p f (r j) -> p (f r) j", j=SLICE),
                                       xf[:, bass.ds(s * FG, FG), :].rearrange("p f (r j) -> p (f r) j", j=SLICE),
                                       oh_fix[:].rearrange("p f r -> p (f r)").unsqueeze(2).broadcast_to([P, FG * ROUTES, SLICE]),
                                       ALU.mult).then_inc(R["pick0"], 1)

            def pstep_base(turn):
                return n0 + 2 * turn

            routed(0)
            pool.wait_ge(stage_done, 2)
            base = n0 + 4
            cc = Chain(pool, p_step, base)
            for i in range(PROBS):
                pool.tensor_copy(id_many[:, i], ident[:]).then_inc(Z["cons"], 1)
            for q in range(P // BLK):
                qs = slice(q * BLK, (q + 1) * BLK)
                pool.wait_ge(Z["cons"], past(PROBS + q))
                pool.tensor_scalar(id2c[qs, :], ident[qs, q * BLK:(q + 1) * BLK], 2.0, 0.0, ALU.mult, ALU.add).then_inc(Z["cons"], 1)
            for q in range(P // BLK):
                qs = slice(q * BLK, (q + 1) * BLK)
                pool.wait_ge(Z["cons"], past(PROBS + P // BLK + q))
                pool.tensor_scalar(id1c[qs, :], ident[qs, q * BLK:(q + 1) * BLK], 1.0, 0.0, ALU.mult, ALU.add).then_inc(Z["cons"], 1)
            pool.wait_ge(Z["cons"], past(PROBS + 2 * (P // BLK)))
            for m in (BDL, BDT[0], BDT[1], BDN):
                pool.memset(m[:], 0.0).then_inc(Z["cons"], 1)
            pool.tensor_copy(LT[:].rearrange("p c h t -> p (c h) t")[:, :, 0:1], id_many[:, :, 0:1]).then_inc(Z["cons"], 1)
            pool.wait_ge(Z["var"], past(1))
            pool.tensor_tensor(rstd[:], rstd[:], half_neg[:], ALU.pow).then_inc(Z["rstd"], 1)
            def slot(f, h, n, fp):
                def add_shifted(u):
                    kind, pair = u // 2, u % 2
                    pool.wait_ge(Z["conv"], past(12 * f + 2 * u + 2))
                    dst = acc[:, kind, 2 * pair:2 * pair + 2, 1:]
                    pool.tensor_tensor(dst, dst, shifted[:, u % 2, :, 1:], ALU.add).then_inc(Z["summed"], 1)

                def add_identity(tc):
                    pool.wait_ge(Z["read"], past(4 * f + 2 * tc + 2))
                    pool.tensor_tensor(LT[:, tc, :, 1:P], LT[:, tc, :, 1:P], id_many[:, 0:HG, 1:P], ALU.add).then_inc(Z["LM"], 1)

                front, back = f is not None, n is not None
                if front:
                    for u in range(5):
                        add_shifted(u)
                if back:
                    pool.wait_ge(Z["ovar"], past(n + 1))
                    pool.tensor_tensor(ors[:], ovar[:], half_neg[:, 0:PROBS], ALU.pow).then_inc(Z["ors"], 1)
                if front:
                    add_shifted(5)
                if back:
                    for c in range(TPS):
                        pool.wait_ge(Z["gate"], past(2 * n + 2))
                        pool.wait_ge(Z["yout"], past(n))
                        pool.wait_ge(Z["oT"], past(2 * n + c + 1))
                        pool.tensor_tensor(oG[:, c], oT[:, c], gT[fp][:, :, c * P:(c + 1) * P], ALU.mult).then_inc(Z["oG"], 1)
                if front:
                    add_identity(0), add_identity(1)

            pipeline(pool, slot)
            routed(1)

        @block.scalar
        def _(act):
            act.wait_ge(consts, 12)

            def tokens(b):
                act.wait_ge(A["xTp"], past(b + 1))
                act.copy(xT[:].rearrange("p k t -> p (k t)"), bank[0][:]).then_inc(A["xT"], 1)

            def head(b, part):
                if part == 0:
                    return
                act.wait_ge(A["qkv"], past(2 * b + 2))
                for j in range(TPS):
                    act.copy(vx[:, j, :, 0:HD], bank[2][:, j * C:(j + 1) * C].rearrange("p (h d) -> p h d", d=HD)).then_inc(A["v"], 1)
                for m in (1, 0, 3, 2):
                    act.wait_ge(A["rotp"], past(4 * b + m + 1))
                    ts = slice((m // 2) * P, (m // 2 + 1) * P)
                    src = bank[ROT_BANKS[m]][:].rearrange("p (g t) -> p g t", g=4)
                    if m % 2:
                        act.copy(kT[:, :, ts], src).then_inc(A["qkT"], 1)
                    else:
                        for r in range(4):
                            sl = slice(SLOT * r, SLOT * (r + 1))
                            act.copy(qT[sl, r, :, ts], src[sl]).then_inc(A["qkT"], 1)

            def body(b, head):
                for pair in range(0, UNITS + 2, 2):
                    for turn, u in ((0, pair), (1, pair - 2), (0, pair + 1), (1, pair - 1)):
                        if turn == 0 and u < UNITS:
                            act.wait_ge(A["shift"], past(UNITS * b + u + 1))
                            act.activation(prob[:, u % 4], prob[:, u % 4], ACT.Exp, scale=float(HD) ** -0.5).then_inc(A["exp"], 1)
                        if turn == 1 and u >= 0:
                            if u == UNITS - 1 and head:
                                tokens(b + 1)
                            act.wait_ge(A["pT"], past(UNITS * b + u + 1))
                            if u >= 4:
                                act.wait_ge(A["av"], past(UNITS * b + u - 3))
                            act.copy(probT[:, u % 4], bank[6 + u % 2][:]).then_inc(A["probT"], 1)
                act.wait_ge(A["attTp"], past(b + 1))
                act.copy(attT[:].rearrange("p k t -> p (k t)"), bank[3][:]).then_inc(A["attT"], 1)
                if head:
                    head(b + 1, 1)

            tokens(0)
            sequences(act, head, body)

            def routed(turn):
                with act.Fori(0, FSTEPS) as s:
                    n = s + FSTEPS * turn
                    act.wait_ge(R["xf"], past(n + 1))
                    act.activation(sgn[:], xf[:, bass.ds(s * FG, FG), :], ACT.Sign).then_inc(R["sign"], 1)
                with act.Fori(0, FSTEPS) as s:
                    n = s + FSTEPS * turn
                    act.wait_ge(R["ohTp"], past(n + 1))
                    act.copy(ohT[:].rearrange("r f t -> r (f t)"), bank[0][0:ROUTES, :]).then_inc(R["ohT"], 1)
                    act.wait_ge(R["selp"], past(n + 1))
                    act.wait_ge(R["delta"], past(n))
                    for h in range(2):
                        act.copy(selr[:, 2 * h:2 * h + 2, :], bank[1 + h][:].rearrange("p (i w) -> p i w", i=2)[:, :, 0:TABW]).then_inc(R["sel"], 1)

            routed(0)
            act.wait_ge(Z["wab"], past(16 * 13))
            with act.Fori(0, SEQS) as b:
                act.wait_ge(Z["xTp"], past(b + 1))
                act.wait_ge(Z["stored"], past(32 * b))
                for k in range(CT):
                    act.copy(cxT[:, k], bank[0][:, k * SEQ:(k + 1) * SEQ]).then_inc(Z["xT"], 1)
                act.wait_ge(Z["abp"], past(2 * b + 1))
                act.activation(beta[:, bass.ds(2 * b, 2), :], bank[1][:, 0:2 * 2 * DH].rearrange("p (j n) -> p j n", j=2)[:, :, DH:], ACT.Sigmoid).then_inc(Z["ab"], 1)
                act.wait_ge(Z["abp"], past(2 * b + 2))
                act.wait_ge(Z["rows"], past(b))
                act.activation(alphaT[:], bank[2][0:DH, 0:SEQ], ACT.Sigmoid, bias=b_a[:]).then_inc(Z["ab"], 1)
                act.wait_ge(Z["gamp"], past(b + 1))
                act.mul(gam_q[:, bass.ds(2 * b, 2), :], bank[3][:, 0:2 * DH].rearrange("p (j n) -> p j n", j=2), KAPPA).then_inc(Z["gam"], 1)
                act.mul(gam_k[:, bass.ds(2 * b, 2), :], bank[3][:, 2 * DH:4 * DH].rearrange("p (j n) -> p j n", j=2), -KAPPA2).then_inc(Z["gam"], 1)
            def slot(f, h, n, fp):

                def tap(u):
                    kind, pair = u // 2, u % 2
                    act.wait_ge(Z["silu"], past(3 * f))
                    act.wait_ge(Z["proj"], past(8 * f + u + 1))
                    if middle or u > 1:
                        act.wait_ge(Z["summed"], past(6 * f + u - 1))
                    for i in (2 * pair, 2 * pair + 1):
                        head = (f // SEQS) * HG + i
                        act.activation(shifted[:, u % 2, i % 2, 1:], bank[RING["proj"][u] % 3][:, (i % 2) * SEQ:(i % 2 + 1) * SEQ - 1], ACT.Copy,
                                       scale=conv_w[:, kind, bass.ds(head, 1), TAPS - 2:TAPS - 1].rearrange("p a b -> p (a b)")).then_inc(Z["tap"], 1)
                        act.activation(acc[:, kind, i], bank[RING["proj"][u] % 3][:, (i % 2) * SEQ:(i % 2 + 1) * SEQ], ACT.Identity,
                                       scale=conv_w[:, kind, bass.ds(head, 1), TAPS - 1:TAPS].rearrange("p a b -> p (a b)"),
                                       bias=conv_b[:, kind, bass.ds(head, 1)]).then_inc(Z["tap"], 1)

                def silu(kind):
                    act.wait_ge(Z["summed"], past(6 * f + 2 * kind + 2))
                    if kind < 2:
                        act.wait_ge(Z["QS"], past(f - 1 if n is not None else 0))
                        act.activation(kq[fp][:, :, :, kind, :], acc[:, kind].rearrange("p h (c t) -> p h c t", c=TPS), ACT.Silu).then_inc(Z["silu"], 1)
                    else:
                        act.wait_ge(Z["vTp"], past(3 * f))
                        act.activation(vT[:], acc[:, kind], ACT.Silu).then_inc(Z["silu"], 1)

                def gate(i):
                    act.wait_ge(Z["oG"], past(2 * f - 2 if n is not None else 0))
                    act.wait_ge(Z["proj"], past(8 * f + 7 + i))
                    act.activation(gT[fp][:, 2 * i:2 * i + 2, :].rearrange("p h t -> p (h t)"), bank[RING["proj"][6 + i] % 3][:], ACT.Sigmoid).then_inc(Z["gate"], 1)

                def tokens_major(m):
                    act.wait_ge(Z["vTp"], past(3 * f + m + 1))
                    dst = vn[fp][:, m] if m < TPS else kn[fp][:]
                    act.copy(dst.rearrange("p h v -> p (h v)"), bank[(12 + m) % 3][:]).then_inc(Z["vn"], 1)

                def diagonal():
                    act.wait_ge(Z["X"], past(2 * f))
                    act.wait_ge(Z["LM"], past(2 * f + 2))
                    for q in range(P // BLK):
                        qs = slice(q * BLK, (q + 1) * BLK)
                        act.copy(BDL[qs, :, :, qs].rearrange("p c h t -> p (c h) t"),
                                 LT[qs, :, :, qs].rearrange("p c h t -> p (c h) t")).then_inc(Z["bdl"], 1)

                def blocks(lev, c):
                    act.wait_ge(Z["Y"], past(8 * h + 2 * (lev - 1) + c + 1))
                    act.copy(PT[:, c, :, 0, :], powers_of(lev, c)[:, :, 0, :]).then_inc(Z["Cev"], 1)

                def updates(c):
                    act.wait_ge(Z["Up"], past(2 * (n if c else h) + c + 1))
                    act.copy(U[:, c].rearrange("p h v -> p (h v)"), bank[6][:]).then_inc(Z["Uev"], 1)

                def first_out():
                    act.wait_ge(Z["Op"], past(2 * h + 1))
                    act.copy(o[:, 0].rearrange("p h v -> p (h v)"), bank[7][:]).then_inc(Z["oev"], 1)

                def state():
                    act.wait_ge(Z["Sp"], past(h + 1))
                    act.copy(S[:].rearrange("p h v -> p (h v)"), bank[5][:]).then_inc(Z["Sev"], 1)

                def from_state():
                    act.wait_ge(Z["QS"], past(h + 1))
                    for i in range(HG):
                        act.activation(oi[:, i], bank[5][:, i * DK:(i + 1) * DK], ACT.Copy,
                                       scale=gam_q[:, bass.ds(2 * (h % SEQS) + 1, 1), bass.ds((h // SEQS) * HG + i, 1)].rearrange("p a b -> p (a b)")).then_inc(Z["oi"], 1)

                def affine(c):
                    act.wait_ge(Z["oTp"], past(2 * n + c + 1))
                    act.activation(oT[:, c].rearrange("p h t -> p (h t)"), bank[6 + c][:], ACT.Identity,
                                   scale=ln_w[:], bias=ln_b[:]).then_inc(Z["oT"], 1)

                front, middle, back = f is not None, h is not None, n is not None
                if front:
                    tap(0)
                if middle:
                    blocks(1, 0), blocks(1, 1)
                if front:
                    tap(1)
                if middle:
                    blocks(2, 0), blocks(2, 1)
                if front:
                    tap(2), tap(3)
                if middle:
                    blocks(3, 0), blocks(3, 1)
                if back:
                    updates(1)
                if front:
                    tap(4)
                    silu(0), silu(1)
                    tap(5)
                if front:
                    silu(2)
                if back:
                    affine(0), affine(1)
                if front:
                    gate(0)
                if middle:
                    updates(0)
                if front:
                    gate(1)
                if middle:
                    state()
                if front:
                    tokens_major(0), tokens_major(1), tokens_major(2)
                    diagonal()
                if middle:
                    from_state()
                    first_out()

            pipeline(act, slot)
            routed(1)

        @block.vector
        def _(dve):
            ch = Chain(dve, v_step)
            base = 0

            def all_moments(eps_to, ready):
                with dve.Fori(0, TILES // 8) as t:
                    c = Chain(dve, v_step, base + 3 * t)
                    for i in range(8):
                        ins = dve.bn_stats(stats[:, i, :], stream[:, bass.ds(t * 8 + i, 1), :].rearrange("p a c -> p (a c)"))
                    c.link(ins)
                    dve.memset(pad[:], 0.0)
                    for i in range(8):
                        ins = dve.bn_aggr(mom8[:, i, :], stats[:, i, :])
                    c.link(ins)
                    c.link(dve.tensor_copy(moments[:, bass.ds(t * 8, 8), :], mom8[:]))
                dve.tensor_scalar(rstd[:], moments[:, :, 1], EPS, None, ALU.add).then_inc(ready, 1)
                return base + 3 * (TILES // 8)

            dve.wait_ge(loaded_x, 64)
            base = all_moments(rstd, A["var"])
            dve.wait_ge(A["rstd"], past(1))
            dve.wait_ge(consts, 12)
            dve.wait_ge(loaded_a, 96)
            base_a = base
            PER_A = 4

            def normalised(b):
                for j in range(TPS):
                    dve.wait_ge(A["xTp"], past(b))
                    dve.tensor_scalar(xn[:, j], stream[:, bass.ds(2 * b + j, 1), :].rearrange("p a c -> p (a c)"),
                                      moments[:, bass.ds(2 * b + j, 1), 0:1].rearrange("p a c -> p (a c)"),
                                      rstd[:, bass.ds(2 * b + j, 1)], ALU.subtract, ALU.mult).then_inc(A["xn"], 1)

            def head(b, j, c):
                dve.wait_ge(A["qkv"], past(2 * b + j + 1))
                src = bank[4 + j][:].rearrange("p (h i two) -> p h i two", i=HALF, two=2)
                cs = cosT[:, j:j + 1, :].broadcast_to([P, 2 * HEADS, HALF])
                sn = sinT[:, j:j + 1, :].broadcast_to([P, 2 * HEADS, HALF])
                t = [rope_t[:, m, j].rearrange("p (h i) -> p h i", i=HALF) for m in range(4)]
                dve.tensor_tensor(t[0], src[:, :, :, 0], cs, ALU.mult)
                dve.tensor_tensor(t[1], src[:, :, :, 1], sn, ALU.mult)
                dve.tensor_tensor(t[2], src[:, :, :, 0], sn, ALU.mult)
                c.link(dve.tensor_tensor(t[3], src[:, :, :, 1], cs, ALU.mult))
                dve.wait_ge(A["rotp"], past(4 * b))
                dve.tensor_tensor(rot[:, j, :, 0:HALF], t[0], t[1], ALU.subtract).then_inc(A["rope"], 1)
                dve.tensor_tensor(rot[:, j, :, HALF:HD], t[2], t[3], ALU.add).then_inc(A["rope"], 1)

            def body(b, head):
                c = Chain(dve, v_step, base_a + 2 + PER_A * b)
                if head:
                    normalised(b + 1)
                for u in range(UNITS):
                    heads = 4 if u % 3 == 0 else 2
                    sc3 = bank[SCORE_BANKS[u % 4]][:].rearrange("p (h s) -> p h s", h=heads)
                    dve.wait_ge(A["score"], past(UNITS * b + u + 1))
                    dve.tensor_reduce(row_max[:, u % 2, 0:heads], sc3, AX.X, ALU.max).then_inc(A["res"], 1)
                    dve.wait_ge(A["res"], past(b * (UNITS + 1) + u + 1))
                    if u >= 4:
                        dve.wait_ge(A["pT"], past(UNITS * b + u - 3))
                    dve.tensor_tensor(prob[:, u % 4].rearrange("p (h s) -> p h s", h=heads), sc3,
                                      row_max[:, u % 2, 0:heads].unsqueeze(2).broadcast_to([P, heads, 512 // heads]),
                                      ALU.subtract).then_inc(A["shift"], 1)
                if head:
                    head(b + 1, 0, c)
                dve.wait_ge(A["av"], past(UNITS * b + UNITS))
                for j in range(TPS):
                    av = bank[(3, 1)[j]][:, 0:HEADS * (HD + 1)].rearrange("p (h d) -> p h d", d=HD + 1)
                    c.link(dve.reciprocal(rsum[:, j, :], av[:, :, HD]))
                    dve.tensor_tensor(att[:, j].rearrange("p (h d) -> p h d", d=HD), av[:, :, 0:HD],
                                      rsum[:, j, :].unsqueeze(2).broadcast_to([P, HEADS, HD]), ALU.mult).then_inc(A["att"], 1)
                if head:
                    head(b + 1, 1, c)
                dve.wait_ge(A["yout"], past(b + 1))
                x2 = stream[:, bass.ds(2 * b, 2), :].rearrange("p j c -> p (j c)")
                dve.tensor_tensor(x2, x2, bank[1][:], ALU.add).then_inc(A["res"], 1)

            normalised(0)
            ch = Chain(dve, v_step, base_a)
            sequences(dve, lambda b, j, c=ch: head(b, j, c), body)
            base = base_a + 2 + PER_A * (SEQS - 1) + 2
            dve.wait_ge(A["res"], past(SEQS * (UNITS + 1)))
            dve.memset(pad[:], 0.0).then_inc(stage_done, 1)

            def routed(turn, base):
                dve.wait_ge(R["loaded"], past(96 * (turn + 1)))
                dve.wait_ge(R["cons"], past(4 * (turn + 1)))
                c = Chain(dve, v_step, base)
                c.link(dve.tensor_reduce(sl_sum[:], sl_all[:], AX.X, ALU.add))
                c.link(dve.tensor_scalar(sl_sign[:], sl_sum[:], 0.0, None, ALU.is_lt))
                c.link(dve.scalar_tensor_tensor(out=sl_sign[:], in0=sl_sum[:], scalar=0.0, in1=sl_sign[:],
                                                op0=ALU.is_gt, op1=ALU.subtract))
                base = base + c.n
                PER = 19
                with dve.Fori(0, FSTEPS) as s:
                    n = s + FSTEPS * turn
                    c = Chain(dve, v_step, base + PER * s)
                    xs4 = stream[:, bass.ds(s * FG, FG), :]
                    for i in range(FG):
                        ins = dve.bn_stats(stats[:, i, :], stream[:, bass.ds(s * FG + i, 1), :].rearrange("p a c -> p (a c)"))
                    c.link(ins)
                    dve.memset(pad[:], 0.0)
                    for i in range(FG):
                        ins = dve.bn_aggr(fmom[:, i, :], stats[:, i, :])
                    c.link(ins)
                    dve.tensor_scalar(fvar[:], fmom[:, :, 1], EPS, None, ALU.add).then_inc(R["var"], 1)
                    dve.wait_ge(R["rs"], past(2 * n + 1))
                    dve.wait_ge(R["added"], past(n))
                    for i in range(FG):
                        ins = dve.tensor_scalar(z[:, i], stream[:, bass.ds(s * FG + i, 1), :].rearrange("p a c -> p (a c)"),
                                                fmom[:, i, 0:1], frs[:, i:i + 1], ALU.subtract, ALU.mult)
                    ins.then_inc(R["z"], 1)
                    dve.wait_ge(R["z"], past(n + 1))
                    for i in range(FG):
                        ins = dve.bn_stats(stats[:, i, :], z[:, i])
                    c.link(ins)
                    dve.memset(pad[:], 0.0)
                    for i in range(FG):
                        ins = dve.bn_aggr(fmom2[:, i, :], stats[:, i, :])
                    c.link(ins)
                    dve.tensor_scalar(fvar2[:], fmom2[:, :, 1], EPS, None, ALU.add).then_inc(R["var"], 1)
                    dve.wait_ge(R["rs"], past(2 * n + 2))
                    xf4 = xf[:, bass.ds(s * FG, FG), :]
                    for i in range(FG):
                        ins = dve.tensor_scalar(xf[:, bass.ds(s * FG + i, 1), :].rearrange("p a c -> p (a c)"), z[:, i],
                                                fmom2[:, i, 0:1], frs2[:, i:i + 1], ALU.subtract, ALU.mult)
                    c.link(ins)
                    c.link(dve.tensor_tensor(xf4, xf4, gam[:].unsqueeze(1).broadcast_to([P, FG, C]), ALU.mult))
                    dve.tensor_tensor(xf4, xf4, bet[:].unsqueeze(1).broadcast_to([P, FG, C]), ALU.add).then_inc(R["xf"], 1)
                    dve.wait_ge(R["xf"], past(n + 1))
                    dve.memset(pad[:], 0.0)
                    x4 = xf4.rearrange("p f (r j) -> p (f r) j", j=SLICE)
                    dve.tensor_reduce(smin[:].rearrange("p f r -> p (f r)"), x4, AX.X, ALU.min)
                    c.link(dve.tensor_reduce(smax[:].rearrange("p f r -> p (f r)"), x4, AX.X, ALU.max))
                    dve.wait_ge(R["sign"], past(n + 1))
                    c.link(dve.tensor_tensor(sgn[:], sgn[:], sl_sign[:].unsqueeze(1).broadcast_to([P, FG, C]), ALU.mult))
                    c.link(dve.tensor_reduce(tsc[:].rearrange("p f r -> p (f r)"), sgn[:].rearrange("p f (r j) -> p (f r) j", j=SLICE), AX.X, ALU.add))
                    c.link(dve.tensor_reduce(csc[:].rearrange("p f k -> p (f k)"), tsc[:].rearrange("p f (k i) -> p (f k) i", k=CLUSTER), AX.X, ALU.add))
                    c.link(dve.scalar_tensor_tensor(out=comp[:], in0=tsc[:], scalar=float(ROUTES // CLUSTER),
                                                    in1=rank[:].unsqueeze(1).broadcast_to([P, FG, ROUTES]), op0=ALU.mult, op1=ALU.add))
                    cm = comp[:].rearrange("p f (k i) -> p (f k) i", k=CLUSTER)
                    c.link(dve.scalar_tensor_tensor(out=cm, in0=csc[:].rearrange("p f k -> p (f k)").unsqueeze(2).broadcast_to([P, FG * CLUSTER, ROUTES // CLUSTER]),
                                                    scalar=float(P * CLUSTER), in1=cm, op0=ALU.mult, op1=ALU.add))
                    c.link(dve.tensor_reduce(best[:], comp[:], AX.X, ALU.max))
                    oh4 = onehot[:, bass.ds(s * FG, FG), :]
                    c.link(dve.tensor_tensor(oh4, comp[:], best[:].unsqueeze(2).broadcast_to([P, FG, ROUTES]), ALU.is_equal))
                    c.link(dve.tensor_scalar(far[:], oh4, -FAR, FAR, ALU.mult, ALU.add))
                    c.link(dve.tensor_tensor(smin[:], smin[:], far[:], ALU.add))
                    c.link(dve.tensor_tensor(smax[:], far[:], smax[:], ALU.subtract))
                    c.link(dve.tensor_tensor(run_min[:], run_min[:], smin[:], ALU.min))
                    c.link(dve.tensor_tensor(run_nmax[:], run_nmax[:], smax[:], ALU.min))
                    assert c.n == PER, c.n
                base = base + PER * FSTEPS
                dve.memset(pad[:], 0.0).then_inc(R["pass1"], 1)
                dve.wait_ge(R["minT"], past(2 * (turn + 1)))
                c = Chain(dve, v_step, base)
                c.link(dve.tensor_reduce(ext[:, 0:1], bank[3][0:ROUTES, :], AX.X, ALU.min))
                c.link(dve.tensor_reduce(ext[:, 1:2], bank[4][0:ROUTES, :], AX.X, ALU.min))
                w = 2 * SLICE * GRID
                c.link(dve.tensor_copy(table[:, w + 1:w + 2], ext[:, 0:1]))
                c.link(dve.tensor_tensor(ext[:, 0:1], ext[:, 0:1], ext[:, 1:2], ALU.add))
                c.link(dve.tensor_scalar(ext[:, 0:1], ext[:, 0:1], -1.0, 1e-8, ALU.mult, ALU.add))
                dve.reciprocal(table[:, w + 2:w + 3], ext[:, 0:1]).then_inc(R["table"], 1)
                base = base + c.n
                PER2 = 16
                with dve.Fori(0, FSTEPS) as s:
                    n = s + FSTEPS * turn
                    c = Chain(dve, v_step, base + PER2 * s)
                    dve.wait_ge(R["pick0"], past(n + 1))
                    c.link(dve.tensor_reduce(xs[:], pick[:].rearrange("p f (r j) -> p f j r", j=SLICE), AX.X, ALU.add))
                    dve.wait_ge(R["sel"], past(2 * n + 2))
                    mn = selr[:, :, w + 1:w + 2].broadcast_to([P, FG, SLICE])
                    rd = selr[:, :, w + 2:w + 3].broadcast_to([P, FG, SLICE])
                    osc = selr[:, :, w:w + 1].broadcast_to([P, FG, SLICE])
                    c.link(dve.tensor_tensor(xs[:], xs[:], mn, ALU.subtract))
                    c.link(dve.tensor_tensor(xs[:], xs[:], rd, ALU.mult))
                    c.link(dve.tensor_scalar(xs[:], xs[:], 0.0, 1.0 - 1e-6, ALU.max, ALU.min))
                    c.link(dve.tensor_scalar(u16[:], xs[:], float(GRID), None, ALU.mult))
                    uf = u16[:].rearrange("p f j -> p (f j)")
                    c.link(dve.tensor_tensor(ge[:], uf.unsqueeze(2).broadcast_to([P, FG * SLICE, GRID + 1]),
                                             kgrid[:].unsqueeze(1).broadcast_to([P, FG * SLICE, GRID + 1]), ALU.is_ge))
                    c.link(dve.tensor_reduce(floor1[:], ge[:], AX.X, ALU.add))
                    gm = gmask[:].rearrange("p f (j k) -> p (f j) k", k=GRID)
                    c.link(dve.tensor_tensor(gm, ge[:, :, 0:GRID], ge[:, :, 1:GRID + 1], ALU.subtract))
                    hw = SLICE * GRID
                    tg = tmpg[:].rearrange("p f (j k) -> p (f j) k", k=GRID)
                    c.link(dve.tensor_tensor(tmpg[:], gmask[:], selr[:, :, 0:hw], ALU.mult))
                    c.link(dve.tensor_reduce(bsel[:], tg, AX.X, ALU.add))
                    c.link(dve.tensor_tensor(tmpg[:], gmask[:], selr[:, :, hw:2 * hw], ALU.mult))
                    c.link(dve.tensor_reduce(ssel[:], tg, AX.X, ALU.add))
                    c.link(dve.tensor_scalar(floor1[:], floor1[:], -1.0, None, ALU.add))
                    c.link(dve.tensor_tensor(uf, uf, floor1[:], ALU.subtract))
                    c.link(dve.tensor_tensor(ssel[:], ssel[:], uf, ALU.mult))
                    c.link(dve.tensor_tensor(bsel[:], bsel[:], ssel[:], ALU.add))
                    dve.tensor_tensor(delta[:], bsel[:].rearrange("p (f j) -> p f j", j=SLICE), osc, ALU.mult).then_inc(R["delta"], 1)
                    dve.wait_ge(R["delta"], past(n + 1))
                    pk = pick[:].rearrange("p f (r j) -> p f r j", j=SLICE)
                    dve.tensor_tensor(pk, oh_fix[:].unsqueeze(3).broadcast_to([P, FG, ROUTES, SLICE]),
                                      delta[:].unsqueeze(2).broadcast_to([P, FG, ROUTES, SLICE]), ALU.mult).then_inc(R["scat"], 1)
                    dve.wait_ge(R["scat"], past(n + 1))
                    xs4 = stream[:, bass.ds(s * FG, FG), :]
                    dve.tensor_tensor(xs4, xs4, pick[:], ALU.add).then_inc(R["res"], 1)
                    assert c.n == PER2, c.n
                dve.wait_ge(R["res"], past(FSTEPS * (turn + 1)))
                dve.memset(pad[:], 0.0).then_inc(stage_done, 1)
                return base + PER2 * FSTEPS

            base = routed(0, base)
            dve.wait_ge(stage_done, 2)
            base = all_moments(rstd, Z["var"])
            dve.wait_ge(Z["rstd"], past(1))
            PER_P = 4
            base_p = base
            with dve.Fori(0, SEQS) as b:
                c = Chain(dve, v_step, base_p + PER_P * b)
                for j in range(TPS):
                    dve.wait_ge(Z["xTp"], past(b))
                    dve.tensor_scalar(cxn[:, j], stream[:, bass.ds(2 * b + j, 1), :].rearrange("p a c -> p (a c)"),
                                      moments[:, bass.ds(2 * b + j, 1), 0:1].rearrange("p a c -> p (a c)"),
                                      rstd[:, bass.ds(2 * b + j, 1)], ALU.subtract, ALU.mult).then_inc(Z["xn"], 1)
                dve.wait_ge(Z["ab"], past(2 * b + 2))
                dve.wait_ge(Z["stored"], past(32 * b))
                dve.wait_ge(Z["gamp"], past(b))
                c.link(dve.tensor_copy(alpha_z[:], alphaT[:]))
                c.link(dve.memset(alpha_z[:, 0:SEQ:P], 0.0))
                c.link(dve.tensor_tensor(alpha_r[:], alphaT[:], alpha_z[:], ALU.subtract))
                c.link(dve.tensor_tensor_scan(gam_row[:], alpha_z[:], alpha_r[:], 0.0, ALU.mult, ALU.add))
                dve.memset(gprev_row[:, 0:SEQ:P], 1.0)
                dve.tensor_copy(gprev_row[:].rearrange("h (c t) -> h c t", c=TPS)[:, :, 1:P],
                                gam_row[:].rearrange("h (c t) -> h c t", c=TPS)[:, :, 0:P - 1]).then_inc(Z["rows"], 1)
            base = base_p + PER_P * SEQS
            dve.wait_ge(Z["ab"], past(2 * SEQS))
            c = Chain(dve, v_step, base)
            dve.tensor_scalar(beta_k[:], beta[:], KAPPA2, None, ALU.mult)
            c.link(dve.tensor_scalar(beta_q[:], beta[:], KAPPA, None, ALU.mult))
            base = base + c.n
            dve.wait_ge(Z["cons"], past(PROBS + 2 * (P // BLK) + 5))
            PER_C = 23
            before = []

            def slot(f, h, n, fp):
                hp = 1 - fp
                if h is None and f is not None:
                    c = Chain(dve, v_step, base)
                elif n is None:
                    c = Chain(dve, v_step, base + before[0])
                else:
                    c = Chain(dve, v_step, base + sum(before) + PER_C * n + (after[-1] - PER_C if f is None and h is None else 0))
                quads = [slice(q * BLK, (q + 1) * BLK) for q in range(P // BLK)]
                if f is not None:
                    fb, fg = f % SEQS, f // SEQS
                if h is not None:
                    hb, hg = h % SEQS, h // SEQS

                def conv(u):
                    kind, pair = u // 2, u % 2
                    dve.wait_ge(Z["tap"], past(24 * f + 4 * u + 4))
                    last = {}
                    for t in range(2, TAPS):
                        for i in (2 * pair, 2 * pair + 1):
                            pj = bank[RING["proj"][u] % 3][:, (i % 2) * SEQ:(i % 2 + 1) * SEQ]
                            wcol = conv_w[:, kind, bass.ds(fg * HG + i, 1), TAPS - 1 - t:TAPS - t].rearrange("p a b -> p (a b)")
                            if t > 2:
                                c.wait(last[i])
                            ins = dve.scalar_tensor_tensor(out=acc[:, kind, i, t:], in0=pj[:, 0:SEQ - t], scalar=wcol,
                                                           in1=acc[:, kind, i, t:], op0=ALU.mult, op1=ALU.add)
                            if t < TAPS - 1:
                                last[i] = c.mark(ins)
                            else:
                                ins.then_inc(Z["conv"], 1)

                def decays():
                    dve.wait_ge(Z["abc"], past(16 * f + 16))
                    dve.tensor_tensor_scan(dec[:].rearrange("p h t -> p (h t)"), abc[:].rearrange("p h t -> p (h t)"),
                                           id_many[:].rearrange("p n t -> p (n t)"), 0.0, ALU.mult, ALU.add).then_inc(Z["dec"], 1)
                    dve.wait_ge(Z["dec"], past(f + 1))
                    dve.tensor_tensor(wgt[fp][:], dec[:, :, P - 1], beta[:, bass.ds(2 * fb, 1), bass.ds(fg * HG, HG)].rearrange("p a b -> p (a b)"),
                                      ALU.mult).then_inc(Z["wgt"], 1)

                def products(u):
                    tc, pair = u // 2, u % 2
                    dve.wait_ge(Z["Gp"], past(2 * (f if h is None else h + 1)))
                    dve.wait_ge(Z["kq"], past(4 * f + u + 1))
                    for i in (2 * pair, 2 * pair + 1):
                        src = bank[RING["products"][u] % 3][:, (i % 2) * 2 * P:(i % 2 + 1) * 2 * P]
                        bk = beta_k[:, bass.ds(2 * fb + tc, 1), bass.ds(fg * HG + i, 1)].rearrange("p a b -> p (a b)")
                        bq = beta_q[:, bass.ds(2 * fb + tc, 1), bass.ds(fg * HG + i, 1)].rearrange("p a b -> p (a b)")
                        dve.scalar_tensor_tensor(out=LT[:, tc, i, 1:P], in0=src[:, 1:P], scalar=bk,
                                                 in1=dec[:, i, tc * P:tc * P + P - 1], op0=ALU.mult, op1=ALU.mult)
                        ins = dve.scalar_tensor_tensor(out=MT[fp][:, tc, i, :], in0=src[:, P:2 * P], scalar=bq,
                                                       in1=dec[:, i, tc * P:(tc + 1) * P], op0=ALU.mult, op1=ALU.mult)
                    ins.then_inc(Z["read"], 1)

                def start_inverse():
                    dve.wait_ge(Z["LM"], past(2 * f + 2))
                    for qs in quads:
                        ins = dve.tensor_tensor(BDT[fp][qs, :, :, qs].rearrange("p c h t -> p (c h) t"),
                                                id2c[qs, :].unsqueeze(1).broadcast_to([BLK, PROBS, BLK]),
                                                LT[qs, :, :, qs].rearrange("p c h t -> p (c h) t"), ALU.subtract)
                        c.mark(ins)
                    for m, qs in enumerate(quads):
                        c.wait(c.n - 3)
                        ins = dve.transpose(PT[qs, :, :, 1, :].rearrange("p c h t -> p (c h) t"), BDT[fp][qs, :, :, qs].rearrange("p c h t -> p (c h) t"))
                        if m < 3:
                            c.mark(ins)
                        else:
                            ins.then_inc(Z["t1"], 1)

                def first_power(tc):
                    dve.wait_ge(Z["X"], past(2 * h + tc + 1))
                    dve.scalar_tensor_tensor(out=PT[:, tc, :, 0, :], in0=powers_of(0, tc)[:, :, 0, :], scalar=-1.0,
                                             in1=id1c[:].unsqueeze(1).broadcast_to([P, HG, BLK]), op0=ALU.mult, op1=ALU.add).then_inc(Z["P1"], 1)

                def add_term(lev, tc):
                    return dve.tensor_tensor(PT[:, tc, :, 1, :], PT[:, tc, :, 1, :], powers_of(lev, tc)[:, :, 1, :], ALU.add)

                def turn(lev, tc):
                    if lev:
                        dve.wait_ge(Z["Cev"], past(6 * h + 2 * (lev - 1) + tc + 1))
                    else:
                        dve.wait_ge(Z["P1"], past(2 * h + tc + 1))
                    for qs in quads:
                        ins = dve.transpose(BDT[hp][qs, tc, :, qs], PT[qs, tc, :, 0, :])
                    if lev:
                        ins = add_term(lev, tc)
                    ins.then_inc(Z["Tn"], 1)

                def finish():
                    for tc in range(TPS):
                        dve.wait_ge(Z["Y"], past(8 * h + 6 + tc + 1))
                        c.mark(add_term(4, tc))
                    c.wait(c.n)

                def transposed_blocks():
                    for tc in range(TPS):
                        for qs in quads:
                            dve.transpose(BDT[hp][qs, tc, :, qs], PT[qs, tc, :, 1, :])

                def plain_blocks():
                    for qs in quads:
                        ins = dve.tensor_copy(BDN[qs, :, :, qs].rearrange("p c h t -> p (c h) t"), PT[qs, :, :, 1, :].rearrange("p c h t -> p (c h) t"))
                    ins.then_inc(Z["bdn"], 1)

                def off_blocks(tc):
                    dve.wait_ge(Z["Gp"], past(2 * h + tc + 1))
                    dve.tensor_tensor(GT[hp][:, tc], id_many[:, 0:HG], bank[3 + tc][:].rearrange("p (h t) -> p h t", h=HG), ALU.subtract).then_inc(Z["Gev"], 1)

                def sweep(tc, k):
                    dve.wait_ge(Z["ap"], past(6 * (n if tc else h) + 3 * tc + k + 1))
                    dve.tensor_tensor(y[:], vn[hp][:, 0] if tc == 0 else r1[:], bank[5][:].rearrange("p (h v) -> p h v", h=HG), ALU.add).then_inc(Z["yv"], 1)

                def weighted():
                    dve.wait_ge(Z["wgt"], past(h + 1))
                    dve.wait_ge(Z["Uev"], past(2 * h + 1))
                    dve.tensor_tensor(Uw[:], U[:, 0], wgt[hp][:].unsqueeze(2).broadcast_to([P, HG, DK]), ALU.mult).then_inc(Z["Uw"], 1)

                def second_rhs():
                    dve.wait_ge(Z["KS"], past(h + 1))
                    for i in range(HG):
                        gk = gam_k[:, bass.ds(2 * hb + 1, 1), bass.ds(hg * HG + i, 1)].rearrange("p a b -> p (a b)")
                        ins = dve.scalar_tensor_tensor(out=r1[:, i], in0=bank[6][:, i * DK:(i + 1) * DK], scalar=gk,
                                                       in1=vn[hp][:, 1, i], op0=ALU.mult, op1=ALU.add)
                    ins.then_inc(Z["r1"], 1)
                    dve.wait_ge(Z["r1"], past(h + 1))

                of = o[:].rearrange("p c h v -> p (c h) v")

                def moments_of_out():
                    dve.wait_ge(Z["Op"], past(2 * n + 2))
                    dve.wait_ge(Z["oi"], past(4 * n + 4))
                    dve.tensor_tensor(o[:, 1], oi[:], bank[7][:].rearrange("p (h v) -> p h v", h=HG), ALU.add).then_inc(Z["oev"], 1)
                    dve.wait_ge(Z["oev"], past(2 * n + 2))
                    for m in range(PROBS):
                        ins = dve.bn_stats(ostat[:, m], of[:, m])
                    c.link(ins)
                    dve.memset(pad[:], 0.0)
                    for m in range(PROBS):
                        ins = dve.bn_aggr(omom[:, m], ostat[:, m])
                    c.link(ins)
                    dve.tensor_scalar(ovar[:], omom[:, :, 1], EPS, None, ALU.add).then_inc(Z["ovar"], 1)

                def normalise():
                    dve.wait_ge(Z["ors"], past(n + 1))
                    for m in range(PROBS):
                        ins = dve.tensor_scalar(of[:, m], of[:, m], omom[:, m, 0:1], ors[:, m:m + 1], ALU.subtract, ALU.mult)
                    ins.then_inc(Z["on"], 1)

                def residual():
                    dve.wait_ge(Z["yout"], past(n + 1))
                    x2 = stream[:, bass.ds(2 * (n % SEQS), 2), :].rearrange("p j c -> p (j c)")
                    dve.tensor_tensor(x2, x2, bank[7][:], ALU.add).then_inc(Z["res"], 1)

                front, middle, back = f is not None, h is not None, n is not None
                if middle:
                    first_power(0), first_power(1)
                    turn(0, 0), turn(0, 1)
                if front:
                    decays()
                    conv(0)
                if back:
                    sweep(1, 0)
                if middle:
                    turn(1, 0), turn(1, 1)
                if front:
                    conv(1)
                if back:
                    sweep(1, 1)
                if middle:
                    turn(2, 0), turn(2, 1)
                if front:
                    conv(2)
                if back:
                    sweep(1, 2)
                if front:
                    conv(3)
                if middle:
                    turn(3, 0), turn(3, 1)
                if front:
                    conv(4)
                if middle:
                    finish()
                    plain_blocks()
                if back:
                    moments_of_out()
                if middle:
                    off_blocks(0), off_blocks(1)
                if front:
                    conv(5)
                if middle:
                    transposed_blocks()
                    sweep(0, 0)
                if back:
                    normalise()
                if front:
                    products(0), products(1)
                if middle:
                    sweep(0, 1)
                if front:
                    products(2), products(3)
                if middle:
                    sweep(0, 2)
                if front:
                    start_inverse()
                if middle:
                    weighted()
                if back:
                    residual()
                if middle:
                    second_rhs()
                if n is None:
                    before.append(c.n)
                elif front:
                    assert c.n == PER_C, c.n
                after.append(c.n)

            after = []
            pipeline(dve, slot)
            base = base + sum(before) + PER_C * (STEPS - 2) + after[-2] + after[-1]
            dve.wait_ge(Z["res"], past(STEPS))
            dve.memset(pad[:], 0.0).then_inc(stage_done, 1)
            base = routed(1, base)

        @block.tensor
        def _(pe):
            pe.wait_ge(loaded_a, 96)
            pe.wait_ge(consts, 12)

            def tokens(b):
                pe.wait_ge(A["xn"], past(2 * b + 2))
                if not isinstance(b, int):
                    pe.wait_ge(A["shift"], past(UNITS * b - 1))
                for k in range(CT):
                    for j in range(TPS):
                        mm = pe.transpose(bank[0][:, k * SEQ + j * P:k * SEQ + (j + 1) * P], xn[:, j, k * P:(k + 1) * P], ident[:])
                mm.then_inc(A["xTp"], 1)

            def rotated(b, j):
                for qk in range(2):
                    pe.wait_ge(A["rope"], past(4 * b + 2 * j + 2))
                    for g in range(4):
                        h0 = qk * HEADS + 4 * g
                        mm = pe.transpose(bank[ROT_BANKS[2 * j + qk]][:, g * P:(g + 1) * P],
                                          rot[:, j, h0:h0 + 4, :].rearrange("p h d -> p (h d)"), ident[:])
                    mm.then_inc(A["rotp"], 1)

            def head(b, j):
                pe.wait_ge(A["xT"], past(b + 1))
                if j == 0 and not isinstance(b, int):
                    pe.wait_ge(A["shift"], past(UNITS * b))
                for dst, lo, hi in ((bank[4 + j][:], 0, 2 * C), (bank[2][:, j * C:(j + 1) * C], 2 * C, 3 * C)):
                    pe.matmul(dst, ones_row[:], b_qkv[:, lo:hi], start=True, stop=False)
                    for k in range(CT):
                        mm = pe.matmul(dst, xT[:, k, j * P:(j + 1) * P], w_qkv[:, k, lo:hi], start=False, stop=(k == CT - 1))
                mm.then_inc(A["qkv"], 1)
                if j == 1 and isinstance(b, int):
                    rotated(b, 0)

            def body(b, head):
                rotated(b, 1)

                def heads_of(u):
                    r, part = u // 3, u % 3
                    return [(g, r) for g in (range(4) if part == 0 else (2 * (part - 1), 2 * (part - 1) + 1))], (0 if part == 0 else 1)

                def scores(u):
                    hs, j = heads_of(u)
                    bk = bank[SCORE_BANKS[u % 4]]
                    if u < 3:
                        pe.wait_ge(A["qkT"], past(10 * b + (2, 7, 10)[u]))
                    if u >= 4:
                        pe.wait_ge(A["shift"], past(UNITS * b + u - 3))
                    elif u == 3:
                        pe.wait_ge(A["v"], past(2 * b + 2))
                    pe.matmul(bk[:], identb[:], (maskd if j == 0 else masko)[:].rearrange("p a s -> p (a s)"), start=True, stop=True)
                    w = (j + 1) * P
                    for m, (g, r) in enumerate(hs):
                        mm = pe.matmul(bk[:, m * w:(m + 1) * w], qT[:, r, g, j * P:(j + 1) * P], kT[:, g, 0:w], start=False,
                                       stop=True, skip_group_check=True)
                    mm.then_inc(A["score"], 1)

                def weigh(u):
                    pe.wait_ge(A["exp"], past(UNITS * b + u + 1))
                    if u >= 2:
                        pe.wait_ge(A["probT"], past(UNITS * b + u - 1))
                    for m in range(4):
                        mm = pe.transpose(bank[6 + u % 2][:, m * P:(m + 1) * P], prob[:, u % 4, m * P:(m + 1) * P], ident[:])
                    mm.then_inc(A["pT"], 1)

                def apply(u):
                    hs, j = heads_of(u)
                    pe.wait_ge(A["probT"], past(UNITS * b + u + 1))
                    if u == 0:
                        pe.wait_ge(A["v"], past(2 * b + 2))
                    if u == 1:
                        pe.wait_ge(A["res"], past(b * (UNITS + 1)))
                    for m, (g, r) in enumerate(hs):
                        h = 4 * g + r
                        for st in range(j + 1):
                            mm = pe.matmul(bank[(3, 1)[j]][:, h * (HD + 1):(h + 1) * (HD + 1)],
                                           probT[:, u % 4, (m * (j + 1) + st) * P:(m * (j + 1) + st + 1) * P], vx[:, st, h, :],
                                           start=(st == 0), stop=(st == j))
                    mm.then_inc(A["av"], 1)

                def ahead(part):
                    if not head:
                        return
                    if part == 2:
                        tokens(b + 1)
                    else:
                        head(b + 1, part)

                for pair in range(0, UNITS, 2):
                    for stage, u in ((scores, pair), (apply, pair - 4), (scores, pair + 1), (weigh, pair - 2),
                                     (apply, pair - 3), (weigh, pair - 1)):
                        if 0 <= u < UNITS:
                            stage(u)
                last = UNITS - 1
                for stage, u in ((apply, last - 3), (weigh, last - 1), (ahead, 2), (apply, last - 2), (weigh, last),
                                 (ahead, 0), (apply, last - 1), (apply, last), (ahead, 1)):
                    stage(u)
                pe.wait_ge(A["att"], past(2 * b + 2))
                for k in range(CT):
                    for j in range(TPS):
                        mm = pe.transpose(bank[3][:, k * SEQ + j * P:k * SEQ + (j + 1) * P], att[:, j, k * P:(k + 1) * P], ident[:])
                mm.then_inc(A["attTp"], 1)
                if head:
                    rotated(b + 1, 0)
                pe.wait_ge(A["attT"], past(b + 1))
                for j in range(TPS):
                    dst = bank[1][:, j * C:(j + 1) * C]
                    pe.matmul(dst, ones_row[:], b_out[:], start=True, stop=False)
                    for k in range(CT):
                        mm = pe.matmul(dst, attT[:, k, j * P:(j + 1) * P], w_out[:, k, :], start=False, stop=(k == CT - 1))
                mm.then_inc(A["yout"], 1)

            tokens(0)
            sequences(pe, head, body)

            def routed(turn):
                pe.wait_ge(R["pass1"], past(turn + 1))
                for m, src in enumerate((run_min, run_nmax)):
                    for i in range(FG):
                        mm = pe.transpose(bank[3 + m][0:ROUTES, i * P:(i + 1) * P], src[:, i, :], ident[:])
                    mm.then_inc(R["minT"], 1)
                pe.wait_ge(R["table"], past(turn + 1))
                with pe.Fori(0, FSTEPS) as s:
                    n = s + FSTEPS * turn
                    pe.wait_ge(R["fix"], past(n + 1))
                    pe.transpose(bank[0][:, 0:P], ident[:], ident[:])
                    for i in range(FG):
                        mm = pe.transpose(bank[0][0:ROUTES, i * P:(i + 1) * P], oh_fix[:, i, :], ident[:])
                    mm.then_inc(R["ohTp"], 1)
                    pe.wait_ge(R["ohT"], past(n + 1))
                    pe.wait_ge(R["sel"], past(2 * n))
                    for i in range(FG):
                        mm = pe.matmul(bank[1 + i // 2][:, (i % 2) * 256:(i % 2) * 256 + TABW], ohT[:, i, :], table[:], start=True, stop=True)
                    mm.then_inc(R["selp"], 1)

            routed(0)
            pe.wait_ge(Z["wab"], past(16 * 13))
            with pe.Fori(0, SEQS) as b:
                pe.wait_ge(Z["xn"], past(2 * b + 2))
                for k in range(CT):
                    for j in range(TPS):
                        mm = pe.transpose(bank[0][:, k * SEQ + j * P:k * SEQ + (j + 1) * P], cxn[:, j, k * P:(k + 1) * P], ident[:])
                mm.then_inc(Z["xTp"], 1)
                pe.wait_ge(Z["xT"], past(2 * b + 2))
                for j in range(TPS):
                    dst = bank[1][:, j * 2 * DH:(j + 1) * 2 * DH]
                    pe.matmul(dst, ones_row[:], b_ab[:], start=True, stop=False)
                    for k in range(CT):
                        mm = pe.matmul(dst, cxT[:, k, j * P:(j + 1) * P], w_ab[:, k, :], start=False, stop=(k == CT - 1))
                mm.then_inc(Z["abp"], 1)
                for k in range(CT):
                    mm = pe.matmul(bank[2][0:DH, 0:SEQ], w_ab[:, k, 0:DH], cxT[:, k, :], start=(k == 0), stop=(k == CT - 1))
                mm.then_inc(Z["abp"], 1)
                pe.wait_ge(Z["rows"], past(b + 1))
                pe.wait_ge(Z["gam"], past(2 * b))
                pe.transpose(bank[3][:, 0:P], ident[:], ident[:])
                for m, src in enumerate((gam_row, gprev_row)):
                    for j in range(TPS):
                        mm = pe.transpose(bank[3][:, (2 * m + j) * DH:(2 * m + j + 1) * DH], src[:, j * P:(j + 1) * P], ident[0:DH, 0:DH])
                mm.then_inc(Z["gamp"], 1)
            pe.wait_ge(Z["ab"], past(2 * SEQS))
            pe.wait_ge(Z["gam"], past(2 * SEQS))
            def slot(f, h, n, fp):
                hp = 1 - fp

                def ring_free(pos):
                    if pos >= 3:
                        pos, step = pos - 3, f
                    elif h is None:
                        return
                    else:
                        pos, step = pos + 12, h
                    if pos in RING["proj"]:
                        u = RING["proj"].index(pos)
                        if u < 6:
                            pe.wait_ge(Z["conv"], past(12 * step + 2 * u + 2))
                        else:
                            pe.wait_ge(Z["gate"], past(2 * step + u - 5))
                    elif pos in RING["products"]:
                        pe.wait_ge(Z["read"], past(4 * step + RING["products"].index(pos) + 1))
                    else:
                        pe.wait_ge(Z["vn"], past(3 * step + pos - 11))

                def proj(u):
                    if u == 0:
                        pe.wait_ge(Z["wg"], past(64 * (f // SEQS) + 64))
                        pe.wait_ge(Z["xin"], past(16 * f + 16))
                    ring_free(RING["proj"][u])
                    for i in range(2):
                        head = 2 * (u % 2) + i
                        for k in range(CT):
                            mm = pe.matmul(bank[RING["proj"][u] % 3][:, i * SEQ:(i + 1) * SEQ], w4[:, u // 2, k, head * DK:(head + 1) * DK], xTb[:, k, :],
                                           start=(k == 0), stop=(k == CT - 1))
                    mm.then_inc(Z["proj"], 1)

                def products(u):
                    c, pair = u // 2, u % 2
                    pe.wait_ge(Z["silu"], past(3 * f + 2))
                    ring_free(RING["products"][u])
                    for i in (2 * pair, 2 * pair + 1):
                        mm = pe.matmul(bank[RING["products"][u] % 3][:, (i % 2) * 2 * P:(i % 2 + 1) * 2 * P], kq[fp][:, i, c, 0, :],
                                       kq[fp][:, i, c].rearrange("p a t -> p (a t)"), start=True, stop=True)
                    mm.then_inc(Z["kq"], 1)

                def tokens_major(m):
                    pe.wait_ge(Z["silu"], past(3 * f + 3))
                    ring_free(12 + m)
                    for i in range(HG):
                        src = vT[:, i, m * P:(m + 1) * P] if m < TPS else kq[fp][:, i, 0, 0, :]
                        mm = pe.transpose(bank[(12 + m) % 3][:, i * DK:(i + 1) * DK], src, ident[:])
                    mm.then_inc(Z["vTp"], 1)

                def residue(c):
                    pe.wait_ge(Z["Gev"], past(2 * h))
                    pe.wait_ge(Z["bdl"], past(4 * h + 4))
                    pe.wait_ge(Z["t1"], past(h + 1))
                    for i in range(HG):
                        mm = pe.matmul(powers_of(0, c)[:, i, 0, :], BDL[:, c, i], PT[:, c, i, 1, :], start=True, stop=True)
                    mm.then_inc(Z["X"], 1)

                def power(lev, c):
                    pe.wait_ge(Z["Tn"], past(8 * h + 2 * (lev - 1) + c + 1))
                    for i in range(HG):
                        if lev < 4:
                            dst, src = powers_of(lev, c)[:, i].rearrange("p a t -> p (a t)"), PT[:, c, i].rearrange("p a t -> p (a t)")
                        else:
                            dst, src = powers_of(lev, c)[:, i, 1, :], PT[:, c, i, 1, :]
                        mm = pe.matmul(dst, BDT[hp][:, c, i], src, start=True, stop=True)
                    mm.then_inc(Z["Y"], 1)

                def off_blocks(c):
                    pe.wait_ge(Z["bdn"], past(h + 1))
                    for i in range(HG):
                        mm = pe.matmul(bank[3 + c][:, i * P:(i + 1) * P], BDN[:, c, i], LT[:, c, i], start=True, stop=True)
                    mm.then_inc(Z["Gp"], 1)

                def of(c):
                    return (n, fp) if c else (h, hp)

                def sweep(c, k):
                    step, par = of(c)
                    if k == 0:
                        pe.wait_ge(Z["Gev"], past(2 * step + c + 1))
                        if c == 0:
                            pe.wait_ge(Z["vn"], past(3 * step + 1))
                        else:
                            pe.wait_ge(Z["oi"], past(4 * step + 4))
                            pe.wait_ge(Z["r1"], past(n + 1))
                    else:
                        pe.wait_ge(Z["yv"], past(6 * step + 3 * c + k))
                    src = y if k else (r1, vn[hp][:, 0])[c == 0]
                    for i in range(HG):
                        mm = pe.matmul(bank[5][:, i * DK:(i + 1) * DK], GT[par][:, c, i], src[:, i], start=True, stop=True)
                    mm.then_inc(Z["ap"], 1)

                def updates(c):
                    step, par = of(c)
                    if c == 0:
                        pe.wait_ge(Z["oT"], past(2 * step))
                    pe.wait_ge(Z["yv"], past(6 * step + 3 * c + 3))
                    for i in range(HG):
                        mm = pe.matmul(bank[6][:, i * DK:(i + 1) * DK], BDT[par][:, c, i], y[:, i], start=True, stop=True)
                    mm.then_inc(Z["Up"], 1)

                def outputs(c):
                    step, par = of(c)
                    pe.wait_ge(Z["Uev"], past(2 * step + c + 1))
                    if c == 0:
                        pe.wait_ge(Z["res"], past(step))
                    else:
                        pe.wait_ge(Z["oev"], past(2 * step + 1))
                    for i in range(HG):
                        mm = pe.matmul(bank[7][:, i * DK:(i + 1) * DK], MT[par][:, c, i], U[:, c, i], start=True, stop=True)
                    mm.then_inc(Z["Op"], 1)

                def state():
                    pe.wait_ge(Z["Uw"], past(h + 1))
                    for i in range(HG):
                        mm = pe.matmul(bank[5][:, i * DK:(i + 1) * DK], kn[hp][:, i], Uw[:, i], start=True, stop=True)
                    mm.then_inc(Z["Sp"], 1)

                def from_state():
                    pe.wait_ge(Z["Sev"], past(h + 1))
                    for a, sg in ((0, "KS"), (1, "QS")):
                        for i in range(HG):
                            mm = pe.matmul(bank[6 - a][:, i * DK:(i + 1) * DK], kq[hp][:, i, 1, a, :], S[:, i], start=True, stop=True)
                        mm.then_inc(Z[sg], 1)

                def outT(c):
                    pe.wait_ge(Z["on"], past(n + 1))
                    for i in range(HG):
                        mm = pe.transpose(bank[6 + c][:, i * P:(i + 1) * P], o[:, c, i], ident[:])
                    mm.then_inc(Z["oTp"], 1)

                def project_out(c):
                    if c == 0:
                        pe.wait_ge(Z["wo"], past(16 * (n // SEQS) + 16))
                        pe.wait_ge(Z["oT"], past(2 * n + 2))
                    pe.wait_ge(Z["oG"], past(2 * n + c + 1))
                    for i in range(HG):
                        mm = pe.matmul(bank[7][:, c * C:(c + 1) * C], oG[:, c, i], w_o[:, i], start=(i == 0), stop=(i == HG - 1))
                    if c:
                        mm.then_inc(Z["yout"], 1)

                front, middle, back = f is not None, h is not None, n is not None
                if middle:
                    residue(0), residue(1)
                if front:
                    proj(0)
                if back:
                    sweep(1, 0)
                if middle:
                    power(1, 0), power(1, 1)
                if front:
                    proj(1)
                if back:
                    sweep(1, 1)
                if middle:
                    power(2, 0), power(2, 1)
                if front:
                    proj(2)
                if back:
                    sweep(1, 2)
                if front:
                    proj(3)
                if middle:
                    power(3, 0), power(3, 1)
                if back:
                    updates(1)
                if front:
                    proj(4)
                if back:
                    outputs(1)
                if middle:
                    power(4, 0), power(4, 1)
                if front:
                    proj(5)
                if front:
                    products(0), products(1)
                if middle:
                    off_blocks(0), off_blocks(1)
                    sweep(0, 0)
                if front:
                    proj(6)
                if middle:
                    sweep(0, 1)
                if back:
                    outT(0), outT(1)
                if front:
                    products(2), products(3)
                if middle:
                    sweep(0, 2)
                if back:
                    project_out(0)
                if middle:
                    updates(0)
                if back:
                    project_out(1)
                if front:
                    proj(7)
                if middle:
                    state()
                if front:
                    tokens_major(0), tokens_major(1), tokens_major(2)
                if middle:
                    from_state()
                    outputs(0)

            pipeline(pe, slot)
            routed(1)


def kernel(**inputs):
    import concourse.bacc as bacc
    from concourse.bass_utils import run_bass_kernel_spmd

    a, d, f = "L0_attn_a_", "L0_attn_b_", "L0_ffn_"
    nc = bacc.Bacc("TRN2", target_bir_lowering=False, num_devices=1)
    theta = (np.float32(10000.0) ** (-np.arange(HALF, dtype=np.float32) / np.float32(HALF))).astype(np.float32)
    angle = np.arange(SEQ, dtype=np.float32)[:, None] * theta[None, :]
    get = {k: np.asarray(v) for k, v in inputs.items()}
    arrays = {
        "x": get[a + "x"].reshape(-1, C), "w_qkv": get[a + "w_qkv"].T, "w_out": get[a + "w_out"].T,
        "b_qkv": get[a + "b_qkv"], "b_out": get[a + "b_out"], "cos": np.cos(angle), "sin": np.sin(angle),
        "gamma": get[f + "ln_gamma"], "beta": get[f + "ln_beta"], "bases": get[f + "spline_bases"],
        "slopes": get[f + "spline_slopes"], "oscale": get[f + "output_scale"],
        "ln_w": get[d + "ln_w"], "ln_b": get[d + "ln_b"], "ba": get[d + "ba"], "bb": get[d + "bb"],
        "Wa": get[d + "Wa"], "Wb": get[d + "Wb"], "Wq": get[d + "Wq"], "Wk": get[d + "Wk"],
        "Wv": get[d + "Wv"], "Wg": get[d + "Wg"], "Wo": get[d + "Wo"],
    }
    for k in "qkv":
        arrays[f"cw_{k}"] = get[d + f"conv_{k}_w"].reshape(DH, DK, TAPS).transpose(1, 0, 2)
        arrays[f"cb_{k}"] = get[d + f"conv_{k}_b"].reshape(DH, DK).T
    arrays = {k: np.ascontiguousarray(v) for k, v in arrays.items()}
    io = {k: nc.dram_tensor(f"in_{k}", v.shape, mybir.dt.from_np(v.dtype), kind="ExternalInput").ap() for k, v in arrays.items()}
    io["out"] = nc.dram_tensor("out", [SEQS * SEQ, C], F32, kind="ExternalOutput").ap()
    program(nc, io)
    r = run_bass_kernel_spmd(nc, [{f"in_{k}": v for k, v in arrays.items()}], core_ids=[0])
    return r.results[0]["out"].reshape(SEQS, SEQ, C)
```
